# Optimizing a Trainium2 kernel written in Bass

```python
import numpy as np
import jax
import jax.numpy as jnp

def _softmax(x, axis=-1):
    return jax.nn.softmax(x, axis=axis)

def _gelu(x):
    return jax.nn.gelu(x, approximate=True)

def _silu(x):
    return jax.nn.silu(x)

def _sigmoid(x):
    return jax.nn.sigmoid(x)

def _layernorm(x, axis=-1, eps=1e-05):
    m = jnp.mean(x, axis=axis, keepdims=True)
    v = jnp.var(x, axis=axis, keepdims=True)
    return (x - m) / jnp.sqrt(v + eps)

def _scatter_add(tgt, idx, src, axis=0):
    return tgt.at[idx].add(src)

def _segment_sum(src, seg, n):
    return jax.ops.segment_sum(src, seg, n)
kernel_name = 'mk_xattn_ffn_d2_seqx_r8_a6c5c4'

def setup_inputs(seed: int=0):
    np.random.seed(seed)
    _w = jnp.asarray

    def _rec_inputs():
        import jax
        import jax.numpy as jnp
        _rk = jax.random.key(seed)
        x = -0.0003929 + 0.9999 * jax.random.normal(jax.random.fold_in(_rk, 1), (4, 256, 256), jnp.float32)
        _lenS = 256 - jax.random.randint(jax.random.fold_in(_rk, 7), (4,), 0, max(1, 256 // 4) + 1, jnp.int32)
        _lenS2 = 256 - jax.random.randint(jax.random.fold_in(_rk, 8), (4,), 0, max(1, 256 // 4) + 1, jnp.int32)
        _ctx_2048P = jax.random.normal(jax.random.fold_in(_rk, 11), (4, 16, 256), jnp.float32)
        _ctx_2048c = jax.random.dirichlet(jax.random.fold_in(_rk, 511), 0.3 * jnp.ones((16,), jnp.float32), (4, 256))
        _ctx_2048t = jnp.einsum('bsk,bkd->bsd', _ctx_2048c, _ctx_2048P)
        _ctx_2048t = _ctx_2048t * jax.lax.rsqrt(jnp.mean(jnp.square(_ctx_2048t)) + 1e-12) * 0.953939
        ctx_2048 = -0.000514642 + 1.00011 * (_ctx_2048t + 0.3 * jax.random.normal(jax.random.fold_in(_rk, 611), (4, 256, 256), jnp.float32))
        itok_BxS_0_1023 = jax.random.randint(jax.random.fold_in(_rk, 13), (4, 256), 0, 128, jnp.int32)
        _validS = jnp.arange(256)[None, :] < _lenS[:, None]
        _validS2 = jnp.arange(256)[None, :] < _lenS2[:, None]
        _causal = jnp.tril(jnp.ones((256, 256), dtype=bool))
        mask_BxSxS2_ff0 = jnp.where(jnp.ones((4, 256, 256), dtype=bool), 0.0, -1000000000.0).astype(jnp.float32)
        return (x, ctx_2048, itok_BxS_0_1023, mask_BxSxS2_ff0)
    x, ctx_2048, itok_BxS_0_1023, mask_BxSxS2_ff0 = _rec_inputs()

    def _L0_xattn_setup():
        import jax, jax.numpy as jnp
        import numpy as np
        NUM_HEADS = 16
        EPS = 1e-08

        def _dyn_quant(x):
            s = jnp.maximum(jnp.max(jnp.abs(x), axis=-1, keepdims=True) / 127.0, EPS)
            q = jnp.clip(jnp.round(x / s), -127.0, 127.0)
            return (q, s)

        def _quant_weight(w):
            s = jnp.maximum(jnp.max(jnp.abs(w), axis=1, keepdims=True) / 127.0, EPS)
            q = jnp.clip(jnp.round(w / s), -127.0, 127.0)
            return (q, s)

        def _w8a8_linear(x, w, b):
            qx, sx = _dyn_quant(x)
            qw, sw = _quant_weight(w)
            y = jnp.einsum('bnc,oc->bno', qx, qw) * (sx * sw[:, 0])
            return y + b
        key = jax.random.key(seed)
        ks = jax.random.split(key, 9)
        B, N, L, C = (2, 512, 64, 256)
        sc = 0.02
        return {'x': jax.random.normal(ks[0], (B, N, C), jnp.float32), 'cond': jax.random.normal(ks[1], (B, L, C), jnp.float32), 'mask': jnp.zeros((B, N, L), jnp.float32), 'wq': jax.random.normal(ks[2], (C, C), jnp.float32) * sc, 'bq': jnp.zeros((C,), jnp.float32), 'wk': jax.random.normal(ks[3], (C, C), jnp.float32) * sc, 'bk': jnp.zeros((C,), jnp.float32), 'wv': jax.random.normal(ks[4], (C, C), jnp.float32) * sc, 'bv': jnp.zeros((C,), jnp.float32), 'wo': jax.random.normal(ks[5], (C, C), jnp.float32) * sc, 'bo': jnp.zeros((C,), jnp.float32)}
    _L0_xattn_all = _L0_xattn_setup()
    _L0_xattn_in = {k: v for k, v in _L0_xattn_all.items() if k in ('wq', 'bq', 'wk', 'bk', 'wv', 'bv', 'wo', 'bo')}
    del _L0_xattn_all

    def _L0_ffn_setup():
        import jax, jax.numpy as jnp
        import numpy as np
        GOLDEN_CENTER = 1.0 / np.e
        GOLDEN_LOWER = 0.5 - np.log(4.0 / 3.0)
        GOLDEN_UPPER = 0.5

        def _golden_weights(x, Wr, temperature):
            inh = jax.nn.sigmoid(x @ Wr / temperature)
            in_zone = (inh >= GOLDEN_LOWER) & (inh <= GOLDEN_UPPER)
            distance = jnp.abs(inh - GOLDEN_CENTER)
            weights = jnp.exp(-distance / 0.1) * in_zone.astype(x.dtype)
            wsum = jnp.sum(weights, axis=-1, keepdims=True)
            no_expert = wsum < 1e-08
            fb = jnp.exp(-distance / 0.3)
            _, top2 = jax.lax.top_k(fb, 2)
            fb_mask = jnp.sum(jax.nn.one_hot(top2, weights.shape[-1], dtype=x.dtype), axis=-2)
            fb_w = fb * fb_mask
            fb_w = fb_w / jnp.maximum(jnp.sum(fb_w, axis=-1, keepdims=True), 1e-08)
            weights = jnp.where(no_expert, fb_w, weights)
            weights = weights / jnp.maximum(jnp.sum(weights, axis=-1, keepdims=True), 1e-08)
            return weights
        key = jax.random.key(seed)
        ks = jax.random.split(key, 5)
        B, T, D, E, F = (2, 256, 256, 8, 256)
        s_in = 1.0 / np.sqrt(D)
        s_f = 1.0 / np.sqrt(F)
        return {'x': jax.random.normal(ks[0], (B, T, D), dtype=jnp.float32), 'Wg': jax.random.normal(ks[1], (E, D, F), dtype=jnp.float32) * s_in, 'Wu': jax.random.normal(ks[2], (E, D, F), dtype=jnp.float32) * s_in, 'Wd': jax.random.normal(ks[3], (E, F, D), dtype=jnp.float32) * s_f, 'Wr': jax.random.normal(ks[4], (D, E), dtype=jnp.float32) * s_in, 'temperature': jnp.ones((1,), dtype=jnp.float32)}
    _L0_ffn_all = _L0_ffn_setup()
    _L0_ffn_in = {k: v for k, v in _L0_ffn_all.items() if k in ('Wg', 'Wu', 'Wd', 'Wr', 'temperature')}
    del _L0_ffn_all

    def _L1_xattn_setup():
        import jax, jax.numpy as jnp
        import numpy as np
        B, Lq, Lk = (2, 512, 128)
        Q_DIM, KV_DIM = (256, 256)
        H, HD = (16, 128)
        KVC, QC, R = (64, 96, 64)
        LOOKBACK = 8
        NEG = -1e+30

        def _rope(x, L):
            half = x.shape[-1] // 2
            inv_freq = 1.0 / 10000.0 ** (jnp.arange(half, dtype=jnp.float32) / half)
            ang = jnp.arange(L, dtype=jnp.float32)[:, None] * inv_freq
            cos, sin = (jnp.cos(ang), jnp.sin(ang))
            x1, x2 = (x[..., :half], x[..., half:])
            return jnp.concatenate([x1 * cos - x2 * sin, x1 * sin + x2 * cos], axis=-1)
        key = jax.random.key(seed)
        ks = jax.random.split(key, 11)

        def w(k, shape, fan_in):
            return jax.random.normal(k, shape, jnp.float32) / np.sqrt(fan_in).astype(np.float32)
        return {'q': jax.random.normal(ks[0], (B, Lq, Q_DIM), jnp.float32), 'kv': jax.random.normal(ks[1], (B, Lk, KV_DIM), jnp.float32), 'seg_id': jnp.sort(jax.random.randint(ks[2], (B, Lq), 0, Lk), axis=-1), 'W_kvc': w(ks[3], (KV_DIM, KVC), KV_DIM), 'W_dq': w(ks[4], (Q_DIM, QC), Q_DIM), 'W_uq': w(ks[5], (QC, H * HD), QC), 'W_qr': w(ks[6], (QC, H * R), QC), 'W_uk': w(ks[7], (KVC, H * HD), KVC), 'W_kr': w(ks[8], (KVC, R), KVC), 'W_uv': w(ks[9], (KVC, H * HD), KVC), 'W_o': w(ks[10], (H * HD, Q_DIM), H * HD)}
    _L1_xattn_all = _L1_xattn_setup()
    _L1_xattn_in = {k: v for k, v in _L1_xattn_all.items() if k in ('W_kvc', 'W_dq', 'W_uq', 'W_qr', 'W_uk', 'W_kr', 'W_uv', 'W_o')}
    del _L1_xattn_all

    def _L1_ffn_setup():
        import jax, jax.numpy as jnp
        import numpy as np
        H = 256
        NH = 32
        KVH = 4
        HD = 128
        E = 32
        TOPK = 8
        I = 128
        EPS = 1e-05
        THETA = 10000.0

        def _rmsnorm(x, w, eps=EPS):
            xf = x.astype(jnp.float32)
            var = jnp.mean(xf * xf, axis=-1, keepdims=True)
            return (w * (xf * jax.lax.rsqrt(var + eps))).astype(x.dtype)

        def _rope(x, pos):
            d = x.shape[-1]
            inv_freq = 1.0 / THETA ** (jnp.arange(0, d, 2, dtype=jnp.float32) / d)
            ang = pos.astype(jnp.float32)[:, None] * inv_freq[None, :]
            cos = jnp.cos(ang)[None, :, None, :]
            sin = jnp.sin(ang)[None, :, None, :]
            x1, x2 = jnp.split(x, 2, axis=-1)
            return jnp.concatenate([x1 * cos - x2 * sin, x1 * sin + x2 * cos], axis=-1)
        key = jax.random.key(seed)
        ks = jax.random.split(key, 16)
        s = 0.02
        n = lambda k, shape: jax.random.normal(k, shape, dtype=jnp.float32) * s
        return {'hidden_states': jax.random.normal(ks[0], (1, 64, H), dtype=jnp.float32), 'ln1_w': jnp.ones((H,), jnp.float32), 'ln2_w': jnp.ones((H,), jnp.float32), 'Wq': n(ks[1], (H, NH * HD)), 'Wk': n(ks[2], (H, KVH * HD)), 'Wv': n(ks[3], (H, KVH * HD)), 'Wo': n(ks[4], (NH * HD, H)), 'Wr': n(ks[5], (H, E)), 'expert_bias': jax.random.normal(ks[6], (E,), dtype=jnp.float32) * 0.1, 'Wg': n(ks[7], (E, H, I)), 'Wu': n(ks[8], (E, H, I)), 'Wd': n(ks[9], (E, I, H)), 'Wsg': n(ks[10], (H, I)), 'Wsu': n(ks[11], (H, I)), 'Wsd': n(ks[12], (I, H))}
    _L1_ffn_all = _L1_ffn_setup()
    _L1_ffn_in = {k: v for k, v in _L1_ffn_all.items() if k in ('ln1_w', 'ln2_w', 'Wq', 'Wk', 'Wv', 'Wo', 'Wr', 'expert_bias', 'Wg', 'Wu', 'Wd', 'Wsg', 'Wsu', 'Wsd')}
    del _L1_ffn_all
    return {'x': x, 'ctx_2048': ctx_2048, 'itok_BxS_0_1023': itok_BxS_0_1023, 'mask_BxSxS2_ff0': mask_BxSxS2_ff0, 'L0_xattn_wq': _L0_xattn_in['wq'], 'L0_xattn_bq': _L0_xattn_in['bq'], 'L0_xattn_wk': _L0_xattn_in['wk'], 'L0_xattn_bk': _L0_xattn_in['bk'], 'L0_xattn_wv': _L0_xattn_in['wv'], 'L0_xattn_bv': _L0_xattn_in['bv'], 'L0_xattn_wo': _L0_xattn_in['wo'], 'L0_xattn_bo': _L0_xattn_in['bo'], 'L0_ffn_Wg': _L0_ffn_in['Wg'], 'L0_ffn_Wu': _L0_ffn_in['Wu'], 'L0_ffn_Wd': _L0_ffn_in['Wd'], 'L0_ffn_Wr': _L0_ffn_in['Wr'], 'L0_ffn_temperature': _L0_ffn_in['temperature'], 'L1_xattn_W_kvc': _L1_xattn_in['W_kvc'], 'L1_xattn_W_dq': _L1_xattn_in['W_dq'], 'L1_xattn_W_uq': _L1_xattn_in['W_uq'], 'L1_xattn_W_qr': _L1_xattn_in['W_qr'], 'L1_xattn_W_uk': _L1_xattn_in['W_uk'], 'L1_xattn_W_kr': _L1_xattn_in['W_kr'], 'L1_xattn_W_uv': _L1_xattn_in['W_uv'], 'L1_xattn_W_o': _L1_xattn_in['W_o'], 'L1_ffn_ln1_w': _L1_ffn_in['ln1_w'], 'L1_ffn_ln2_w': _L1_ffn_in['ln2_w'], 'L1_ffn_Wq': _L1_ffn_in['Wq'], 'L1_ffn_Wk': _L1_ffn_in['Wk'], 'L1_ffn_Wv': _L1_ffn_in['Wv'], 'L1_ffn_Wo': _L1_ffn_in['Wo'], 'L1_ffn_Wr': _L1_ffn_in['Wr'], 'L1_ffn_expert_bias': _L1_ffn_in['expert_bias'], 'L1_ffn_Wg': _L1_ffn_in['Wg'], 'L1_ffn_Wu': _L1_ffn_in['Wu'], 'L1_ffn_Wd': _L1_ffn_in['Wd'], 'L1_ffn_Wsg': _L1_ffn_in['Wsg'], 'L1_ffn_Wsu': _L1_ffn_in['Wsu'], 'L1_ffn_Wsd': _L1_ffn_in['Wsd']}

def reference(x, ctx_2048, itok_BxS_0_1023, mask_BxSxS2_ff0, L0_xattn_wq, L0_xattn_bq, L0_xattn_wk, L0_xattn_bk, L0_xattn_wv, L0_xattn_bv, L0_xattn_wo, L0_xattn_bo, L0_ffn_Wg, L0_ffn_Wu, L0_ffn_Wd, L0_ffn_Wr, L0_ffn_temperature, L1_xattn_W_kvc, L1_xattn_W_dq, L1_xattn_W_uq, L1_xattn_W_qr, L1_xattn_W_uk, L1_xattn_W_kr, L1_xattn_W_uv, L1_xattn_W_o, L1_ffn_ln1_w, L1_ffn_ln2_w, L1_ffn_Wq, L1_ffn_Wk, L1_ffn_Wv, L1_ffn_Wo, L1_ffn_Wr, L1_ffn_expert_bias, L1_ffn_Wg, L1_ffn_Wu, L1_ffn_Wd, L1_ffn_Wsg, L1_ffn_Wsu, L1_ffn_Wsd):
    import jax
    import jax.numpy as jnp

    def _L0_xattn_ref(x, cond, mask, wq, bq, wk, bk, wv, bv, wo, bo):
        import jax, jax.numpy as jnp
        import numpy as np
        NUM_HEADS = 16
        EPS = 1e-08

        def _dyn_quant(x):
            s = jnp.maximum(jnp.max(jnp.abs(x), axis=-1, keepdims=True) / 127.0, EPS)
            q = jnp.clip(jnp.round(x / s), -127.0, 127.0)
            return (q, s)

        def _quant_weight(w):
            s = jnp.maximum(jnp.max(jnp.abs(w), axis=1, keepdims=True) / 127.0, EPS)
            q = jnp.clip(jnp.round(w / s), -127.0, 127.0)
            return (q, s)

        def _w8a8_linear(x, w, b):
            qx, sx = _dyn_quant(x)
            qw, sw = _quant_weight(w)
            y = jnp.einsum('bnc,oc->bno', qx, qw) * (sx * sw[:, 0])
            return y + b
        B, N, C = x.shape
        L = cond.shape[1]
        H = NUM_HEADS
        D = C // H
        inv_sqrt_d = np.float32(1.0 / np.sqrt(D))
        q = _w8a8_linear(x, wq, bq).reshape(B, N, H, D).transpose(0, 2, 1, 3)
        k = (cond @ wk.T + bk).reshape(B, L, H, D).transpose(0, 2, 1, 3)
        v = (cond @ wv.T + bv).reshape(B, L, H, D).transpose(0, 2, 1, 3)
        scores = jnp.einsum('bhnd,bhld->bhnl', q, k) * inv_sqrt_d + mask[:, None]
        attn = jax.nn.softmax(scores, axis=-1)
        o = jnp.einsum('bhnl,bhld->bhnd', attn, v)
        o = o.transpose(0, 2, 1, 3).reshape(B, N, C)
        return _w8a8_linear(o, wo, bo)

    def _L0_ffn_ref(x, Wg, Wu, Wd, Wr, temperature):
        import jax, jax.numpy as jnp
        import numpy as np
        GOLDEN_CENTER = 1.0 / np.e
        GOLDEN_LOWER = 0.5 - np.log(4.0 / 3.0)
        GOLDEN_UPPER = 0.5

        def _golden_weights(x, Wr, temperature):
            inh = jax.nn.sigmoid(x @ Wr / temperature)
            in_zone = (inh >= GOLDEN_LOWER) & (inh <= GOLDEN_UPPER)
            distance = jnp.abs(inh - GOLDEN_CENTER)
            weights = jnp.exp(-distance / 0.1) * in_zone.astype(x.dtype)
            wsum = jnp.sum(weights, axis=-1, keepdims=True)
            no_expert = wsum < 1e-08
            fb = jnp.exp(-distance / 0.3)
            _, top2 = jax.lax.top_k(fb, 2)
            fb_mask = jnp.sum(jax.nn.one_hot(top2, weights.shape[-1], dtype=x.dtype), axis=-2)
            fb_w = fb * fb_mask
            fb_w = fb_w / jnp.maximum(jnp.sum(fb_w, axis=-1, keepdims=True), 1e-08)
            weights = jnp.where(no_expert, fb_w, weights)
            weights = weights / jnp.maximum(jnp.sum(weights, axis=-1, keepdims=True), 1e-08)
            return weights
        weights = _golden_weights(x, Wr, temperature)
        gate = jnp.einsum('btd,edf->betf', x, Wg)
        up = jnp.einsum('btd,edf->betf', x, Wu)
        h = jax.nn.silu(gate) * up
        e_out = jnp.einsum('betf,efd->betd', h, Wd)
        out = jnp.einsum('bte,betd->btd', weights, e_out)
        return out

    def _L1_xattn_ref(q, kv, seg_id, W_kvc, W_dq, W_uq, W_qr, W_uk, W_kr, W_uv, W_o):
        import jax, jax.numpy as jnp
        import numpy as np
        B, Lq, Lk = (2, 512, 128)
        Q_DIM, KV_DIM = (256, 256)
        H, HD = (16, 128)
        KVC, QC, R = (64, 96, 64)
        LOOKBACK = 8
        NEG = -1e+30

        def _rope(x, L):
            half = x.shape[-1] // 2
            inv_freq = 1.0 / 10000.0 ** (jnp.arange(half, dtype=jnp.float32) / half)
            ang = jnp.arange(L, dtype=jnp.float32)[:, None] * inv_freq
            cos, sin = (jnp.cos(ang), jnp.sin(ang))
            x1, x2 = (x[..., :half], x[..., half:])
            return jnp.concatenate([x1 * cos - x2 * sin, x1 * sin + x2 * cos], axis=-1)
        b, lq, _ = q.shape
        lk = kv.shape[1]
        kv_c = kv @ W_kvc
        q_c = q @ W_dq
        q_nope = (q_c @ W_uq).reshape(b, lq, H, HD).transpose(0, 2, 1, 3)
        q_rope = (q_c @ W_qr).reshape(b, lq, H, R).transpose(0, 2, 1, 3)
        k_nope = (kv_c @ W_uk).reshape(b, lk, H, HD)
        v = (kv_c @ W_uv).reshape(b, lk, H, HD)
        k_rope = kv_c @ W_kr
        q_rope = _rope(q_rope, lq)
        k_rope = _rope(k_rope, lk)
        scale = 1.0 / np.sqrt(HD + R).astype(np.float32)
        scores = (jnp.einsum('bhqd,bkhd->bhqk', q_nope, k_nope) + jnp.einsum('bhqr,bkr->bhqk', q_rope, k_rope)) * scale
        k_ids = jnp.arange(lk)[None, None, :]
        qs = seg_id[:, :, None]
        good = (k_ids <= qs) & (k_ids >= qs - LOOKBACK)
        scores = jnp.where(good[:, None, :, :], scores, NEG)
        attn = jax.nn.softmax(scores, axis=-1)
        out = jnp.einsum('bhqk,bkhd->bqhd', attn, v).reshape(b, lq, H * HD)
        return out @ W_o

    def _L1_ffn_ref(hidden_states, ln1_w, ln2_w, Wq, Wk, Wv, Wo, Wr, expert_bias, Wg, Wu, Wd, Wsg, Wsu, Wsd):
        import jax, jax.numpy as jnp
        import numpy as np
        H = 256
        NH = 32
        KVH = 4
        HD = 128
        E = 32
        TOPK = 8
        I = 128
        EPS = 1e-05
        THETA = 10000.0

        def _rmsnorm(x, w, eps=EPS):
            xf = x.astype(jnp.float32)
            var = jnp.mean(xf * xf, axis=-1, keepdims=True)
            return (w * (xf * jax.lax.rsqrt(var + eps))).astype(x.dtype)

        def _rope(x, pos):
            d = x.shape[-1]
            inv_freq = 1.0 / THETA ** (jnp.arange(0, d, 2, dtype=jnp.float32) / d)
            ang = pos.astype(jnp.float32)[:, None] * inv_freq[None, :]
            cos = jnp.cos(ang)[None, :, None, :]
            sin = jnp.sin(ang)[None, :, None, :]
            x1, x2 = jnp.split(x, 2, axis=-1)
            return jnp.concatenate([x1 * cos - x2 * sin, x1 * sin + x2 * cos], axis=-1)
        B, S, _ = hidden_states.shape
        resid = hidden_states
        h = _rmsnorm(hidden_states, ln1_w)
        pos = jnp.arange(S)
        q = (h @ Wq).reshape(B, S, NH, HD)
        k = (h @ Wk).reshape(B, S, KVH, HD)
        v = (h @ Wv).reshape(B, S, KVH, HD)
        q = _rope(q, pos)
        k = _rope(k, pos)
        rep = NH // KVH
        k = jnp.repeat(k, rep, axis=2)
        v = jnp.repeat(v, rep, axis=2)
        scores = jnp.einsum('bqhd,bkhd->bhqk', q, k) / jnp.sqrt(jnp.float32(HD))
        causal = jnp.tril(jnp.ones((S, S), dtype=bool))
        scores = jnp.where(causal[None, None], scores, jnp.float32(-1000000000.0))
        attn = jax.nn.softmax(scores, axis=-1)
        o = jnp.einsum('bhqk,bkhd->bqhd', attn, v).reshape(B, S, NH * HD) @ Wo
        x = resid + o
        resid = x
        h = _rmsnorm(x, ln2_w)
        t = h.reshape(-1, H)
        T = t.shape[0]
        router_scores = jax.nn.sigmoid(t @ Wr)
        _, idx = jax.lax.top_k(router_scores + expert_bias[None, :], TOPK)
        w = jnp.take_along_axis(router_scores, idx, axis=1)
        w = w / jnp.sum(w, axis=-1, keepdims=True)
        wfull = jnp.zeros((T, E), jnp.float32).at[jnp.arange(T)[:, None], idx].set(w)
        g = jnp.einsum('th,ehi->tei', t, Wg)
        u = jnp.einsum('th,ehi->tei', t, Wu)
        act = jax.nn.silu(g) * u
        moe = jnp.einsum('tei,te,eih->th', act, wfull, Wd)
        shared = jax.nn.silu(t @ Wsg) * (t @ Wsu) @ Wsd
        return resid + (moe + shared).reshape(B, S, H)
    x = x + _L0_xattn_ref(_layernorm(x, axis=-1), ctx_2048, mask_BxSxS2_ff0, L0_xattn_wq, L0_xattn_bq, L0_xattn_wk, L0_xattn_bk, L0_xattn_wv, L0_xattn_bv, L0_xattn_wo, L0_xattn_bo)
    x = x + _L0_ffn_ref(_layernorm(x, axis=-1), L0_ffn_Wg, L0_ffn_Wu, L0_ffn_Wd, L0_ffn_Wr, L0_ffn_temperature)
    x = x + _L1_xattn_ref(_layernorm(x, axis=-1), ctx_2048, itok_BxS_0_1023, L1_xattn_W_kvc, L1_xattn_W_dq, L1_xattn_W_uq, L1_xattn_W_qr, L1_xattn_W_uk, L1_xattn_W_kr, L1_xattn_W_uv, L1_xattn_W_o)
    x = x + _L1_ffn_ref(_layernorm(x, axis=-1), L1_ffn_ln1_w, L1_ffn_ln2_w, L1_ffn_Wq, L1_ffn_Wk, L1_ffn_Wv, L1_ffn_Wo, L1_ffn_Wr, L1_ffn_expert_bias, L1_ffn_Wg, L1_ffn_Wu, L1_ffn_Wd, L1_ffn_Wsg, L1_ffn_Wsu, L1_ffn_Wsd)
    return x

_drawn_inputs = setup_inputs


def setup_inputs(seed=0):
    import zlib

    import numpy as np

    out = dict(_drawn_inputs(seed))
    spreads = {'L0_xattn_bq': (0.0, 0.8),
     'L0_xattn_bk': (0.0, 0.8),
     'L0_xattn_bv': (0.0, 0.1),
     'L0_xattn_bo': (0.0, 0.1),
     'L1_ffn_ln1_w': (1.0, 0.6),
     'L1_ffn_ln2_w': (1.0, 0.6)}
    factors = {'L0_xattn_wq': 5.314,
     'L0_xattn_wk': 4.545,
     'L1_ffn_Wq': 8.0,
     'L1_ffn_Wk': 8.0,
     'L1_ffn_Wr': 8.0,
     'L1_ffn_expert_bias': 8.0,
     'L1_ffn_Wg': 8.0,
     'L1_ffn_Wu': 8.0,
     'L1_ffn_Wd': 8.0,
     'L1_ffn_Wsg': 8.0,
     'L1_ffn_Wsu': 8.0,
     'L1_ffn_Wsd': 8.0}
    for name, (base, spread) in spreads.items():
        noise = np.random.default_rng([zlib.crc32(name.encode()), seed]).standard_normal(out[name].shape)
        drawn = base * np.exp(spread * noise) if base else spread * noise
        out[name] = jnp.asarray(drawn.astype(out[name].dtype))
    for name, factor in factors.items():
        out[name] = (out[name] * factor).astype(out[name].dtype)
    return out
```

```python
import math
from contextlib import ExitStack

import concourse.bass as bass
from concourse import mybir

F32 = mybir.dt.float32
F32R = mybir.dt.float32r
BF16 = mybir.dt.bfloat16
I32 = mybir.dt.int32
ALU = mybir.AluOpType
ACT = mybir.ActivationFunctionType
AX_X = mybir.AxisListType.X

P = 128
B, S, D = 4, 256, 256
TOK = B * S
NT = TOK // P
KD = D // P
MAGIC = 1.5 * 2.0 ** 23
NEG = -1e30


class Env:

    def __init__(self, nc, ctx, dram):
        self.nc, self.ctx, self.dram = nc, ctx, dram
        self.stage_ctx, self.stage_sems = ctx, []

    def sb(self, name, shape, dt=F32, ctx=None):
        return (ctx or self.ctx).enter_context(self.nc.sbuf_tensor(name, shape, dt))

    def sem(self, name):
        handle = self.stage_ctx.enter_context(self.nc.semaphore(name))
        self.stage_sems.append(handle)
        return handle

    def stage(self, build):
        with ExitStack() as self.stage_ctx:
            self.stage_sems = []
            build()
            numbers = sorted(s.num for s in self.stage_sems)
            runs, first = [], numbers[0]
            for a, b in zip(numbers, numbers[1:] + [None]):
                if b != a + 1:
                    runs.append(range(first, a + 1))
                    first = b
            with self.nc.Block() as block:
                @block.sync
                def _(sp):
                    for run in runs:
                        sp.sem_clear(run)


def tokens(t):
    return slice(t * P, (t + 1) * P)


def wait_from_one(eng, sem, value):
    if not isinstance(value, int) or value > 0:
        eng.wait_ge(sem, value)


def split3(pe, out, a, b, start, stop):
    (ah, al), (bh, bl) = a, b
    pe.matmul(out, ah, bh, start=start, stop=False, skip_group_check=True)
    pe.matmul(out, ah, bl, start=False, stop=False, skip_group_check=True)
    return pe.matmul(out, al, bh, start=False, stop=stop, skip_group_check=True)


class Norm:

    def __init__(self, env, tag, mem, rms_weight=None, dst=None):
        self.e, self.tag, self.rms = env, tag, rms_weight
        sb = lambda n, s, d=F32: env.sb(f"{tag}_{n}", s, d, mem)
        self.stats = sb("bn_stats", [P, NT, 6])
        self.moments = sb("moments", [P, NT, 2])
        self.square = sb("square", [P, D]) if rms_weight is not None else None
        self.var_eps = sb("var_eps", [P, NT])
        self.rstd = sb("rstd", [P, NT])
        self.xn = sb("xn", [P, NT, D]) if dst is None else dst
        s = lambda n: env.sem(f"{tag}_{n}")
        self.s_stats, self.s_moments, self.s_var = s("stats_done"), s("moments_done"), s("var_done")
        self.s_rstd, self.s_xn = s("rstd_done"), s("xn_ready")
        self.s_tr, self.s_hi, self.s_lo = s("xT_in_psum"), s("xT_hi_ready"), s("xT_lo_ready")

    def scalar_stats(self, act):
        for t in range(NT):
            if t:
                act.wait_ge(self.s_stats, t)
            act.activation(self.square[:], self.e.x[:, t, :], ACT.Square,
                           accum_out=self.moments[:, t, 0:1]).then_inc(self.s_stats, 1)

    def vector_normalise(self, dve, kept=None):
        x = self.e.x
        if self.rms is None:
            for t in range(NT):
                dve.bn_stats(self.stats[:, t, :], x[:, t, :]).then_inc(self.s_stats, 1)
            for t in range(NT):
                dve.wait_ge(self.s_stats, t + 1)
                dve.bn_aggr(self.moments[:, t, :], self.stats[:, t, :]).then_inc(self.s_moments, 1)
            dve.wait_ge(self.s_moments, NT)
            dve.tensor_scalar(self.var_eps[:], self.moments[:, :, 1], 1e-5, None, ALU.add).then_inc(self.s_var, 1)
        else:
            dve.wait_ge(self.s_stats, NT)
            dve.tensor_scalar(self.var_eps[:], self.moments[:, :, 0], 1.0 / D, 1e-5,
                              ALU.mult, ALU.add).then_inc(self.s_var, 1)
        dve.wait_ge(self.s_rstd, 1)
        if kept is not None:
            dve.wait_ge(kept, 1)
        for t in range(NT):
            if self.rms is None:
                dve.tensor_scalar(self.xn[:, t, :], x[:, t, :], self.moments[:, t, 0:1], self.rstd[:, t:t + 1],
                                  ALU.subtract, ALU.mult).then_inc(self.s_xn, 1)
            else:
                dve.scalar_tensor_tensor(self.xn[:, t, :], x[:, t, :], self.rstd[:, t:t + 1], self.rms[:],
                                         ALU.mult, ALU.mult).then_inc(self.s_xn, 1)

    def gpsimd_rstd(self, pool):
        pool.wait_ge(self.s_var, 1)
        pool.tensor_tensor(self.rstd[:], self.var_eps[:], self.e.minus_half[:], ALU.pow).then_inc(self.s_rstd, 1)

    def tensor_transpose(self, pe, banks):
        for b in range(B):
            pe.wait_ge(self.s_xn, 2 * b + 2)
            if b >= 2:
                pe.wait_ge(self.s_lo, b - 1)
            bank = banks[b % 2][:].rearrange("p (k t q) -> p k t q", k=KD, t=2)
            for k in range(KD):
                for t in range(2):
                    last = pe.transpose(bank[:, k, t, :], self.xn[:, 2 * b + t, k * P:(k + 1) * P], self.e.ident[:])
            last.then_inc(self.s_tr, 1)

    def scalar_hi(self, act, banks, hi):
        for b in range(B):
            act.wait_ge(self.s_tr, b + 1)
            act.activation(hi[:, :, b * S:(b + 1) * S], banks[b % 2][:].rearrange("p (k q) -> p k q", k=KD),
                           ACT.Copy).then_inc(self.s_hi, 1)

    def vector_lo(self, dve, banks, hi, lo):
        for b in range(B):
            dve.wait_ge(self.s_hi, b + 1)
            cols = slice(b * S, (b + 1) * S)
            dve.tensor_tensor(lo[:, :, cols], banks[b % 2][:].rearrange("p (k q) -> p k q", k=KD),
                              hi[:, :, cols].bitcast(F32), ALU.subtract).then_inc(self.s_lo, 1)
H0, HD0 = 16, 16
HG0 = 4
NG0 = H0 // HG0
QMAX, QEPS = 127.0, 1e-8


class Quant:

    def __init__(self, env, tag, mem, n):
        self.n = n
        self.scale, self.inv = env.sb(f"{tag}_scale", [P, n], F32, mem), env.sb(f"{tag}_inv", [P, n], F32, mem)
        self.work = env.sb(f"{tag}_work", [P, n, D], F32, mem)
        self.whole = env.sb(f"{tag}_whole", [P, n, D], BF16, mem)
        self.stepped, self.ready = env.sem(f"{tag}_stepped"), env.sem(f"{tag}_ready")

    def run(self, dve, rows):
        n = self.n
        dve.tensor_reduce(self.scale[:], rows, AX_X, ALU.max, apply_absolute_value=True).then_inc(self.stepped, 1)
        dve.wait_ge(self.stepped, 1)
        dve.tensor_scalar(self.scale[:], self.scale[:], 1.0 / QMAX, QEPS, ALU.mult, ALU.max).then_inc(self.stepped, 1)
        dve.wait_ge(self.stepped, 2)
        dve.reciprocal(self.inv[:], self.scale[:]).then_inc(self.stepped, 1)
        dve.wait_ge(self.stepped, 3)
        for i in range(n):
            dve.tensor_scalar(self.work[:, i, :], rows[:, i, :], self.inv[:, i:i + 1], QMAX,
                              ALU.mult, ALU.min).then_inc(self.stepped, 1)
        dve.wait_ge(self.stepped, 3 + n)
        dve.tensor_scalar(self.work[:], self.work[:], -QMAX, MAGIC, ALU.max, ALU.add).then_inc(self.stepped, 1)
        dve.wait_ge(self.stepped, 4 + n)
        dve.tensor_scalar(self.whole[:], self.work[:], MAGIC, None, ALU.subtract).then_inc(self.ready, 1)


def quantised_attention(env):
    nc, dram, x = env.nc, env.dram, env.x
    bank = env.bank
    with ExitStack() as mem:
        sb = lambda n, s, d=F32: env.sb(f"qa_{n}", s, d, mem)
        sem = lambda n: env.sem(f"qa_{n}")
        q_tok, kv_tok, o_tok = sb("q_tok", [P, NT, D]), sb("kv_tok", [P, NT, 2 * D]), sb("o_tok", [P, NT, D])
        mask = sb("mask", [P, NT, S])
        w_rows = sb("w_rows", [P, 2, D])
        wT = sb("wT", [P, 2, KD, D], BF16)
        bias_rows = sb("bias_rows", [P, 4, D])
        s_in, s_mask = sem("inputs_loaded"), sem("mask_loaded")
        half_banks = lambda t: bank[4 + t // 2 % 4][:, (t % 2) * D:(t % 2 + 1) * D]

        def turn_rows(pe, quant, done):
            for n in range(2):
                v = bank[n][:].bitcast(BF16).rearrange("p (k t m) -> p k t m", k=KD, t=4)
                for k in range(KD):
                    for t in range(4):
                        last = pe.transpose(v[:, k, t, :], quant.whole[:, 4 * n + t, k * P:(k + 1) * P], env.ident_bf[:])
                last.then_inc(done, 1)

        with ExitStack() as prep:
            sp_ = lambda n, s, d=F32: env.sb(f"qa_{n}", s, d, prep)
            norm = Norm(env, "qa", prep)
            wq_wo = sp_("wq_wo", [P, 4, D])
            ctxT, wkvT = sp_("ctxT", [P, KD, TOK]), sp_("wkvT", [P, KD, 2 * D])
            c_hi, c_lo = sp_("c_hi", [P, KD, TOK], F32R), sp_("c_lo", [P, KD, TOK], F32R)
            wkv_hi, wkv_lo = sp_("wkv_hi", [P, KD, 2 * D], F32R), sp_("wkv_lo", [P, KD, 2 * D], F32R)
            ones, diag = sp_("ones", [P, P]), sp_("diag", [P, 4, P])
            xqT = sp_("xqT", [P, KD, TOK], BF16)
            wquant, xquant = Quant(env, "qa_wq", prep, 4), Quant(env, "qa_xq", prep, NT)
            s_hi, s_lo, s_ones = sem("hi_ready"), sem("lo_ready"), sem("ones_ready")
            s_diag, s_rows, s_rowc = sem("diag_ready"), sem("w_rows_in_psum"), sem("w_rows_copied")
            s_wTp, s_wT, s_xTp, s_xT = sem("wT_in_psum"), sem("wT_ready"), sem("xqT_in_psum"), sem("xqT_ready")
            s_kv, s_kvc, s_q, s_qs, s_qb = (sem(n) for n in (
                "kv_in_psum", "kv_ready", "q_in_psum", "q_scaled", "q_ready"))
            block = prep.enter_context(nc.Block())

            @block.sync
            def _(sp):
                for dst, name in ((wq_wo, "wq_wo"), (ctxT, "ctxT"), (wkvT, "wkvT"), (bias_rows, "l0_bias")):
                    sp.dma_start(dst[:], dram[name]).then_inc(s_in, 16)
                sp.dma_start(mask[:], dram["mask"]).then_inc(s_mask, 16)

            @block.gpsimd
            def _(pool):
                pool.memset(ones[:], 1.0).then_inc(s_ones, 1)
                norm.gpsimd_rstd(pool)
                pool.wait_ge(s_hi, 1)
                pool.tensor_tensor(wkv_lo[:], wkvT[:], wkv_hi[:].bitcast(F32), ALU.subtract).then_inc(s_lo, 1)
                pool.wait_ge(s_hi, 2)
                pool.tensor_tensor(c_lo[:], ctxT[:], c_hi[:].bitcast(F32), ALU.subtract).then_inc(s_lo, 1)

            @block.scalar
            def _(act):
                act.wait_ge(s_in, 64)
                act.activation(wkv_hi[:], wkvT[:], ACT.Copy).then_inc(s_hi, 1)
                act.activation(c_hi[:], ctxT[:], ACT.Copy).then_inc(s_hi, 1)
                act.wait_ge(s_rows, 1)
                act.activation(w_rows[:].rearrange("p w d -> p (w d)"), bank[0][:], ACT.Copy).then_inc(s_rowc, 1)
                act.wait_ge(s_wTp, 1)
                act.activation(wT[:].rearrange("p w k d -> p (w k d)"), bank[1][:].bitcast(BF16),
                               ACT.Copy).then_inc(s_wT, 1)
                for n in range(2):
                    act.wait_ge(s_xTp, n + 1)
                    act.activation(xqT[:, :, n * 512:(n + 1) * 512],
                                   bank[n][:].bitcast(BF16).rearrange("p (k q) -> p k q", k=KD), ACT.Copy).then_inc(s_xT, 1)

            @block.vector
            def _(dve):
                dve.wait_ge(s_in, 64)
                wquant.run(dve, wq_wo[:])
                for i in range(4):
                    dve.tensor_scalar(diag[:, i, :], env.ident[:], wquant.scale[:, i:i + 1], None, ALU.mult).then_inc(s_diag, 1)
                norm.vector_normalise(dve)
                dve.wait_ge(norm.s_xn, NT)
                xquant.run(dve, norm.xn[:])
                for t in range(NT):
                    dve.wait_ge(s_kv, t + 1)
                    dve.tensor_tensor(kv_tok[:, t, :], bank[2 + t % 2][:], bias_rows[:, 1:3, :].rearrange("p a d -> p (a d)"),
                                      ALU.add).then_inc(s_kvc, 1)
                dve.wait_ge(s_rowc, 1)
                for t in range(NT):
                    dve.wait_ge(s_q, t // 2 * 2 + 2)
                    dve.scalar_tensor_tensor(q_tok[:, t, :], half_banks(t), xquant.scale[:, t:t + 1], w_rows[:, 0, :],
                                             ALU.mult, ALU.mult).then_inc(s_qs, 1)
                dve.wait_ge(s_qs, NT)
                dve.tensor_tensor(q_tok[:], q_tok[:], bias_rows[:, 0, :].unsqueeze(1).broadcast_to([P, NT, D]),
                                  ALU.add).then_inc(s_qb, 1)
                dve.wait_ge(s_qb, 1)

            @block.tensor
            def _(pe):
                pe.wait_ge(s_ones, 1)
                pe.wait_ge(s_diag, 4)
                pe.matmul(bank[0][:], ones[:], diag[:].rearrange("p i m -> p (i m)"), start=True, stop=True).then_inc(s_rows, 1)
                pe.wait_ge(wquant.ready, 1)
                wb = bank[1][:].bitcast(BF16).rearrange("p (w k o m) -> p w k o m", w=2, k=KD, o=2)
                for w in range(2):
                    for k in range(KD):
                        for o in range(2):
                            last = pe.transpose(wb[:, w, k, o, :], wquant.whole[:, 2 * w + o, k * P:(k + 1) * P],
                                                env.ident_bf[:])
                last.then_inc(s_wTp, 1)
                pe.wait_ge(s_lo, 2)
                for t in range(NT):
                    if t >= 2:
                        pe.wait_ge(s_kvc, t - 1)
                    for k in range(KD):
                        last = split3(pe, bank[2 + t % 2][:], (c_hi[:, k, tokens(t)], c_lo[:, k, tokens(t)]),
                                      (wkv_hi[:, k, :], wkv_lo[:, k, :]), k == 0, k == KD - 1)
                    last.then_inc(s_kv, 1)
                pe.wait_ge(xquant.ready, 1)
                pe.wait_ge(s_rowc, 1)
                pe.wait_ge(s_wT, 1)
                turn_rows(pe, xquant, s_xTp)
                for t in range(NT):
                    pe.wait_ge(s_xT, t // 4 + 1)
                    for k in range(KD):
                        last = pe.matmul(half_banks(t), xqT[:, k, tokens(t)], wT[:, 0, k, :], start=k == 0, stop=k == KD - 1)
                    last.then_inc(s_q, 1)

        with ExitStack() as loop:
            sl = lambda n, s, d=F32: env.sb(f"qa_{n}", s, d, loop)
            qd, kd = sl("qd", [P, 2, HG0, 4, HD0], F32R), sl("kd", [P, 2, HG0, 4, HD0], F32R)
            qT = sl("qT", [P, 2, S], F32R)
            kT = sl("kT", [P, 2, 2, S], F32R)
            vp = sl("vp", [P, 2, HG0, 32])
            prob = sl("prob", [P, 4, 2, S])
            nmax, rsum, rinv = sl("nmax", [P, 4, 2]), sl("rsum", [P, 4, 2]), sl("rinv", [P, 4, 2])
            pT = sl("pT", [P, 2, HG0, S])
            oT = sl("oT", [P, S])
            s_zero = sem("zeros_ready")
            s_dh, s_dl, s_v = sem("parts_hi_ready"), sem("parts_lo_ready"), sem("values_ready")
            s_T, s_Ta, s_Tv = sem("qk_T_in_psum"), sem("q_and_low_keys_copied"), sem("high_keys_copied")
            s_s, s_sm, s_max, s_exp, s_inv = (sem(n) for n in (
                "scores_in_psum", "scores_masked", "max_ready", "exp_ready", "row_inverse_ready"))
            s_pT, s_pTa, s_pTv = sem("pT_in_psum"), sem("pT_copied_by_scalar"), sem("pT_copied_by_vector")
            s_o, s_oc, s_oT, s_done = sem("oT_in_psum"), sem("oT_copied"), sem("o_in_psum"), sem("o_ready")
            block = loop.enter_context(nc.Block())

            def slices(v, b, g, t, lo=0):
                w = v.shape[-1]
                flat = v[:].rearrange("p t d -> p (t d)")
                return flat[:, bass.ds(b * (2 * w) + g * (HG0 * HD0) + t * w + lo, HG0 * HD0)].rearrange(
                    "p (h d) -> p h d", h=HG0)

            twice = lambda v: v.unsqueeze(2).broadcast_to([P, HG0, 2, HD0])

            def pT_view(u):
                return pT[:, :, 2 * (u // 2):2 * (u // 2) + 2, (u % 2) * P:(u % 2 + 1) * P]

            def pT_bank(u):
                return bank[2 + u % 2][:].rearrange("p (k j n) -> p k j n", k=2, j=2)

            @block.gpsimd
            def _(pool):
                pool.memset(vp[:], 0.0).then_inc(s_zero, 1)
                pool.memset(kT[:].bitcast(F32), 0.0).then_inc(s_zero, 1)
                pool.wait_ge(s_zero, 2)
                with pool.Fori(0, B) as b:
                    with pool.Fori(0, NG0) as g:
                        it = b * NG0 + g
                        pool.wait_ge(s_done, 2 * it + 1)
                        for t in range(2):
                            pool.tensor_copy(vp[:, t, :, 0:HD0], slices(kv_tok, b, g, t, D)).then_inc(s_v, 1)

            @block.scalar
            def _(act):
                act.wait_ge(s_mask, 16)
                act.wait_ge(s_zero, 2)
                with act.Fori(0, B) as b:
                    with act.Fori(0, NG0) as g:
                        it = b * NG0 + g
                        for t in range(2):
                            act.activation(qd[:, t, :, 0:2, :], twice(slices(q_tok, b, g, t)), ACT.Copy).then_inc(s_dh, 1)
                            act.activation(kd[:, t, :, 0::2, :], twice(slices(kv_tok, b, g, t)), ACT.Copy).then_inc(s_dh, 1)
                        act.wait_ge(s_T, 2 * it + 1)
                        act.activation(kT[0:64, :, 0, :], bank[0][0:64, :].rearrange("p (a n) -> p a n", a=2),
                                       ACT.Copy).then_inc(s_Ta, 1)
                        act.wait_ge(s_T, 2 * it + 2)
                        act.activation(qT[:].rearrange("p a n -> p (a n)"), bank[1][:], ACT.Copy).then_inc(s_Ta, 1)
                        for u in range(4):
                            act.wait_ge(s_max, 4 * it + u + 1)
                            for j in range(2):
                                act.activation(prob[:, u, j, :], prob[:, u, j, :], ACT.Exp, bias=nmax[:, u, j:j + 1],
                                               accum_out=rsum[:, u, j:j + 1]).then_inc(s_exp, 1)
                            if u == 2:
                                act.wait_ge(s_pT, 4 * it + 1)
                                act.activation(pT_view(0), pT_bank(0), ACT.Copy).then_inc(s_pTa, 1)
                        act.wait_ge(s_pT, 4 * it + 3)
                        act.activation(pT_view(2), pT_bank(2), ACT.Copy).then_inc(s_pTa, 1)

            @block.vector
            def _(dve):
                dve.memset(nmax[:, 0, :], 0.0).then_inc(s_done, 1)
                dve.wait_ge(s_zero, 2)
                dve.wait_ge(s_mask, 16)
                with dve.Fori(0, B) as b:
                    with dve.Fori(0, NG0) as g:
                        it = b * NG0 + g
                        for t in range(2):
                            dve.wait_ge(s_dh, 4 * it + 2 * t + 2)
                            dve.tensor_tensor(qd[:, t, :, 2:4, :], twice(slices(q_tok, b, g, t)),
                                              qd[:, t, :, 0:2, :].bitcast(F32), ALU.subtract).then_inc(s_dl, 1)
                            dve.tensor_tensor(kd[:, t, :, 1::2, :], twice(slices(kv_tok, b, g, t)),
                                              kd[:, t, :, 0::2, :].bitcast(F32), ALU.subtract).then_inc(s_dl, 1)
                        dve.wait_ge(s_T, 2 * it + 1)
                        dve.tensor_copy(kT[64:P, :, 1, :], bank[0][64:P, :].rearrange("p (a n) -> p a n", a=2)).then_inc(s_Tv, 1)
                        for u in range(4):
                            dve.wait_ge(s_s, 4 * it + u + 1)
                            row = mask[:].rearrange("p t n -> p (t n)")[:, bass.ds(b * 2 * S + (u % 2) * S, S)]
                            dve.scalar_tensor_tensor(prob[:, u], bank[4 + u][:].rearrange("p (j n) -> p j n", j=2), 0.25,
                                                     row.unsqueeze(1).broadcast_to([P, 2, S]),
                                                     ALU.mult, ALU.add).then_inc(s_sm, 1)
                            dve.wait_ge(s_sm, 4 * it + u + 1)
                            dve.tensor_reduce(nmax[:, u, :], prob[:, u], AX_X, ALU.max, negate=True).then_inc(s_max, 1)
                        for u in (1, 3):
                            dve.wait_ge(s_pT, 4 * it + u + 1)
                            dve.tensor_copy(pT_view(u), pT_bank(u)).then_inc(s_pTv, 1)
                        dve.reciprocal(rinv[:], rsum[:]).then_inc(s_inv, 1)
                        for h in range(HG0):
                            if h % 2 == 0:
                                dve.wait_ge(s_o, 2 * it + h // 2 + 1)
                            r = slice(32 * h, 32 * h + 32)
                            dve.tensor_copy(oT[r, :], bank[h // 2][r, (h % 2) * S:(h % 2 + 1) * S]).then_inc(s_oc, 1)
                        dve.wait_ge(s_oT, it + 1)
                        dve.wait_ge(s_inv, it + 1)
                        for t in range(2):
                            o4 = bank[2][:, t * P:(t + 1) * P].rearrange("p (a j d) -> p a j d", a=2, j=2)
                            inv = rinv[:, t::2, :].unsqueeze(3).broadcast_to([P, 2, 2, HD0])
                            out = slices(o_tok, b, g, t).rearrange("p (a j) d -> p a j d", a=2)
                            dve.tensor_tensor(out, o4[:, :, :, 0:HD0], inv, ALU.mult).then_inc(s_done, 1)
                dve.wait_ge(s_done, 2 * B * NG0 + 1)

            @block.tensor
            def _(pe):
                with pe.Fori(0, B * NG0) as it:
                    for n, src in ((0, kd), (1, qd)):
                        pe.wait_ge(s_dl, 4 * it + 4)
                        for p in range(2):
                            for t in range(2):
                                last = pe.transpose(bank[n][:, p * S + t * P:p * S + (t + 1) * P],
                                                    src[:, t, 2 * p:2 * p + 2, :, :].rearrange("p h a d -> p (h a d)").bitcast(F32),
                                                    env.ident[:])
                        last.then_inc(s_T, 1)
                    pe.wait_ge(s_Ta, 2 * it + 2)
                    pe.wait_ge(s_Tv, it + 1)
                    for u in range(4):
                        p, t = u // 2, u % 2
                        pe.matmul(bank[4 + u][:], qT[:, p, tokens(t)], kT[:, p].rearrange("p j n -> p (j n)"),
                                  start=True, stop=True).then_inc(s_s, 1)
                    for u in range(4):
                        pe.wait_ge(s_exp, 8 * it + 2 * u + 2)
                        if u == 2:
                            pe.wait_ge(s_pTa, 2 * it + 1)
                        if u == 3:
                            pe.wait_ge(s_pTv, 2 * it + 1)
                        for k in range(2):
                            for j in range(2):
                                last = pe.transpose(pT_bank(u)[:, k, j, :], prob[:, u, j, k * P:(k + 1) * P], env.ident[:])
                        last.then_inc(s_pT, 1)
                    pe.wait_ge(s_v, 2 * it + 2)
                    for p in range(2):
                        pe.wait_ge(s_pTa, 2 * it + p + 1)
                        pe.wait_ge(s_pTv, 2 * it + p + 1)
                        for k in range(2):
                            last = pe.matmul(bank[p][:], vp[:, k].rearrange("p h d -> p (h d)"),
                                             pT[:, k, 2 * p:2 * p + 2, :].rearrange("p h n -> p (h n)"),
                                             start=k == 0, stop=k == 1)
                        last.then_inc(s_o, 1)
                    pe.wait_ge(s_oc, 4 * it + 4)
                    for t in range(2):
                        last = pe.transpose(bank[2][:, t * P:(t + 1) * P], oT[:, tokens(t)], env.ident[:])
                    last.then_inc(s_oT, 1)

        with ExitStack() as fin:
            oquant = Quant(env, "qa_oq", fin, NT)
            oqT = env.sb("qa_oqT", [P, KD, TOK], BF16, fin)
            y = env.sb("qa_y", [P, NT, D], F32, fin)
            s_oTp, s_oT2, s_y, s_ys, s_add = (sem(n) for n in (
                "oqT_in_psum", "oqT_ready", "y_in_psum", "y_scaled", "residual_step"))
            block = fin.enter_context(nc.Block())

            @block.scalar
            def _(act):
                for n in range(2):
                    act.wait_ge(s_oTp, n + 1)
                    act.activation(oqT[:, :, n * 512:(n + 1) * 512],
                                   bank[n][:].bitcast(BF16).rearrange("p (k q) -> p k q", k=KD), ACT.Copy).then_inc(s_oT2, 1)

            @block.gpsimd
            def _(pool):
                pool.tensor_tensor(x[:], x[:], bias_rows[:, 3, :].unsqueeze(1).broadcast_to([P, NT, D]),
                                   ALU.add).then_inc(s_add, 1)

            @block.vector
            def _(dve):
                oquant.run(dve, o_tok[:])
                for t in range(NT):
                    dve.wait_ge(s_y, t // 2 * 2 + 2)
                    dve.scalar_tensor_tensor(y[:, t, :], half_banks(t), oquant.scale[:, t:t + 1], w_rows[:, 1, :],
                                             ALU.mult, ALU.mult).then_inc(s_ys, 1)
                dve.wait_ge(s_ys, NT)
                dve.wait_ge(s_add, 1)
                dve.tensor_tensor(x[:], x[:], y[:], ALU.add).then_inc(s_add, 1)
                dve.wait_ge(s_add, 2)

            @block.tensor
            def _(pe):
                pe.wait_ge(oquant.ready, 1)
                turn_rows(pe, oquant, s_oTp)
                for t in range(NT):
                    pe.wait_ge(s_oT2, t // 4 + 1)
                    for k in range(KD):
                        last = pe.matmul(half_banks(t), oqT[:, k, tokens(t)], wT[:, 1, k, :], start=k == 0, stop=k == KD - 1)
                    last.then_inc(s_y, 1)


GOLDEN_CENTER = 1.0 / math.e
GOLDEN_LOWER = 0.5 - math.log(4.0 / 3.0)
GOLDEN_UPPER = 0.5


I = 128
CH = 512
NC = TOK // CH
RW = 33


def experts(env, tag, layer):
    nc, dram, x = env.nc, env.dram, env.x
    E = 8 if layer == 0 else 32
    UNITS = 16 if layer == 0 else 33
    LOOPS = 7 if layer == 0 else 15
    weights = dram[f"{tag}_weights"]
    WCOLS = 2 * KD * I + D

    with ExitStack() as mem:
        sb = lambda n, s, d=F32: env.sb(f"{tag}_{n}", s, d, mem)
        sem = lambda n: env.sem(f"{tag}_{n}")
        rms_w = sb("rms_w", [P, D]) if layer else None
        norm = Norm(env, tag, mem, rms_w)
        h_hi, h_lo = sb("h_hi", [P, KD, TOK], F32R), sb("h_lo", [P, KD, TOK], F32R)
        wr = sb("wr", [P, KD, P])
        wr_hi, wr_lo = sb("wr_hi", [P, KD, P], F32R), sb("wr_lo", [P, KD, P], F32R)
        rt_bias = sb("rt_bias", [P, 32])
        logitT = sb("logitT", [32, TOK])
        sel = sb("sel", [3 * RW, RW * P], BF16)
        score = sb("score", [P, NT, 32])
        wfull = sb("wfull", [P, NT, RW])
        wpart = sb("wpart", [P, NT, 3, RW], BF16)
        wrest = sb("wrest", [P, NT, RW])
        wT = sb("wT", [3 * RW, TOK], BF16)
        stage = [sb(f"stage{j}", [P, WCOLS]) for j in range(2)]
        w_hi = [sb(f"w_hi{j}", [P, WCOLS], F32R) for j in range(2)]
        w_lo = [sb(f"w_lo{j}", [P, WCOLS], F32R) for j in range(2)]
        sg = sb("silu_gate", [P, CH])
        gu = sb("gate_up", [P, CH])
        act_f = sb("act_f", [P, CH])
        act_hi = [sb(f"act_hi{c}", [P, CH], F32R) for c in range(NC)]
        act_lo = [sb(f"act_lo{c}", [P, CH], F32R) for c in range(NC)]
        zero = sb("zero", [P, CH], BF16)
        total, no_expert = sb("total", [P, NT]), sb("no_expert", [P, NT])
        if layer == 0:
            dist, zone, rank = (sb(n, [P, NT, E]) for n in ("dist", "zone", "rank"))
            in_zone_w, fallback = sb("in_zone_w", [P, NT, E]), sb("fallback", [P, NT, E])
            pairs, before = sb("pairs", [P, NT, E, E]), sb("before", [P, E, E])
        else:
            best = sb("best", [P, NT, 8])

        s_const, s_wr, s_stage = sem("const_loaded"), sem("wr_split"), [sem(f"stage_loaded{j}") for j in range(2)]
        s_lg, s_lgc, s_lgt = sem("logitsT_in_psum"), sem("logitsT_copied"), sem("logits_in_psum")
        s_sc, s_step, s_z = sem("scores_ready"), sem("route_step"), sem("logits_scaled")
        s_dist, s_ex = sem("distance_ready"), sem("route_exps_ready")
        s_wpart, s_wTp, s_wT = sem("w_parts_ready"), sem("wT_in_psum"), sem("wT_ready")
        s_hi, s_lo = sem("unit_hi_ready"), sem("unit_lo_ready")
        s_gate, s_up, s_wb = sem("gate_in_psum"), sem("up_in_psum"), sem("w_rows_in_psum")
        s_sg, s_gu, s_act = sem("silu_ready"), sem("gate_up_ready"), sem("act_ready")
        s_ahi, s_alo = sem("act_hi_ready"), sem("act_lo_ready")
        s_down, s_zero, s_zd = sem("down_done"), sem("zero_ready"), sem("y_zeroed")
        s_add, s_twice = sem("residual_added"), sem("input_added_again")

        Y = env.bank[0:4]
        GATE, UP, WB, X7 = env.bank[4:8]
        gate_w = lambda w, k: w[:, k * I:(k + 1) * I]
        up_w = lambda w, k: w[:, (KD + k) * I:(KD + k + 1) * I]
        down_w = lambda w: w[:, 2 * KD * I:]
        block = mem.enter_context(nc.Block())

        @block.sync
        def _(sp):
            sp.dma_start(wr[:], dram[f"{tag}_wr"]).then_inc(s_const, 16)
            sp.dma_start(rt_bias[:], dram[f"{tag}_route"]).then_inc(s_const, 16)
            if layer:
                sp.dma_start(rms_w[:], dram["ln2_rows"]).then_inc(s_const, 16)
            else:
                sp.dma_start(before[:], dram["before"]).then_inc(s_const, 16)
            sp.dma_start(sel[:], dram["sel"]).then_inc(s_const, 16)
            for j in range(2):
                sp.dma_start(stage[j][:], weights[j]).then_inc(s_stage[j], 16)

            def load(u, j, it):
                sp.wait_ge(s_hi, 2 * it + j + 1)
                sp.wait_ge(s_lo, 2 * it + j + 1)
                sp.dma_start(stage[j][:], weights[u]).then_inc(s_stage[j], 16)

            with sp.Fori(0, (UNITS - 2) // 2) as it:
                for j in range(2):
                    load(2 * it + 2 + j, j, it)
            if UNITS % 2:
                load(UNITS - 1, 0, (UNITS - 3) // 2)

        n_const = 64

        @block.gpsimd
        def _(pool):
            if layer:
                pool.wait_ge(s_const, n_const)
            norm.gpsimd_rstd(pool)
            pool.wait_ge(s_wr, 1)
            pool.tensor_tensor(wr_lo[:], wr[:], wr_hi[:].bitcast(F32), ALU.subtract).then_inc(s_wr, 1)

            def lo_half(u, j, it):
                pool.wait_ge(s_hi, u + 1)
                if it is not None:
                    pool.wait_ge(s_down, 4 * it + 2 * j + 2)
                pool.tensor_tensor(w_lo[j][:], stage[j][:], w_hi[j][:].bitcast(F32),
                                   ALU.subtract).then_inc(s_lo, 1)

            for j in range(2):
                lo_half(j, j, None)
            with pool.Fori(0, (UNITS - 2) // 2) as it:
                for j in range(2):
                    lo_half(2 * it + 2 + j, j, it)
            if UNITS % 2:
                lo_half(UNITS - 1, 0, (UNITS - 3) // 2)

        @block.scalar
        def _(act):
            if layer:
                norm.scalar_stats(act)
            act.wait_ge(s_const, n_const)
            act.activation(wr_hi[:], wr[:], ACT.Copy).then_inc(s_wr, 1)

            def hi_half(u, j, it, n):
                act.wait_ge(s_stage[j], 16 * n)
                if it is not None:
                    act.wait_ge(s_down, 4 * it + 2 * j + 2)
                act.activation(w_hi[j][:], stage[j][:], ACT.Copy).then_inc(s_hi, 1)

            for j in range(2):
                hi_half(j, j, None, 1)
            norm.scalar_hi(act, [GATE, UP], h_hi)
            for c in range(NC):
                act.wait_ge(s_lg, c + 1)
                act.activation(logitT[:, c * CH:(c + 1) * CH], [WB, X7][c][0:32, :], ACT.Copy).then_inc(s_lgc, 1)
            if layer == 0:
                act.wait_ge(s_z, 1)
                act.activation(score[:, :, 0:E], score[:, :, 0:E], ACT.Sigmoid).then_inc(s_sc, 1)
                act.wait_ge(s_dist, 1)
                act.activation(in_zone_w[:], dist[:], ACT.Exp, scale=-1.0 / 0.1).then_inc(s_ex, 1)
                act.activation(fallback[:], dist[:], ACT.Exp, scale=-1.0 / 0.3).then_inc(s_ex, 1)
            else:
                act.wait_ge(s_lgt, 1)
                act.activation(score[:], env.bank[4][:, 0:NT * 32].rearrange("p (t e) -> p t e", e=32),
                               ACT.Sigmoid).then_inc(s_sc, 1)

            def unit(n):
                n, c = n
                act.wait_ge(s_gate, n + 1)
                wait_from_one(act, s_gu, n)
                act.activation(sg[:], GATE[:], ACT.Silu).then_inc(s_sg, 1)
                act.wait_ge(s_act, n + 1)
                act.activation(act_hi[c][:], act_f[:], ACT.Copy).then_inc(s_ahi, 1)

            run_units(act, unit, hi_half, LOOPS, UNITS)

        @block.vector
        def _(dve):
            if layer:
                dve.wait_ge(s_const, n_const)
            norm.vector_normalise(dve)
            norm.vector_lo(dve, [GATE, UP], h_hi, h_lo)
            dve.memset(zero[:], 0.0).then_inc(s_zero, 1)
            if layer:
                dve.tensor_tensor(x[:], x[:], env.x_in[:], ALU.add).then_inc(s_twice, 1)
            taken = [0]

            def link(ins):
                taken[0] += 1
                ins.then_inc(s_step, 1)
                dve.wait_ge(s_step, taken[0])

            row = lambda v, n: v.unsqueeze(2).broadcast_to([P, NT, n])
            if layer == 0:
                inh, e8 = score[:, :, 0:E], [P, NT, E, E]
                by_j = lambda v: v.unsqueeze(2).broadcast_to(e8)
                by_e = lambda v: v.unsqueeze(3).broadcast_to(e8)
                dve.wait_ge(s_const, n_const)
                link(dve.reciprocal(total[:, 0:1], rt_bias[:, 0:1]))
                dve.wait_ge(s_lgt, 1)
                dve.tensor_scalar(inh, GATE[:, 0:NT * 32].rearrange("p (t e) -> p t e", e=32)[:, :, 0:E],
                                  total[:, 0:1], None, ALU.mult).then_inc(s_z, 1)
                dve.wait_ge(s_sc, 1)
                link(dve.tensor_scalar(dist[:], inh, GOLDEN_CENTER, None, ALU.subtract))
                link(dve.scalar_tensor_tensor(dist[:], dist[:], -1.0, dist[:], ALU.mult, ALU.max))
                dve.tensor_scalar(zone[:], inh, GOLDEN_LOWER, None, ALU.is_ge).then_inc(s_dist, 1)
                dve.wait_ge(s_dist, 1)
                link(dve.scalar_tensor_tensor(zone[:], inh, GOLDEN_UPPER, zone[:], ALU.is_le, ALU.mult))
                dve.wait_ge(s_ex, 2)
                link(dve.tensor_tensor(in_zone_w[:], in_zone_w[:], zone[:], ALU.mult))
                link(dve.tensor_reduce(total[:], in_zone_w[:], AX_X, ALU.add))
                link(dve.tensor_scalar(no_expert[:], total[:], 1e-8, None, ALU.is_lt))
                link(dve.tensor_tensor(pairs[:], by_j(fallback[:]), by_e(fallback[:]), ALU.is_gt))
                link(dve.tensor_reduce(rank[:], pairs[:], AX_X, ALU.add))
                link(dve.tensor_tensor(pairs[:], by_j(fallback[:]), by_e(fallback[:]), ALU.is_equal))
                link(dve.tensor_tensor(pairs[:], pairs[:], before[:].unsqueeze(1).broadcast_to(e8), ALU.mult))
                link(dve.tensor_reduce(dist[:], pairs[:], AX_X, ALU.add))
                link(dve.tensor_tensor(rank[:], rank[:], dist[:], ALU.add))
                link(dve.scalar_tensor_tensor(fallback[:], rank[:], 1.5, fallback[:], ALU.is_lt, ALU.mult))
                link(dve.tensor_reduce(total[:], fallback[:], AX_X, ALU.add))
                link(dve.tensor_scalar(total[:], total[:], 1e-8, None, ALU.max))
                link(dve.reciprocal(total[:], total[:]))
                link(dve.tensor_tensor(total[:], total[:], no_expert[:], ALU.mult))
                link(dve.tensor_tensor(fallback[:], fallback[:], row(total[:], E), ALU.mult))
                link(dve.tensor_scalar(no_expert[:], no_expert[:], -1.0, 1.0, ALU.mult, ALU.add))
                link(dve.tensor_tensor(in_zone_w[:], in_zone_w[:], row(no_expert[:], E), ALU.mult))
                link(dve.tensor_tensor(in_zone_w[:], in_zone_w[:], fallback[:], ALU.add))
                link(dve.tensor_reduce(total[:], in_zone_w[:], AX_X, ALU.add))
                link(dve.tensor_scalar(total[:], total[:], 1e-8, None, ALU.max))
                link(dve.reciprocal(total[:], total[:]))
                link(dve.memset(wfull[:], 0.0))
                link(dve.tensor_tensor(wfull[:, :, 0:E], in_zone_w[:], row(total[:], E), ALU.mult))
            else:
                dve.wait_ge(s_sc, 1)
                link(dve.tensor_tensor(wrest[:, :, 0:E], score[:], rt_bias[:].unsqueeze(1).broadcast_to([P, NT, E]),
                                       ALU.add))
                for t in range(NT):
                    dve.max(best[:, t, :], wrest[:, t, 0:E]).then_inc(s_z, 1)
                dve.wait_ge(s_z, NT)
                for t in range(NT):
                    last = dve.match_replace(wfull[:, t, 0:E], best[:, t, :], wrest[:, t, 0:E], NEG)
                    last.then_inc(s_dist, 1)
                dve.wait_ge(s_dist, NT)
                link(dve.tensor_tensor(wrest[:, :, 0:E], wrest[:, :, 0:E], wfull[:, :, 0:E], ALU.not_equal))
                link(dve.tensor_tensor(score[:], score[:], wrest[:, :, 0:E], ALU.mult))
                link(dve.tensor_reduce(total[:], score[:], AX_X, ALU.add))
                link(dve.reciprocal(total[:], total[:]))
                link(dve.tensor_tensor(wfull[:, :, 0:E], score[:], row(total[:], E), ALU.mult))
                link(dve.memset(wfull[:, :, E:E + 1], 1.0))
            steps = [0]

            def step(ins):
                steps[0] += 1
                ins.then_inc(s_wpart, 1)
                dve.wait_ge(s_wpart, steps[0])

            step(dve.tensor_copy(wpart[:, :, 0, :], wfull[:]))
            step(dve.tensor_tensor(wrest[:], wfull[:], wpart[:, :, 0, :], ALU.subtract))
            step(dve.tensor_copy(wpart[:, :, 1, :], wrest[:]))
            step(dve.tensor_tensor(wfull[:], wrest[:], wpart[:, :, 1, :], ALU.subtract))
            step(dve.tensor_copy(wpart[:, :, 2, :], wfull[:]))
            for h in range(2):
                dve.wait_ge(s_wTp, h + 1)
                dve.tensor_copy(wT[:, h * CH:(h + 1) * CH],
                                [WB, X7][h][:].bitcast(BF16)[0:3 * RW, 0:CH]).then_inc(s_wT, 1)

            def unit(n):
                n, c = n
                dve.wait_ge(s_up, n + 1)
                dve.wait_ge(s_sg, n + 1)
                dve.tensor_tensor(gu[:], UP[:], sg[:], ALU.mult).then_inc(s_gu, 1)
                dve.wait_ge(s_wb, n + 1)
                dve.wait_ge(s_gu, n + 1)
                dve.tensor_tensor(act_f[:], WB[:], gu[:], ALU.mult).then_inc(s_act, 1)
                dve.wait_ge(s_ahi, n + 1)
                dve.tensor_tensor(act_lo[c][:], act_f[:], act_hi[c][:].bitcast(F32),
                                  ALU.subtract).then_inc(s_alo, 1)

            run_units(dve, unit, None, LOOPS, UNITS)
            if layer:
                dve.wait_ge(s_twice, 1)
            dve.wait_ge(s_down, NC * UNITS)
            for g in range(NT // 2):
                dve.tensor_tensor(x[:, 2 * g:2 * g + 2, :], Y[g][:].rearrange("p (t d) -> p t d", t=2),
                                  x[:, 2 * g:2 * g + 2, :], ALU.add).then_inc(s_add, 1)
            dve.wait_ge(s_add, NT // 2)

        @block.tensor
        def _(pe):
            norm.tensor_transpose(pe, [GATE, UP])
            pe.wait_ge(s_wr, 2)
            for c in range(NC):
                pe.wait_ge(norm.s_lo, 2 * c + 2)
                cols = slice(c * CH, (c + 1) * CH)
                for k in range(KD):
                    last = split3(pe, [WB, X7][c][:], (wr_hi[:, k, :], wr_lo[:, k, :]),
                                  (h_hi[:, k, cols], h_lo[:, k, cols]), k == 0, k == KD - 1)
                last.then_inc(s_lg, 1)
            pe.wait_ge(s_lgc, 2)
            pe.wait_ge(norm.s_lo, B)
            for t in range(NT):
                last = pe.transpose(GATE[:, t * 32:(t + 1) * 32], logitT[:, tokens(t)], env.ident[0:32, 0:32])
            last.then_inc(s_lgt, 1)
            pe.wait_ge(s_zero, 1)
            for g in range(NT // 2):
                last = pe.matmul(Y[g][:], zero[:, 0:P], zero[:], start=True, stop=True)
            last.then_inc(s_zd, 1)
            pe.wait_ge(s_wpart, 5)
            pe.wait_ge(s_lgc, 2)
            for h in range(2):
                for q in range(4):
                    t = 4 * h + q
                    last = pe.transpose([WB, X7][h][:].bitcast(BF16)[0:3 * RW, q * P:(q + 1) * P],
                                        wpart[:, t, :, :].rearrange("p a e -> p (a e)"), env.ident_bf[:])
                last.then_inc(s_wTp, 1)
            pe.wait_ge(s_wT, 2)
            pe.wait_ge(s_sc, 1)

            def up_part(u, c, j, n, e):
                cols = slice(c * CH, (c + 1) * CH)
                h = [(h_hi[:, k, cols], h_lo[:, k, cols]) for k in range(KD)]
                if c == 0:
                    pe.wait_ge(s_lo, u + 1)
                wait_from_one(pe, s_sg, n)
                for k in range(KD):
                    last = split3(pe, GATE[:], (gate_w(w_hi[j], k), gate_w(w_lo[j], k)), h[k], k == 0, k == KD - 1)
                last.then_inc(s_gate, 1)
                wait_from_one(pe, s_gu, n)
                for k in range(KD):
                    last = split3(pe, UP[:], (up_w(w_hi[j], k), up_w(w_lo[j], k)), h[k], k == 0, k == KD - 1)
                last.then_inc(s_up, 1)
                wait_from_one(pe, s_act, n)
                pe.matmul(WB[:], sel[:, bass.ds(e * P, P)], wT[:, cols], start=True, stop=True).then_inc(s_wb, 1)

            def down_part(c, j, n):
                pe.wait_ge(s_alo, n + 1)
                for q in range(CH // P):
                    t = c * (CH // P) + q
                    last = split3(pe, Y[t // 2][:, (t % 2) * D:(t % 2 + 1) * D],
                                  (act_hi[c][:, tokens(q)], act_lo[c][:, tokens(q)]),
                                  (down_w(w_hi[j]), down_w(w_lo[j])), False, False)
                last.then_inc(s_down, 1)

            of = (lambda it, j: it) if layer == 0 else (lambda it, j: 2 * it + j)
            up_part(0, 0, 0, 0, 0)
            with pe.Fori(0, LOOPS) as it:
                for j in range(2):
                    u = 2 * it + j
                    up_part(u, 1, j, 2 * u + 1, of(it, j))
                    down_part(0, j, 2 * u)
                    nxt = (of(it, 1) if j == 0 else of(it + 1, 0))
                    up_part(u + 1, 0, 1 - j, 2 * u + 2, nxt)
                    down_part(1, j, 2 * u + 1)
            for u in range(2 * LOOPS, UNITS):
                j = u % 2
                e = u // 2 if layer == 0 else u
                up_part(u, 1, j, 2 * u + 1, e)
                down_part(0, j, 2 * u)
                if u + 1 < UNITS:
                    up_part(u + 1, 0, 1 - j, 2 * u + 2, (u + 1) // 2 if layer == 0 else u + 1)
                down_part(1, j, 2 * u + 1)


def run_units(eng, unit, refill, loops, units):
    unit((0, 0))
    with eng.Fori(0, loops) as it:
        for j in range(2):
            n = 2 * (2 * it + j)
            unit((n + 1, 1))
            unit((n + 2, 0))
            if refill is not None:
                refill(2 * it + 2 + j, j, it, it + 2)
    for u in range(2 * loops, units):
        unit((2 * u + 1, 1))
        if u + 1 < units:
            unit((2 * u + 2, 0))
        if refill is not None and u + 2 < units:
            refill(u + 2, u % 2, u // 2, u // 2 + 2)
H1, HD1, RD = 16, 128, 64
QC, KVC = 96, 64
LOOKBACK = 8
HG = 4
NG = H1 // HG
FW = KVC + RD


def latent_attention(env):
    nc, dram, x = env.nc, env.dram, env.x
    with ExitStack() as mem:
        sb = lambda n, s, d=F32: env.sb(f"la_{n}", s, d, mem)
        sem = lambda n: env.sem(f"la_{n}")
        bank = env.bank
        keys = sb("keys", [P, NT, FW])
        kT_hi, kT_lo = sb("kT_hi", [P, TOK], F32R), sb("kT_lo", [P, TOK], F32R)
        vals = sb("vals", [P, NT, 2, KVC], F32R)
        qcT_hi, qcT_lo = sb("qcT_hi", [QC, TOK], F32R), sb("qcT_lo", [QC, TOK], F32R)
        wa_hi, wa_lo = sb("wa_hi", [QC, H1, FW], F32R), sb("wa_lo", [QC, H1, FW], F32R)
        c_hi, c_lo = sb("c_hi", [P, H1, D], F32R), sb("c_lo", [P, H1, D], F32R)
        bias = sb("bias", [P, NT, S], BF16)
        key_cos, key_sin = sb("key_cos", [P, 2, RD]), sb("key_sin", [P, 2, RD])
        s_in = sem("inputs_loaded")
        s_wdq, s_kvT, s_kvTc, s_key, s_keyc = (sem(n) for n in (
            "w_dq_split", "kv_cT_in_psum", "kv_cT_copied", "keys_in_psum", "keys_copied"))
        s_turn, s_kTp, s_kTh, s_kTl = (sem(n) for n in ("keys_turned", "kT_in_psum", "kT_hi_ready", "kT_lo_ready"))
        s_val, s_qcp, s_qch, s_qcl = (sem(n) for n in ("vals_ready", "q_cT_in_psum", "q_cT_hi_ready", "q_cT_lo_ready"))
        s_wap, s_wah, s_wal, s_qrh, s_qrl = (sem(n) for n in (
            "a_in_psum", "a_hi_ready", "a_lo_ready", "qr_hi_ready", "qr_lo_ready"))
        s_cp, s_ch, s_cl = sem("c_in_psum"), sem("c_hi_ready"), sem("c_lo_ready")
        s_bias = sem("bias_step")
        s_slot = sem("batch_slots_ready")
        s_q, s_qc, s_rot, s_roped = sem("q_in_psum"), sem("q_copied"), sem("q_rotated"), sem("q_roped")
        s_qT, s_qTh, s_qTl = sem("qT_in_psum"), sem("qT_hi_ready"), sem("qT_lo_ready")
        s_s, s_max, s_exp, s_inv, s_prob = (sem(n) for n in (
            "scores_in_psum", "max_ready", "exp_ready", "row_inverse_ready", "prob_ready"))
        s_pT, s_pTh, s_pTl = sem("pT_in_psum"), sem("pT_hi_ready"), sem("pT_lo_ready")
        s_o, s_oh, s_ol = sem("oT_in_psum"), sem("oT_hi_ready"), sem("oT_lo_ready")
        s_y, s_add = sem("y_in_psum"), sem("residual_added")
        half = RD // 2
        SCALE = 1.0 / math.sqrt(HD1 + RD)
        with ExitStack() as prep:
            sb = lambda n, s, d=F32: env.sb(f"la_{n}", s, d, prep)
            norm = Norm(env, "la", prep)
            ctxT = sb("ctxT", [P, KD, TOK])
            w_kvc, w_dq = sb("w_kvc", [P, KD, KVC]), sb("w_dq", [P, KD, P])
            w_dq_hi, w_dq_lo = sb("w_dq_hi", [P, KD, P], F32R), sb("w_dq_lo", [P, KD, P], F32R)
            uqT, ukT = sb("uqT", [P, H1, QC]), sb("ukT", [P, H1, KVC])
            uvT2, wo = sb("uvT2", [P, H1, 2 * KVC]), sb("wo", [P, H1, D])
            qr = sb("qr", [QC, H1, RD])
            key_w = sb("key_w", [KVC, FW])
            kvcT = sb("kvcT", [KVC, TOK])
            turn_a, turn_b = sb("turn_a", [P, NT, RD]), sb("turn_b", [P, NT, RD])
            h_hi, h_lo = sb("h_hi", [P, KD, TOK], F32R), sb("h_lo", [P, KD, TOK], F32R)
            seg_i, seg, seg_low = sb("seg_i", [P, NT], I32), sb("seg", [P, NT]), sb("seg_low", [P, NT])
            key_id = sb("key_id", [P, S])
            not_after, good = sb("not_after", [P, NT, S], BF16), sb("good", [P, NT, S], BF16)
            credit = sb("credit", [P, 2])
            loads = [(ctxT, "ctxT"), (w_kvc, "w_kvc"), (w_dq, "w_dq"), (uqT, "uqT"), (ukT, "ukT"), (uvT2, "uvT2"),
                     (wo, "la_wo"), (qr, "qr"), (key_w, "key_w"), (key_cos, "la_cos"), (key_sin, "la_sin"),
                     (seg_i, "seg"), (key_id, "key_id")]
            n_in = 16 * len(loads)
            kvT_bank = [bank[2], bank[3]]
            block = prep.enter_context(nc.Block())

            @block.sync
            def _(sp):
                for dst, name in loads:
                    sp.dma_start(dst[:], dram[name]).then_inc(s_in, 16)

            @block.gpsimd
            def _(pool):
                norm.gpsimd_rstd(pool)
                pool.wait_ge(s_wdq, 1)
                pool.tensor_tensor(w_dq_lo[:], w_dq[:], w_dq_hi[:].bitcast(F32), ALU.subtract).then_inc(s_wdq, 1)
                pool.wait_ge(s_turn, 2)
                pool.tensor_tensor(keys[:, :, KVC:], turn_a[:], turn_b[:], ALU.add).then_inc(s_turn, 1)

                pool.wait_ge(s_qcl, 2)
                pool.wait_ge(s_val, 2)

            @block.scalar
            def _(act):
                act.wait_ge(s_in, n_in)
                act.activation(w_dq_hi[:], w_dq[:], ACT.Copy).then_inc(s_wdq, 1)
                act.activation(wa_hi[:, :, KVC:], qr[:], ACT.Copy, scale=SCALE).then_inc(s_qrh, 1)
                for c in range(2):
                    act.wait_ge(s_kvT, c + 1)
                    act.activation(kvcT[:, c * 512:(c + 1) * 512], kvT_bank[c][0:KVC, :], ACT.Copy).then_inc(s_kvTc, 1)
                for n in range(2):
                    act.wait_ge(s_key, n + 1)
                    act.activation(keys[:, 4 * n:4 * n + 4, :], bank[4 + n][:].rearrange("p (t f) -> p t f", t=4),
                                   ACT.Copy).then_inc(s_keyc, 1)
                act.wait_ge(s_keyc, 2)
                act.activation(vals[:, :, 0, :], keys[:, :, 0:KVC], ACT.Copy).then_inc(s_val, 1)
                for n in range(4):
                    act.wait_ge(s_wap, n + 1)
                    act.activation(wa_hi[:, 4 * n:4 * n + 4, 0:KVC],
                                   bank[6 + n % 2][0:QC, 0:4 * KVC].rearrange("p (h c) -> p h c", h=4),
                                   ACT.Copy, scale=SCALE).then_inc(s_wah, 1)
                for n in range(8):
                    act.wait_ge(s_cp, n + 1)
                    act.activation(c_hi[:, 2 * n:2 * n + 2, :], bank[6 + n % 2][:].rearrange("p (h d) -> p h d", h=2),
                                   ACT.Copy).then_inc(s_ch, 1)
                norm.scalar_hi(act, bank[0:2], h_hi)
                for n in range(2):
                    act.wait_ge(s_kTp, n + 1)
                    act.activation(kT_hi[:, n * 512:(n + 1) * 512], bank[4 + n][:], ACT.Copy).then_inc(s_kTh, 1)
                for c in range(2):
                    act.wait_ge(s_qcp, c + 1)
                    act.activation(qcT_hi[:, c * 512:(c + 1) * 512], bank[2 + c][0:QC, :], ACT.Copy).then_inc(s_qch, 1)

            @block.vector
            def _(dve):
                norm.vector_normalise(dve)
                dve.wait_ge(s_in, n_in)
                steps = [0]

                def link(ins):
                    steps[0] += 1
                    ins.then_inc(s_bias, 1)
                    dve.wait_ge(s_bias, steps[0])

                link(dve.tensor_copy(seg[:], seg_i[:]))
                link(dve.tensor_scalar(seg_low[:], seg[:], float(-LOOKBACK), None, ALU.add))
                for t in range(NT):
                    last = dve.tensor_scalar(not_after[:, t, :], key_id[:], seg[:, t:t + 1], None, ALU.is_le)
                    last.then_inc(s_bias, 1)
                dve.wait_ge(s_bias, 2 + NT)
                for t in range(NT):
                    dve.scalar_tensor_tensor(good[:, t, :], key_id[:], seg_low[:, t:t + 1], not_after[:, t, :],
                                             ALU.is_ge, ALU.mult).then_inc(s_bias, 1)
                dve.wait_ge(s_bias, 2 + 2 * NT)
                dve.tensor_scalar(bias[:], good[:], -1.0, -NEG, ALU.add, ALU.mult).then_inc(s_bias, 1)
                dve.wait_ge(s_keyc, 2)
                k4 = keys[:].rearrange("p (b t) f -> p b t f", t=2)
                a4, b4 = turn_a[:].rearrange("p (b t) f -> p b t f", t=2), turn_b[:].rearrange("p (b t) f -> p b t f", t=2)
                for t in range(2):
                    cs = lambda v, lo, n: v[:, t, lo:lo + n].unsqueeze(1).broadcast_to([P, B, n])
                    last = dve.tensor_tensor(a4[:, :, t, :], k4[:, :, t, KVC:], cs(key_cos, 0, RD), ALU.mult)
                    dve.tensor_tensor(b4[:, :, t, 0:half], k4[:, :, t, KVC + half:], cs(key_sin, 0, half), ALU.mult)
                    last = dve.tensor_tensor(b4[:, :, t, half:], k4[:, :, t, KVC:KVC + half], cs(key_sin, half, half), ALU.mult)
                    last.then_inc(s_turn, 1)
                dve.wait_ge(s_val, 1)
                dve.tensor_tensor(vals[:, :, 1, :], keys[:, :, 0:KVC], vals[:, :, 0, :].bitcast(F32),
                                  ALU.subtract).then_inc(s_val, 1)
                dve.wait_ge(s_qrh, 1)
                dve.scalar_tensor_tensor(wa_lo[:, :, KVC:], qr[:], SCALE, wa_hi[:, :, KVC:].bitcast(F32),
                                         ALU.mult, ALU.subtract).then_inc(s_qrl, 1)
                for n in range(4):
                    dve.wait_ge(s_wah, n + 1)
                    dve.scalar_tensor_tensor(wa_lo[:, 4 * n:4 * n + 4, 0:KVC],
                                             bank[6 + n % 2][0:QC, 0:4 * KVC].rearrange("p (h c) -> p h c", h=4), SCALE,
                                             wa_hi[:, 4 * n:4 * n + 4, 0:KVC].bitcast(F32),
                                             ALU.mult, ALU.subtract).then_inc(s_wal, 1)
                for n in range(8):
                    dve.wait_ge(s_ch, n + 1)
                    dve.tensor_tensor(c_lo[:, 2 * n:2 * n + 2, :], bank[6 + n % 2][:].rearrange("p (h d) -> p h d", h=2),
                                      c_hi[:, 2 * n:2 * n + 2, :].bitcast(F32), ALU.subtract).then_inc(s_cl, 1)
                norm.vector_lo(dve, bank[0:2], h_hi, h_lo)
                for n in range(2):
                    dve.wait_ge(s_kTh, n + 1)
                    cols = slice(n * 512, (n + 1) * 512)
                    dve.tensor_tensor(kT_lo[:, cols], bank[4 + n][:], kT_hi[:, cols].bitcast(F32),
                                      ALU.subtract).then_inc(s_kTl, 1)
                for c in range(2):
                    dve.wait_ge(s_qch, c + 1)
                    cols = slice(c * 512, (c + 1) * 512)
                    dve.tensor_tensor(qcT_lo[:, cols], bank[2 + c][0:QC, :], qcT_hi[:, cols].bitcast(F32),
                                      ALU.subtract).then_inc(s_qcl, 1)

                dve.memset(credit[:, 0:1], 0.0).then_inc(s_ol, 1)
                dve.memset(credit[:, 1:2], 0.0).then_inc(s_add, 1)

            @block.tensor
            def _(pe):
                pe.wait_ge(s_in, n_in)
                for c in range(2):
                    for k in range(KD):
                        last = pe.matmul(kvT_bank[c][0:KVC, :], w_kvc[:, k, :], ctxT[:, k, c * 512:(c + 1) * 512],
                                         start=k == 0, stop=k == KD - 1)
                    last.then_inc(s_kvT, 1)
                pe.wait_ge(s_kvTc, 2)
                for t in range(NT):
                    last = pe.matmul(bank[4 + t // 4][:, (t % 4) * FW:(t % 4 + 1) * FW], kvcT[:, tokens(t)], key_w[:],
                                     start=True, stop=True)
                    if t % 4 == 3:
                        last.then_inc(s_key, 1)
                for n in range(4):
                    if n >= 2:
                        pe.wait_ge(s_wal, n - 1)
                    for j in range(4):
                        h = 4 * n + j
                        last = pe.matmul(bank[6 + n % 2][0:QC, j * KVC:(j + 1) * KVC], uqT[:, h, :], ukT[:, h, :],
                                         start=True, stop=True)
                    last.then_inc(s_wap, 1)
                for n in range(8):
                    pe.wait_ge(s_wal, min(4, 3 + n))
                    if n >= 2:
                        pe.wait_ge(s_cl, n - 1)
                    for j in range(2):
                        h = 2 * n + j
                        last = pe.matmul(bank[6 + n % 2][:, j * D:(j + 1) * D], uvT2[:, h, :], wo[:, h, :],
                                         start=True, stop=True)
                    last.then_inc(s_cp, 1)
                norm.tensor_transpose(pe, bank[0:2])
                pe.wait_ge(s_turn, 3)
                for n in range(2):
                    for j in range(4):
                        last = pe.transpose(bank[4 + n][:, j * P:(j + 1) * P], keys[:, 4 * n + j, :], env.ident[:])
                    last.then_inc(s_kTp, 1)
                pe.wait_ge(s_wdq, 2)
                for c in range(2):
                    pe.wait_ge(norm.s_lo, 2 * c + 2)
                    cols = slice(c * 512, (c + 1) * 512)
                    for k in range(KD):
                        last = split3(pe, bank[2 + c][:], (w_dq_hi[:, k, :], w_dq_lo[:, k, :]),
                                      (h_hi[:, k, cols], h_lo[:, k, cols]), k == 0, k == KD - 1)
                    last.then_inc(s_qcp, 1)
                pe.wait_ge(s_cl, 8)
                pe.wait_ge(s_qrl, 1)
                pe.wait_ge(s_kTl, 2)
                pe.wait_ge(s_qcl, 2)
                pe.wait_ge(s_bias, 3 + 2 * NT)

        sb = lambda n, s, d=F32: env.sb(f"la_{n}", s, d, mem)
        qs_hi, qs_lo = sb("qs_hi", [QC, S], F32R), sb("qs_lo", [QC, S], F32R)
        vs = sb("vs", [P, 2, 2 * KVC], F32R)
        q = sb("q", [P, 2, HG, FW])
        rot_a, rot_b = sb("rot_a", [P, 2, HG, RD]), sb("rot_b", [P, 2, HG, RD])
        qT_hi, qT_lo = sb("qT_hi", [P, 2, HG, P], F32R), sb("qT_lo", [P, 2, HG, P], F32R)
        prob = sb("prob", [P, 4, 2, S])
        nmax, rsum, rinv = sb("nmax", [P, 4, 2]), sb("rsum", [P, 4, 2]), sb("rinv", [P, 4, 2])
        pT_hi, pT_lo = sb("pT_hi", [P, 2, HG, S], F32R), sb("pT_lo", [P, 2, HG, S], F32R)
        oT_hi, oT_lo = sb("oT_hi", [P, HG, S], F32R), sb("oT_lo", [P, HG, S], F32R)

        block = mem.enter_context(nc.Block())

        def pT_view(t, u):
            h, p = u // 2, u % 2
            return t[:, :, 2 * p:2 * p + 2, h * P:(h + 1) * P]

        def pT_part(act, it, u):
            act.wait_ge(s_pT, 4 * it + u + 1)
            act.activation(pT_view(pT_hi, u), bank[2 + u % 2][:].rearrange("p (k j n) -> p k j n", k=2, j=2),
                           ACT.Copy).then_inc(s_pTh, 1)

        @block.gpsimd
        def _(pool):
            with pool.Fori(0, B) as b:
                pool.wait_ge(s_add, NG * b + 1)
                pool.tensor_copy(qs_hi[:], qcT_hi[:, bass.ts(b, S)]).then_inc(s_slot, 1)
                pool.tensor_copy(qs_lo[:], qcT_lo[:, bass.ts(b, S)]).then_inc(s_slot, 1)
                pool.tensor_copy(vs[:], vals[:, bass.ds(2 * b, 2), :, :].rearrange("p t a c -> p t (a c)")).then_inc(s_slot, 1)
                with pool.Fori(0, NG) as g:
                    it = b * NG + g
                    for t in range(2):
                        pool.wait_ge(s_rot, 6 * it + 3 * t + 3)
                        pool.tensor_tensor(q[:, t, :, KVC:], rot_a[:, t], rot_b[:, t], ALU.add).then_inc(s_roped, 1)
                    for u in range(4):
                        pool.wait_ge(s_inv, 4 * it + u + 1)
                        pool.tensor_tensor(prob[:, u], prob[:, u], rinv[:, u, :].unsqueeze(2).broadcast_to([P, 2, S]),
                                           ALU.mult).then_inc(s_prob, 1)

        @block.scalar
        def _(act):
            with act.Fori(0, B * NG) as it:
                for t in range(2):
                    act.wait_ge(s_q, 2 * it + t + 1)
                    act.activation(q[:, t], bank[t][:].rearrange("p (h f) -> p h f", h=HG), ACT.Copy).then_inc(s_qc, 1)
                for t in range(2):
                    act.wait_ge(s_qT, 2 * it + t + 1)
                    act.activation(qT_hi[:, t], bank[2 + t][:].rearrange("p (h n) -> p h n", h=HG),
                                   ACT.Copy).then_inc(s_qTh, 1)
                for u in range(4):
                    act.wait_ge(s_max, 4 * it + u + 1)
                    for j in range(2):
                        act.activation(prob[:, u, j, :], bank[4 + u][:, j * S:(j + 1) * S], ACT.Exp,
                                       bias=nmax[:, u, j:j + 1], accum_out=rsum[:, u, j:j + 1]).then_inc(s_exp, 1)
                    if u >= 2:
                        pT_part(act, it, u - 2)
                pT_part(act, it, 2)
                pT_part(act, it, 3)
                for j in range(2):
                    act.wait_ge(s_o, 2 * it + j + 1)
                    act.activation(oT_hi[:, 2 * j:2 * j + 2, :], bank[j][:].rearrange("p (h n) -> p h n", h=2),
                                   ACT.Copy).then_inc(s_oh, 1)

        @block.vector
        def _(dve):
            with dve.Fori(0, B) as b:
                with dve.Fori(0, NG) as g:
                    it = b * NG + g
                    for t in range(2):
                        dve.wait_ge(s_qc, 2 * it + t + 1)
                        cs = lambda v, lo, n: v[:, t, lo:lo + n].unsqueeze(1).broadcast_to([P, HG, n])
                        dve.tensor_tensor(rot_a[:, t], q[:, t, :, KVC:], cs(key_cos, 0, RD), ALU.mult).then_inc(s_rot, 1)
                        dve.tensor_tensor(rot_b[:, t, :, 0:half], q[:, t, :, KVC + half:], cs(key_sin, 0, half),
                                          ALU.mult).then_inc(s_rot, 1)
                        dve.tensor_tensor(rot_b[:, t, :, half:], q[:, t, :, KVC:KVC + half], cs(key_sin, half, half),
                                          ALU.mult).then_inc(s_rot, 1)
                    for t in range(2):
                        dve.wait_ge(s_qTh, 2 * it + t + 1)
                        dve.tensor_tensor(qT_lo[:, t], bank[2 + t][:].rearrange("p (h n) -> p h n", h=HG),
                                          qT_hi[:, t].bitcast(F32), ALU.subtract).then_inc(s_qTl, 1)
                    def inverse(u):
                        dve.wait_ge(s_exp, 8 * it + 2 * u + 2)
                        dve.reciprocal(rinv[:, u, :], rsum[:, u, :]).then_inc(s_inv, 1)

                    def pT_low(u):
                        dve.wait_ge(s_pTh, 4 * it + u + 1)
                        dve.tensor_tensor(pT_view(pT_lo, u), bank[2 + u % 2][:].rearrange("p (k j n) -> p k j n", k=2, j=2),
                                          pT_view(pT_hi, u).bitcast(F32), ALU.subtract).then_inc(s_pTl, 1)

                    for u in range(4):
                        dve.wait_ge(s_s, 4 * it + u + 1)
                        dve.tensor_reduce(nmax[:, u, :], bank[4 + u][:].rearrange("p (j n) -> p j n", j=2), AX_X,
                                          ALU.max, negate=True).then_inc(s_max, 1)
                        if u >= 1:
                            inverse(u - 1)
                    inverse(3)
                    for u in range(4):
                        pT_low(u)
                    for j in range(2):
                        dve.wait_ge(s_oh, 2 * it + j + 1)
                        dve.tensor_tensor(oT_lo[:, 2 * j:2 * j + 2, :], bank[j][:].rearrange("p (h n) -> p h n", h=2),
                                          oT_hi[:, 2 * j:2 * j + 2, :].bitcast(F32), ALU.subtract).then_inc(s_ol, 1)
                    dve.wait_ge(s_y, it + 1)
                    rows2 = x[:, bass.ds(2 * b, 2), :]
                    dve.tensor_tensor(rows2, bank[4][:].rearrange("p (t d) -> p t d", t=2), rows2,
                                      ALU.add).then_inc(s_add, 1)
            dve.wait_ge(s_add, B * NG + 1)

        @block.tensor
        def _(pe):
            with pe.Fori(0, B) as b:
                with pe.Fori(0, NG) as g:
                    it = b * NG + g
                    pe.wait_ge(s_slot, 3 * b + 3)
                    cols = bass.ts(b, S)
                    pe.wait_ge(s_ol, 2 * it + 1)
                    for t in range(2):
                        last = split3(pe, bank[t][:], (qs_hi[:, tokens(t)], qs_lo[:, tokens(t)]),
                                      (wa_hi[:].rearrange("p h f -> p (h f)")[:, bass.ts(g, 512)],
                                       wa_lo[:].rearrange("p h f -> p (h f)")[:, bass.ts(g, 512)]), True, True)
                        last.then_inc(s_q, 1)
                    for t in range(2):
                        pe.wait_ge(s_roped, 2 * it + t + 1)
                        for h in range(HG):
                            last = pe.transpose(bank[2 + t][:, h * P:(h + 1) * P], q[:, t, h, :], env.ident[:])
                        last.then_inc(s_qT, 1)
                    pe.wait_ge(s_add, it + 1)
                    for u in range(4):
                        t, p = u // 2, u % 2
                        pe.wait_ge(s_qTl, 2 * it + t + 1)
                        for j in range(2):
                            h = 2 * p + j
                            out = bank[4 + u][:, j * S:(j + 1) * S]
                            split3(pe, out, (qT_hi[:, t, h, :], qT_lo[:, t, h, :]), (kT_hi[:, cols], kT_lo[:, cols]),
                                   True, False)
                            last = pe.matmul(out, env.ident_bf[:], bias[:].rearrange("p t n -> p (t n)")[:, bass.ds(b * 2 * S + t * S, S)],
                                             start=False, stop=True, skip_group_check=True)
                        last.then_inc(s_s, 1)
                    for u in range(4):
                        pe.wait_ge(s_prob, 4 * it + u + 1)
                        if u >= 2:
                            pe.wait_ge(s_pTl, 4 * it + u - 1)
                        view = bank[2 + u % 2][:].rearrange("p (k j n) -> p k j n", k=2, j=2)
                        for k in range(2):
                            for j in range(2):
                                last = pe.transpose(view[:, k, j, :], prob[:, u, j, k * P:(k + 1) * P], env.ident[:])
                        last.then_inc(s_pT, 1)
                    for p in range(2):
                        pe.wait_ge(s_pTl, 4 * it + 3 + p)
                        for k in range(2):
                            for part in (pT_hi, pT_lo):
                                last = pe.matmul(bank[p][:], vs[:, k, :],
                                                 part[:, k, 2 * p:2 * p + 2, :].rearrange("p h n -> p (h n)"),
                                                 start=k == 0 and part is pT_hi, stop=k == 1 and part is pT_lo)
                        last.then_inc(s_o, 1)
                    for t in range(2):
                        for h in range(HG):
                            if t == 0 and h % 2 == 0:
                                pe.wait_ge(s_ol, 2 * it + h // 2 + 2)
                            head = bass.ds(g * HG * D + h * D, D)
                            last = split3(pe, bank[4][:, t * D:(t + 1) * D], (oT_hi[:, h, tokens(t)], oT_lo[:, h, tokens(t)]),
                                          (c_hi[:].rearrange("p h d -> p (h d)")[:, head],
                                           c_lo[:].rearrange("p h d -> p (h d)")[:, head]), h == 0, h == HG - 1)
                    last.then_inc(s_y, 1)


NKV, REP, HD = 4, 8, 128
QKV = (REP + 2) * HD
NR = REP + 1


def grouped_attention(env):
    nc, dram, x = env.nc, env.dram, env.x
    SCALE = 1.0 / math.sqrt(HD)
    half = HD // 2
    bank = env.bank
    with ExitStack() as mem:
        sb = lambda n, s, d=F32: env.sb(f"ga_{n}", s, d, mem)
        sem = lambda n: env.sem(f"ga_{n}")
        h_hi, h_lo = sb("h_hi", [P, KD, TOK], F32R), sb("h_lo", [P, KD, TOK], F32R)
        with ExitStack() as prep:
            rms_w = env.sb("ga_rms_w", [P, D], F32, prep)
            layer_norm = Norm(env, "ga_ln", prep, dst=x)
            norm = Norm(env, "ga", prep, rms_w)
            s_w, s_keep = sem("norm_weight_loaded"), sem("input_kept")
            block = prep.enter_context(nc.Block())

            @block.sync
            def _(sp):
                sp.dma_start(rms_w[:], dram["ln1_rows"]).then_inc(s_w, 16)

            @block.gpsimd
            def _(pool):
                pool.tensor_copy(env.x_in[:], x[:]).then_inc(s_keep, 1)
                layer_norm.gpsimd_rstd(pool)
                norm.gpsimd_rstd(pool)

            @block.scalar
            def _(act):
                act.wait_ge(layer_norm.s_xn, NT)
                norm.scalar_stats(act)
                norm.scalar_hi(act, bank[0:2], h_hi)

            @block.vector
            def _(dve):
                layer_norm.vector_normalise(dve, s_keep)
                dve.wait_ge(s_w, 16)
                norm.vector_normalise(dve)
                norm.vector_lo(dve, bank[0:2], h_hi, h_lo)
                dve.wait_ge(norm.s_lo, B)

            @block.tensor
            def _(pe):
                norm.tensor_transpose(pe, bank[0:2])

        cos, sin = sb("cos", [P, 2, HD]), sb("sin", [P, 2, HD])
        causal = sb("causal", [P, P], BF16)
        stage_w, stage_wo = sb("stage_w", [P, KD, QKV]), sb("stage_wo", [P, REP, D])
        w_hi, w_lo = sb("w_hi", [P, KD, QKV], F32R), sb("w_lo", [P, KD, QKV], F32R)
        wo_hi, wo_lo = sb("wo_hi", [P, REP, D], F32R), sb("wo_lo", [P, REP, D], F32R)
        hs_hi, hs_lo = sb("hs_hi", [P, KD, S], F32R), sb("hs_lo", [P, KD, S], F32R)
        qkv = sb("qkv", [P, 2, QKV])
        rot_a, rot_b = sb("rot_a", [P, NR, HD]), sb("rot_b", [P, NR, HD])
        roped = sb("roped", [P, 2, NR, HD])
        T_hi, T_lo = sb("T_hi", [P, NR, S], F32R), sb("T_lo", [P, NR, S], F32R)
        prob = sb("prob", [P, REP, P + S])
        nmax, rsum, rinv = sb("nmax", [P, REP, 2]), sb("rsum", [P, REP, 2]), sb("rinv", [P, REP, 2])
        pT = sb("pT", [P, REP, S + P])
        oT_hi, oT_lo = sb("oT_hi", [P, REP, S], F32R), sb("oT_lo", [P, REP, S], F32R)

        s_const, s_stage, s_stwo = sem("constants_loaded"), sem("w_loaded"), sem("wo_loaded")
        s_whi, s_wlo = sem("w_hi_ready"), sem("w_lo_ready")
        s_hs = sem("batch_slot_ready")
        s_q, s_qc, s_rot, s_rope = sem("qkv_in_psum"), sem("qkv_copied"), sem("qkv_rotated"), sem("qkv_roped")
        s_T, s_Th, s_Tl = sem("T_in_psum"), sem("T_hi_ready"), sem("T_lo_ready")
        s_s, s_max, s_exp, s_inv, s_prob = (sem(n) for n in (
            "scores_in_psum", "max_ready", "exp_ready", "row_inverse_ready", "prob_ready"))
        s_pT, s_pTc = sem("pT_in_psum"), sem("pT_copied")
        s_o, s_oh, s_ol = sem("oT_in_psum"), sem("oT_hi_ready"), sem("oT_lo_ready")
        s_y, s_add = sem("y_in_psum"), sem("residual_added")
        CHUNKS = [(0, 512), (512, 512), (1024, 256)]
        NCH = len(CHUNKS)
        block = mem.enter_context(nc.Block())

        def pT_copy(act, it, h):
            act.wait_ge(s_pT, REP * it + h + 1)
            act.activation(pT[:, h, :], bank[2 + h % 2][:, 0:S + P], ACT.Copy).then_inc(s_pTc, 1)

        def turn(pe, it, h):
            pe.wait_ge(s_prob, 2 * (REP * it + h) + 2)
            if h == 0:
                pe.wait_ge(s_Tl, 5 * it + 5)
            if h >= 2:
                pe.wait_ge(s_pTc, REP * it + h - 1)
            for block_at, src in ((0, 0), (P, P), (S, S)):
                last = pe.transpose(bank[2 + h % 2][:, block_at:block_at + P], prob[:, h, src:src + P], env.ident[:])
            last.then_inc(s_pT, 1)

        @block.sync
        def _(sp):
            for dst, name in ((cos, "ga_cos"), (sin, "ga_sin"), (causal, "causal")):
                sp.dma_start(dst[:], dram[name]).then_inc(s_const, 16)
            sp.dma_start(stage_w[:], dram["ga_w"][0]).then_inc(s_stage, 16)
            sp.dma_start(stage_wo[:], dram["ga_wo"][0]).then_inc(s_stwo, 16)
            with sp.Fori(0, NKV - 1) as g:
                sp.wait_ge(s_whi, 2 * g + 1)
                sp.wait_ge(s_wlo, 2 * g + 1)
                sp.dma_start(stage_w[:], dram["ga_w"][g + 1]).then_inc(s_stage, 16)
                sp.wait_ge(s_whi, 2 * g + 2)
                sp.wait_ge(s_wlo, 2 * g + 2)
                sp.dma_start(stage_wo[:], dram["ga_wo"][g + 1]).then_inc(s_stwo, 16)

        @block.gpsimd
        def _(pool):
            with pool.Fori(0, NKV) as g:
                pool.wait_ge(s_whi, 2 * g + 1)
                pool.tensor_tensor(w_lo[:], stage_w[:], w_hi[:].bitcast(F32), ALU.subtract).then_inc(s_wlo, 1)
                pool.wait_ge(s_whi, 2 * g + 2)
                pool.tensor_tensor(wo_lo[:], stage_wo[:], wo_hi[:].bitcast(F32), ALU.subtract).then_inc(s_wlo, 1)
                with pool.Fori(0, B) as b:
                    it = g * B + b
                    for t in range(2):
                        pool.wait_ge(s_rot, 6 * it + 3 * t + 3)
                        pool.tensor_tensor(roped[:, t], rot_a[:], rot_b[:], ALU.add).then_inc(s_rope, 1)
                    for h in range(REP):
                        pool.wait_ge(s_inv, REP * it + h + 1)
                        for t, cols in ((0, slice(0, P)), (1, slice(P, P + S))):
                            n = cols.stop - cols.start
                            pool.tensor_tensor(prob[:, h, cols], prob[:, h, cols],
                                               rinv[:, h, t:t + 1].broadcast_to([P, n]),
                                               ALU.mult).then_inc(s_prob, 1)

        @block.scalar
        def _(act):
            with act.Fori(0, NKV) as g:
                act.wait_ge(s_add, B * g + 1)
                act.wait_ge(s_stage, 16 * g + 16)
                act.activation(w_hi[:], stage_w[:], ACT.Copy).then_inc(s_whi, 1)
                act.wait_ge(s_stwo, 16 * g + 16)
                act.activation(wo_hi[:], stage_wo[:], ACT.Copy).then_inc(s_whi, 1)
                with act.Fori(0, B) as b:
                    it = g * B + b
                    for t in range(2):
                        for n, (lo, w) in enumerate(CHUNKS):
                            act.wait_ge(s_q, 2 * NCH * it + NCH * t + n + 1)
                            act.activation(qkv[:, t, lo:lo + w], bank[(NCH * t + n) % 2][:, 0:w],
                                           ACT.Copy).then_inc(s_qc, 1)
                    act.wait_ge(s_T, 5 * it + 1)
                    act.activation(T_hi[:, REP, :], bank[2][:, 0:S], ACT.Copy).then_inc(s_Th, 1)
                    for n in range(4):
                        act.wait_ge(s_T, 5 * it + n + 2)
                        act.activation(T_hi[:, 2 * n:2 * n + 2, :], bank[3 - n % 2][:].rearrange("p (h n) -> p h n", h=2),
                                       ACT.Copy, scale=SCALE).then_inc(s_Th, 1)
                    for h in range(REP):
                        act.wait_ge(s_max, 2 * (REP * it + h) + 2)
                        for t, cols in ((0, slice(0, P)), (1, slice(P, P + S))):
                            act.activation(prob[:, h, cols], bank[4 + h % 4][:, t * S:t * S + (t + 1) * P], ACT.Exp,
                                           bias=nmax[:, h, t:t + 1], accum_out=rsum[:, h, t:t + 1]).then_inc(s_exp, 1)
                        if h >= 3:
                            pT_copy(act, it, h - 3)
                    for h in range(REP - 3, REP):
                        pT_copy(act, it, h)
                    for p in range(4):
                        act.wait_ge(s_o, 4 * it + p + 1)
                        act.activation(oT_hi[:, 2 * p:2 * p + 2, :], bank[p % 2][:].rearrange("p (h n) -> p h n", h=2),
                                       ACT.Copy).then_inc(s_oh, 1)

        @block.vector
        def _(dve):
            dve.memset(nmax[:, 0, :], 0.0).then_inc(s_ol, 1)
            dve.memset(nmax[:, 1, :], 0.0).then_inc(s_add, 1)
            dve.wait_ge(s_const, 48)
            with dve.Fori(0, NKV) as g:
                with dve.Fori(0, B) as b:
                    it = g * B + b
                    dve.wait_ge(s_add, it + 1)
                    dve.tensor_copy(hs_hi[:], h_hi[:, :, bass.ts(b, S)]).then_inc(s_hs, 1)
                    dve.tensor_copy(hs_lo[:], h_lo[:, :, bass.ts(b, S)]).then_inc(s_hs, 1)
                    for t in range(2):
                        dve.wait_ge(s_qc, 2 * NCH * it + NCH * t + NCH)
                        if t:
                            dve.wait_ge(s_rope, 2 * it + 1)
                        q3 = qkv[:, t, 0:NR * HD].rearrange("p (h f) -> p h f", h=NR)
                        cs = lambda v, lo, n: v[:, t, lo:lo + n].unsqueeze(1).broadcast_to([P, NR, n])
                        dve.tensor_tensor(rot_a[:], q3, cs(cos, 0, HD), ALU.mult).then_inc(s_rot, 1)
                        dve.tensor_tensor(rot_b[:, :, 0:half], q3[:, :, half:], cs(sin, 0, half), ALU.mult).then_inc(s_rot, 1)
                        dve.tensor_tensor(rot_b[:, :, half:], q3[:, :, 0:half], cs(sin, half, half), ALU.mult).then_inc(s_rot, 1)
                    dve.wait_ge(s_Th, 5 * it + 1)
                    dve.tensor_tensor(T_lo[:, REP, :], bank[2][:, 0:S], T_hi[:, REP, :].bitcast(F32),
                                      ALU.subtract).then_inc(s_Tl, 1)
                    for n in range(4):
                        dve.wait_ge(s_Th, 5 * it + n + 2)
                        dve.scalar_tensor_tensor(T_lo[:, 2 * n:2 * n + 2, :],
                                                 bank[3 - n % 2][:].rearrange("p (h n) -> p h n", h=2), SCALE,
                                                 T_hi[:, 2 * n:2 * n + 2, :].bitcast(F32),
                                                 ALU.mult, ALU.subtract).then_inc(s_Tl, 1)

                    def inverse(h):
                        dve.wait_ge(s_exp, 2 * (REP * it + h) + 2)
                        dve.reciprocal(rinv[:, h, :], rsum[:, h, :]).then_inc(s_inv, 1)

                    for h in range(REP):
                        dve.wait_ge(s_s, REP * it + h + 1)
                        for t in range(2):
                            dve.tensor_reduce(nmax[:, h, t:t + 1], bank[4 + h % 4][:, t * S:t * S + (t + 1) * P], AX_X,
                                              ALU.max, negate=True).then_inc(s_max, 1)
                        if h >= 1:
                            inverse(h - 1)
                    inverse(REP - 1)
                    for p in range(4):
                        dve.wait_ge(s_oh, 4 * it + p + 1)
                        dve.tensor_tensor(oT_lo[:, 2 * p:2 * p + 2, :], bank[p % 2][:].rearrange("p (h n) -> p h n", h=2),
                                          oT_hi[:, 2 * p:2 * p + 2, :].bitcast(F32), ALU.subtract).then_inc(s_ol, 1)
                    dve.wait_ge(s_y, it + 1)
                    rows2 = x[:, bass.ds(2 * b, 2), :]
                    dve.tensor_tensor(rows2, bank[4][:].rearrange("p (t d) -> p t d", t=2), rows2,
                                      ALU.add).then_inc(s_add, 1)
            dve.wait_ge(s_add, B * NKV + 1)

        @block.tensor
        def _(pe):
            pe.wait_ge(s_const, 48)
            with pe.Fori(0, NKV) as g:
                with pe.Fori(0, B) as b:
                    it = g * B + b
                    pe.wait_ge(s_wlo, 2 * g + 2)
                    pe.wait_ge(s_hs, 2 * it + 2)
                    pe.wait_ge(s_ol, 4 * it + 1)
                    for t in range(2):
                        for n, (lo, w) in enumerate(CHUNKS):
                            m = NCH * t + n
                            if m >= 2:
                                pe.wait_ge(s_qc, 2 * NCH * it + m - 1)
                            for k in range(KD):
                                last = split3(pe, bank[m % 2][:, 0:w], (hs_hi[:, k, tokens(t)], hs_lo[:, k, tokens(t)]),
                                              (w_hi[:, k, lo:lo + w], w_lo[:, k, lo:lo + w]), k == 0, k == KD - 1)
                            last.then_inc(s_q, 1)
                    pe.wait_ge(s_rope, 2 * it + 2)
                    for t in range(2):
                        last = pe.transpose(bank[2][:, t * P:(t + 1) * P], roped[:, t, REP, :], env.ident[:])
                    last.then_inc(s_T, 1)
                    for n in range(4):
                        if n >= 1:
                            pe.wait_ge(s_Tl, 5 * it + n)
                        for j in range(2):
                            for t in range(2):
                                last = pe.transpose(bank[3 - n % 2][:, j * S + t * P:j * S + (t + 1) * P],
                                                    roped[:, t, 2 * n + j, :], env.ident[:])
                        last.then_inc(s_T, 1)
                    pe.wait_ge(s_add, it + 1)
                    for h in range(REP):
                        if h >= 4:
                            pe.wait_ge(s_exp, 2 * (REP * it + h - 4) + 2)
                        pe.wait_ge(s_Tl, 5 * it + 2 + h // 2)
                        for t in range(2):
                            out = bank[4 + h % 4][:, t * S:(t + 1) * S]
                            split3(pe, out, (T_hi[:, h, tokens(t)], T_lo[:, h, tokens(t)]),
                                   (T_hi[:, REP, :], T_lo[:, REP, :]), True, False)
                            last = pe.matmul(out[:, t * P:(t + 1) * P], env.ident_bf[:], causal[:], start=False, stop=True,
                                             skip_group_check=True)
                        last.then_inc(s_s, 1)
                        if h >= 3:
                            turn(pe, it, h - 3)
                    for h in range(REP - 3, REP):
                        turn(pe, it, h)
                    for p in range(4):
                        pe.wait_ge(s_pTc, REP * it + 2 * p + 2)
                        if p >= 2:
                            pe.wait_ge(s_ol, 4 * it + p)
                        o3 = bank[p % 2][:].rearrange("p (h n) -> p h n", h=2)
                        pe.matmul(bank[p % 2][:], qkv[:, 0, NR * HD:], pT[:, 2 * p:2 * p + 2, 0:S],
                                  start=True, stop=False, skip_group_check=True)
                        pe.matmul(o3[:, :, P:], qkv[:, 1, NR * HD:], pT[:, 2 * p:2 * p + 2, S:],
                                  start=False, stop=True, skip_group_check=True).then_inc(s_o, 1)
                    for t in range(2):
                        for h in range(REP):
                            if t == 0 and h % 2 == 0:
                                pe.wait_ge(s_ol, 4 * it + h // 2 + 2)
                            last = split3(pe, bank[4][:, t * D:(t + 1) * D], (oT_hi[:, h, tokens(t)], oT_lo[:, h, tokens(t)]),
                                          (wo_hi[:, h, :], wo_lo[:, h, :]), h == 0, h == REP - 1)
                    last.then_inc(s_y, 1)


def program(nc, dram, out, stages=("A", "B", "C", "D", "E")):
    with ExitStack() as ctx:
        env = Env(nc, ctx, dram)
        env.x = env.sb("x", [P, NT, D])
        env.x_in = env.sb("x_in", [P, NT, D])
        env.ident, env.ident_bf = env.sb("ident", [P, P]), env.sb("ident_bf", [P, P], BF16)
        env.minus_half = env.sb("minus_half", [P, NT])
        env.bank = [ctx.enter_context(nc.psum_tensor(f"bank{i}", [P, 512], F32)) for i in range(8)]
        s_in, s_out, s_half = env.sem("inputs_loaded"), env.sem("out_stored"), env.sem("minus_half_ready")
        with nc.Block() as block:
            @block.sync
            def _(sp):
                sp.dma_start(env.x[:], dram["x"]).then_inc(s_in, 16)
                sp.dma_start(env.ident[:], dram["ident"]).then_inc(s_in, 16)
                sp.dma_start(env.ident_bf[:], dram["ident_bf"]).then_inc(s_in, 16)
                sp.wait_ge(s_in, 48)

            @block.gpsimd
            def _(pool):
                pool.memset(env.minus_half[:], -0.5).then_inc(s_half, 1)
                pool.wait_ge(s_half, 1)
        if "A" in stages:
            env.stage(lambda: quantised_attention(env))
        if "B" in stages:
            env.stage(lambda: experts(env, "f0", 0))
        if "C" in stages:
            env.stage(lambda: latent_attention(env))
        if "D" in stages:
            env.stage(lambda: grouped_attention(env))
        if "E" in stages:
            env.stage(lambda: experts(env, "f1", 1))
        with nc.Block() as block:
            @block.sync
            def _(sp):
                sp.dma_start(out, env.x[:]).then_inc(s_out, 16)
                sp.wait_ge(s_out, 16)


def rows(v, n=128):
    import numpy as np
    return np.broadcast_to(v, (n,) + v.shape)


def layout(i):
    import numpy as np
    bf = mybir.dt.np(BF16)
    c = lambda a: np.ascontiguousarray(a)
    tok = lambda a: c(a.reshape(NT, P, -1).transpose(1, 0, 2))
    kmaj = lambda w: w.reshape(KD, P, -1).transpose(1, 0, 2)
    d = {}
    d["x"] = tok(i["x"])
    d["ident"] = np.eye(P, dtype=np.float32)
    d["ident_bf"] = np.eye(P).astype(bf)

    def unit_weights(g, u, w):
        return np.concatenate([kmaj(g).reshape(P, -1), kmaj(u).reshape(P, -1), w], axis=1)

    g, u, w = i["L0_ffn_Wg"], i["L0_ffn_Wu"], i["L0_ffn_Wd"]
    d["f0_weights"] = c(np.stack([unit_weights(g[e][:, f], u[e][:, f], w[e][f]) for e in range(8)
                                  for f in (slice(0, 128), slice(128, 256))]))
    g, u, w = i["L1_ffn_Wg"], i["L1_ffn_Wu"], i["L1_ffn_Wd"]
    d["f1_weights"] = c(np.stack([unit_weights(g[e], u[e], w[e]) for e in range(32)]
                                 + [unit_weights(i["L1_ffn_Wsg"], i["L1_ffn_Wsu"], i["L1_ffn_Wsd"])]))
    for tag, r in (("f0", i["L0_ffn_Wr"]), ("f1", i["L1_ffn_Wr"])):
        pad = np.zeros((P, KD, P), np.float32)
        pad[:, :, :r.shape[1]] = kmaj(r)
        d[f"{tag}_wr"] = pad
    d["f0_route"] = c(np.broadcast_to(i["L0_ffn_temperature"], (P, 32)))
    d["f1_route"] = c(rows(i["L1_ffn_expert_bias"]))
    d["ln2_rows"] = c(rows(i["L1_ffn_ln2_w"]))
    d["before"] = c(rows(np.tril(np.ones((8, 8), np.float32), -1)))
    sel = np.zeros((3, RW, RW, P), np.float32)
    for e in range(RW):
        sel[:, e, e, :] = 1
    d["sel"] = sel.reshape(3 * RW, RW * P).astype(bf)

    d["wq_wo"] = c(np.concatenate([i[f"L0_xattn_w{n}"].reshape(2, P, D) for n in "qo"]).transpose(1, 0, 2))
    d["wkvT"] = c(np.concatenate([kmaj(i[f"L0_xattn_w{n}"].T) for n in "kv"], axis=2))
    d["l0_bias"] = c(rows(np.stack([i[f"L0_xattn_b{n}"] for n in "qkvo"])))
    d["mask"] = tok(i["mask_BxSxS2_ff0"])
    d["ctxT"] = c(i["ctx_2048"].reshape(TOK, KD, P).transpose(2, 1, 0))
    d["w_kvc"] = c(kmaj(i["L1_xattn_W_kvc"]))
    d["w_dq"] = np.zeros((P, KD, P), np.float32)
    d["w_dq"][:, :, :QC] = kmaj(i["L1_xattn_W_dq"])
    d["uqT"] = c(i["L1_xattn_W_uq"].reshape(QC, H1, HD1).transpose(2, 1, 0))
    d["ukT"] = c(i["L1_xattn_W_uk"].reshape(KVC, H1, HD1).transpose(2, 1, 0))
    uvT = i["L1_xattn_W_uv"].reshape(KVC, H1, HD1).transpose(2, 1, 0)
    d["uvT2"] = c(np.concatenate([uvT, uvT], axis=2))
    d["la_wo"] = c(i["L1_xattn_W_o"].reshape(H1, HD1, D).transpose(1, 0, 2))
    d["qr"] = c(i["L1_xattn_W_qr"].reshape(QC, H1, RD))
    d["key_w"] = c(np.concatenate([np.eye(KVC, dtype=np.float32), i["L1_xattn_W_kr"]], axis=1))
    d["la_cos"], d["la_sin"] = rotary(RD)
    d["seg"] = c(i["itok_BxS_0_1023"].reshape(NT, P).T)
    d["key_id"] = c(rows(np.arange(S, dtype=np.float32)))
    wq = kmaj(i["L1_ffn_Wq"]).reshape(P, KD, NKV, REP * HD)
    wk, wv = (kmaj(i[f"L1_ffn_W{n}"]).reshape(P, KD, NKV, HD) for n in "kv")
    d["ga_w"] = c(np.concatenate([wq, wk, wv], axis=3).transpose(2, 0, 1, 3))
    d["ga_wo"] = c(i["L1_ffn_Wo"].reshape(NKV, REP, HD, D).transpose(0, 2, 1, 3))
    d["ln1_rows"] = c(rows(i["L1_ffn_ln1_w"]))
    d["ga_cos"], d["ga_sin"] = rotary(HD)
    d["causal"] = np.where(np.tril(np.ones((P, P), bool)), 0.0, NEG).astype(bf)
    return d


def rotary(width):
    import numpy as np
    half = width // 2
    freq = (np.float32(1.0) / np.float32(10000.0) ** (np.arange(half, dtype=np.float32) / np.float32(half)))
    ang = (np.arange(S, dtype=np.float32)[:, None] * freq.astype(np.float32)).astype(np.float32)
    lay = lambda a, b: np.ascontiguousarray(
        np.concatenate([a, b], axis=1).astype(np.float32).reshape(S // P, P, width).transpose(1, 0, 2))
    cos, sin = np.cos(ang.astype(np.float64)), np.sin(ang.astype(np.float64))
    return lay(cos, cos), lay(-sin, sin)


def kernel(**inputs):
    import numpy as np
    import concourse.bacc as bacc
    from concourse.bass_utils import run_bass_kernel_spmd

    nc = bacc.Bacc("TRN2", target_bir_lowering=False, num_devices=1)
    arrays = {f"in_{k}": v for k, v in layout({k: np.asarray(v) for k, v in inputs.items()}).items()}
    dram = {k[3:]: nc.dram_tensor(k, v.shape, mybir.dt.from_np(v.dtype), kind="ExternalInput").ap()
            for k, v in arrays.items()}
    out = nc.dram_tensor("out", (P, NT, D), F32, kind="ExternalOutput").ap()
    program(nc, dram, out)
    r = run_bass_kernel_spmd(nc, [arrays], core_ids=[0])
    y = r.results[0]["out"]
    return np.ascontiguousarray(y.transpose(1, 0, 2)).reshape(B, S, D)
```

```python
import math
from contextlib import ExitStack

import concourse.bass as bass
from concourse import mybir

F32 = mybir.dt.float32
F32R = mybir.dt.float32r
BF16 = mybir.dt.bfloat16
I32 = mybir.dt.int32
ALU = mybir.AluOpType
ACT = mybir.ActivationFunctionType
AX_X = mybir.AxisListType.X

P = 128
B, S, D = 4, 256, 256
TOK = B * S
NT = TOK // P
KD = D // P
MAGIC = 1.5 * 2.0 ** 23
NEG = -1e30


class Env:

    def __init__(self, nc, ctx, dram):
        self.nc, self.ctx, self.dram = nc, ctx, dram
        self.stage_ctx, self.stage_sems = ctx, []

    def sb(self, name, shape, dt=F32, ctx=None):
        return (ctx or self.ctx).enter_context(self.nc.sbuf_tensor(name, shape, dt))

    def sem(self, name):
        handle = self.stage_ctx.enter_context(self.nc.semaphore(name))
        self.stage_sems.append(handle)
        return handle

    def stage(self, build):
        with ExitStack() as self.stage_ctx:
            self.stage_sems = []
            build()
            numbers = sorted(s.num for s in self.stage_sems)
            runs, first = [], numbers[0]
            for a, b in zip(numbers, numbers[1:] + [None]):
                if b != a + 1:
                    runs.append(range(first, a + 1))
                    first = b
            with self.nc.Block() as block:
                @block.sync
                def _(sp):
                    for run in runs:
                        sp.sem_clear(run)


def tokens(t):
    return slice(t * P, (t + 1) * P)


def wait_from_one(eng, sem, value):
    if not isinstance(value, int) or value > 0:
        eng.wait_ge(sem, value)


def split3(pe, out, a, b, start, stop):
    (ah, al), (bh, bl) = a, b
    pe.matmul(out, ah, bh, start=start, stop=False, skip_group_check=True)
    pe.matmul(out, ah, bl, start=False, stop=False, skip_group_check=True)
    return pe.matmul(out, al, bh, start=False, stop=stop, skip_group_check=True)


class Group:

    def __init__(self, n, outer, inner):
        self.n, self.outer, self.inner = n, outer, inner


def pipelined(eng, outer, inner, begin, step, finish):
    begin(Group(0, 0, 0))
    with eng.Fori(0, outer - 1) as o:
        with eng.Fori(0, inner - 1) as i:
            step(Group(o * inner + i, o, i), Group(o * inner + i + 1, o, i + 1), False)
        step(Group(o * inner + inner - 1, o, inner - 1), Group(o * inner + inner, o + 1, 0), True)
    last = outer - 1
    with eng.Fori(0, inner - 1) as i:
        step(Group(last * inner + i, last, i), Group(last * inner + i + 1, last, i + 1), False)
    finish(Group(outer * inner - 1, last, inner - 1))


class Norm:

    def __init__(self, env, tag, mem, rms_weight=None, dst=None):
        self.e, self.tag, self.rms = env, tag, rms_weight
        sb = lambda n, s, d=F32: env.sb(f"{tag}_{n}", s, d, mem)
        self.stats = sb("bn_stats", [P, NT, 6])
        self.moments = sb("moments", [P, NT, 2])
        self.square = sb("square", [P, D]) if rms_weight is not None else None
        self.var_eps = sb("var_eps", [P, NT])
        self.rstd = sb("rstd", [P, NT])
        self.xn = sb("xn", [P, NT, D]) if dst is None else dst
        s = lambda n: env.sem(f"{tag}_{n}")
        self.s_stats, self.s_moments, self.s_var = s("stats_done"), s("moments_done"), s("var_done")
        self.s_rstd, self.s_xn = s("rstd_done"), s("xn_ready")
        self.s_tr, self.s_hi, self.s_lo = s("xT_in_psum"), s("xT_hi_ready"), s("xT_lo_ready")

    def scalar_stats(self, act):
        for t in range(NT):
            if t:
                act.wait_ge(self.s_stats, t)
            act.activation(self.square[:], self.e.x[:, t, :], ACT.Square,
                           accum_out=self.moments[:, t, 0:1]).then_inc(self.s_stats, 1)

    def vector_normalise(self, dve, kept=None):
        x = self.e.x
        if self.rms is None:
            for t in range(NT):
                dve.bn_stats(self.stats[:, t, :], x[:, t, :]).then_inc(self.s_stats, 1)
            for t in range(NT):
                dve.wait_ge(self.s_stats, t + 1)
                dve.bn_aggr(self.moments[:, t, :], self.stats[:, t, :]).then_inc(self.s_moments, 1)
            dve.wait_ge(self.s_moments, NT)
            dve.tensor_scalar(self.var_eps[:], self.moments[:, :, 1], 1e-5, None, ALU.add).then_inc(self.s_var, 1)
        else:
            dve.wait_ge(self.s_stats, NT)
            dve.tensor_scalar(self.var_eps[:], self.moments[:, :, 0], 1.0 / D, 1e-5,
                              ALU.mult, ALU.add).then_inc(self.s_var, 1)
        dve.wait_ge(self.s_rstd, 1)
        if kept is not None:
            dve.wait_ge(kept, 1)
        for t in range(NT):
            if self.rms is None:
                dve.tensor_scalar(self.xn[:, t, :], x[:, t, :], self.moments[:, t, 0:1], self.rstd[:, t:t + 1],
                                  ALU.subtract, ALU.mult).then_inc(self.s_xn, 1)
            else:
                dve.scalar_tensor_tensor(self.xn[:, t, :], x[:, t, :], self.rstd[:, t:t + 1], self.rms[:],
                                         ALU.mult, ALU.mult).then_inc(self.s_xn, 1)

    def gpsimd_rstd(self, pool):
        pool.wait_ge(self.s_var, 1)
        pool.tensor_tensor(self.rstd[:], self.var_eps[:], self.e.minus_half[:], ALU.pow).then_inc(self.s_rstd, 1)

    def tensor_transpose(self, pe, banks):
        for b in range(B):
            pe.wait_ge(self.s_xn, 2 * b + 2)
            if b >= 2:
                pe.wait_ge(self.s_lo, b - 1)
            bank = banks[b % 2][:].rearrange("p (k t q) -> p k t q", k=KD, t=2)
            for k in range(KD):
                for t in range(2):
                    last = pe.transpose(bank[:, k, t, :], self.xn[:, 2 * b + t, k * P:(k + 1) * P], self.e.ident[:])
            last.then_inc(self.s_tr, 1)

    def scalar_hi(self, act, banks, hi):
        for b in range(B):
            act.wait_ge(self.s_tr, b + 1)
            act.activation(hi[:, :, b * S:(b + 1) * S], banks[b % 2][:].rearrange("p (k q) -> p k q", k=KD),
                           ACT.Copy).then_inc(self.s_hi, 1)

    def vector_lo(self, dve, banks, hi, lo):
        for b in range(B):
            dve.wait_ge(self.s_hi, b + 1)
            cols = slice(b * S, (b + 1) * S)
            dve.tensor_tensor(lo[:, :, cols], banks[b % 2][:].rearrange("p (k q) -> p k q", k=KD),
                              hi[:, :, cols].bitcast(F32), ALU.subtract).then_inc(self.s_lo, 1)
H0, HD0 = 16, 16
HG0 = 4
NG0 = H0 // HG0
QMAX, QEPS = 127.0, 1e-8
MASK_LOW = -1e38


class Quant:

    def __init__(self, env, tag, mem, n):
        self.n = n
        self.scale, self.inv = env.sb(f"{tag}_scale", [P, n], F32, mem), env.sb(f"{tag}_inv", [P, n], F32, mem)
        self.work = env.sb(f"{tag}_work", [P, n, D], F32, mem)
        self.whole = env.sb(f"{tag}_whole", [P, n, D], BF16, mem)
        self.stepped, self.ready = env.sem(f"{tag}_stepped"), env.sem(f"{tag}_ready")

    def run(self, dve, rows):
        n = self.n
        dve.tensor_reduce(self.scale[:], rows, AX_X, ALU.max, apply_absolute_value=True).then_inc(self.stepped, 1)
        dve.wait_ge(self.stepped, 1)
        dve.tensor_scalar(self.scale[:], self.scale[:], 1.0 / QMAX, QEPS, ALU.mult, ALU.max).then_inc(self.stepped, 1)
        dve.wait_ge(self.stepped, 2)
        dve.reciprocal(self.inv[:], self.scale[:]).then_inc(self.stepped, 1)
        dve.wait_ge(self.stepped, 3)
        for i in range(n):
            dve.tensor_scalar(self.work[:, i, :], rows[:, i, :], self.inv[:, i:i + 1], QMAX,
                              ALU.mult, ALU.min).then_inc(self.stepped, 1)
        dve.wait_ge(self.stepped, 3 + n)
        dve.tensor_scalar(self.work[:], self.work[:], -QMAX, MAGIC, ALU.max, ALU.add).then_inc(self.stepped, 1)
        dve.wait_ge(self.stepped, 4 + n)
        dve.tensor_scalar(self.whole[:], self.work[:], MAGIC, None, ALU.subtract).then_inc(self.ready, 1)


def quantised_attention(env):
    nc, dram, x = env.nc, env.dram, env.x
    bank = env.bank
    with ExitStack() as mem:
        sb = lambda n, s, d=F32: env.sb(f"qa_{n}", s, d, mem)
        sem = lambda n: env.sem(f"qa_{n}")
        GROUPS, GW = B * NG0, HG0 * HD0
        q_grp, kv_grp = sb("q_grp", [P, GROUPS + 1, 2, GW]), sb("kv_grp", [P, GROUPS + 1, 2, 2, GW])
        o_tok = sb("o_tok", [P, NT, D])
        mask_hi, mask_lo = sb("mask_hi", [P, NT, S], F32R), sb("mask_lo", [P, NT, S], F32R)
        ident_r = sb("ident_r", [P, P], F32R)
        w_rows = sb("w_rows", [P, 2, D])
        wT = sb("wT", [P, 2, KD, D], BF16)
        bias_rows = sb("bias_rows", [P, 4, D])
        s_in, s_mask = sem("inputs_loaded"), sem("mask_loaded")
        half_banks = lambda t: bank[4 + t // 2 % 4][:, (t % 2) * D:(t % 2 + 1) * D]

        def turn_rows(pe, quant, done):
            for n in range(2):
                v = bank[n][:].bitcast(BF16).rearrange("p (k t m) -> p k t m", k=KD, t=4)
                for k in range(KD):
                    for t in range(4):
                        last = pe.transpose(v[:, k, t, :], quant.whole[:, 4 * n + t, k * P:(k + 1) * P], env.ident_bf[:])
                last.then_inc(done, 1)

        with ExitStack() as prep:
            sp_ = lambda n, s, d=F32: env.sb(f"qa_{n}", s, d, prep)
            norm = Norm(env, "qa", prep)
            wq_wo = sp_("wq_wo", [P, 4, D])
            ctxT, wkvT = sp_("ctxT", [P, KD, TOK]), sp_("wkvT", [P, KD, 2 * D])
            c_hi, c_lo = sp_("c_hi", [P, KD, TOK], F32R), sp_("c_lo", [P, KD, TOK], F32R)
            wkv_hi, wkv_lo = sp_("wkv_hi", [P, KD, 2 * D], F32R), sp_("wkv_lo", [P, KD, 2 * D], F32R)
            mask, q_scaled = sp_("mask", [P, NT, S]), sp_("q_scaled", [P, NT, D])
            ones, diag = sp_("ones", [P, P]), sp_("diag", [P, 4, P])
            xqT = sp_("xqT", [P, KD, TOK], BF16)
            wquant, xquant = Quant(env, "qa_wq", prep, 4), Quant(env, "qa_xq", prep, NT)
            s_hi, s_lo, s_ones = sem("hi_ready"), sem("lo_ready"), sem("ones_ready")
            s_clamp, s_mhi, s_mlo = sem("mask_clamped"), sem("mask_hi_ready"), sem("mask_lo_ready")
            s_end = sem("last_group_zero")
            s_diag, s_rows, s_rowc = sem("diag_ready"), sem("w_rows_in_psum"), sem("w_rows_copied")
            s_wTp, s_wT, s_xTp, s_xT = sem("wT_in_psum"), sem("wT_ready"), sem("xqT_in_psum"), sem("xqT_ready")
            s_kv, s_kvc, s_q, s_qs, s_qb = (sem(n) for n in (
                "kv_in_psum", "kv_ready", "q_in_psum", "q_scaled", "q_ready"))
            block = prep.enter_context(nc.Block())

            @block.sync
            def _(sp):
                for dst, name in ((wq_wo, "wq_wo"), (ctxT, "ctxT"), (wkvT, "wkvT"), (bias_rows, "l0_bias")):
                    sp.dma_start(dst[:], dram[name]).then_inc(s_in, 16)
                sp.dma_start(mask[:], dram["mask"]).then_inc(s_mask, 16)

            @block.gpsimd
            def _(pool):
                pool.memset(ones[:], 1.0).then_inc(s_ones, 1)
                pool.memset(q_grp[:, GROUPS], 0.0).then_inc(s_end, 1)
                pool.memset(kv_grp[:, GROUPS], 0.0).then_inc(s_end, 1)
                norm.gpsimd_rstd(pool)
                pool.wait_ge(s_hi, 1)
                pool.tensor_tensor(wkv_lo[:], wkvT[:], wkv_hi[:].bitcast(F32), ALU.subtract).then_inc(s_lo, 1)
                pool.wait_ge(s_hi, 2)
                pool.tensor_tensor(c_lo[:], ctxT[:], c_hi[:].bitcast(F32), ALU.subtract).then_inc(s_lo, 1)
                pool.wait_ge(s_mhi, 2)
                pool.tensor_tensor(mask_lo[:], mask[:], mask_hi[:].bitcast(F32), ALU.subtract).then_inc(s_mlo, 1)

            @block.scalar
            def _(act):
                act.wait_ge(s_in, 64)
                act.activation(wkv_hi[:], wkvT[:], ACT.Copy).then_inc(s_hi, 1)
                act.activation(c_hi[:], ctxT[:], ACT.Copy).then_inc(s_hi, 1)
                act.activation(ident_r[:], env.ident[:], ACT.Copy).then_inc(s_mhi, 1)
                act.wait_ge(s_clamp, 1)
                act.activation(mask_hi[:], mask[:], ACT.Copy).then_inc(s_mhi, 1)
                act.wait_ge(s_rows, 1)
                act.activation(w_rows[:].rearrange("p w d -> p (w d)"), bank[0][:], ACT.Copy).then_inc(s_rowc, 1)
                act.wait_ge(s_wTp, 1)
                act.activation(wT[:].rearrange("p w k d -> p (w k d)"), bank[1][:].bitcast(BF16),
                               ACT.Copy).then_inc(s_wT, 1)
                for n in range(2):
                    act.wait_ge(s_xTp, n + 1)
                    act.activation(xqT[:, :, n * 512:(n + 1) * 512],
                                   bank[n][:].bitcast(BF16).rearrange("p (k q) -> p k q", k=KD), ACT.Copy).then_inc(s_xT, 1)

            @block.vector
            def _(dve):
                dve.wait_ge(s_in, 64)
                wquant.run(dve, wq_wo[:])
                for i in range(4):
                    dve.tensor_scalar(diag[:, i, :], env.ident[:], wquant.scale[:, i:i + 1], None, ALU.mult).then_inc(s_diag, 1)
                norm.vector_normalise(dve)
                dve.wait_ge(norm.s_xn, NT)
                xquant.run(dve, norm.xn[:])
                dve.wait_ge(s_mask, 16)
                dve.tensor_scalar(mask[:], mask[:], MASK_LOW, None, ALU.max).then_inc(s_clamp, 1)
                for t in range(NT):
                    dve.wait_ge(s_kv, t + 1)
                    dve.tensor_tensor(kv_grp[:, t // 2 * NG0:(t // 2 + 1) * NG0, :, t % 2, :].rearrange("p g a d -> p a g d"),
                                      bank[2 + t % 2][:].rearrange("p (a g d) -> p a g d", a=2, g=NG0),
                                      bias_rows[:, 1:3, :].rearrange("p a (g d) -> p a g d", g=NG0),
                                      ALU.add).then_inc(s_kvc, 1)
                dve.wait_ge(s_rowc, 1)
                for t in range(NT):
                    dve.wait_ge(s_q, t // 2 * 2 + 2)
                    dve.scalar_tensor_tensor(q_scaled[:, t, :], half_banks(t), xquant.scale[:, t:t + 1], w_rows[:, 0, :],
                                             ALU.mult, ALU.mult).then_inc(s_qs, 1)
                dve.wait_ge(s_qs, NT)
                for t in range(NT):
                    dve.tensor_tensor(q_grp[:, t // 2 * NG0:(t // 2 + 1) * NG0, t % 2, :],
                                      q_scaled[:, t, :].rearrange("p (g d) -> p g d", g=NG0),
                                      bias_rows[:, 0, :].rearrange("p (g d) -> p g d", g=NG0), ALU.add).then_inc(s_qb, 1)
                dve.wait_ge(s_qb, NT)
                dve.wait_ge(s_kvc, NT)
                dve.wait_ge(s_mlo, 1)
                dve.wait_ge(s_end, 2)

            @block.tensor
            def _(pe):
                pe.wait_ge(s_ones, 1)
                pe.wait_ge(s_diag, 4)
                pe.matmul(bank[0][:], ones[:], diag[:].rearrange("p i m -> p (i m)"), start=True, stop=True).then_inc(s_rows, 1)
                pe.wait_ge(wquant.ready, 1)
                wb = bank[1][:].bitcast(BF16).rearrange("p (w k o m) -> p w k o m", w=2, k=KD, o=2)
                for w in range(2):
                    for k in range(KD):
                        for o in range(2):
                            last = pe.transpose(wb[:, w, k, o, :], wquant.whole[:, 2 * w + o, k * P:(k + 1) * P],
                                                env.ident_bf[:])
                last.then_inc(s_wTp, 1)
                pe.wait_ge(s_lo, 2)
                for t in range(NT):
                    if t >= 2:
                        pe.wait_ge(s_kvc, t - 1)
                    for k in range(KD):
                        last = split3(pe, bank[2 + t % 2][:], (c_hi[:, k, tokens(t)], c_lo[:, k, tokens(t)]),
                                      (wkv_hi[:, k, :], wkv_lo[:, k, :]), k == 0, k == KD - 1)
                    last.then_inc(s_kv, 1)
                pe.wait_ge(xquant.ready, 1)
                pe.wait_ge(s_rowc, 1)
                pe.wait_ge(s_wT, 1)
                turn_rows(pe, xquant, s_xTp)
                for t in range(NT):
                    pe.wait_ge(s_xT, t // 4 + 1)
                    for k in range(KD):
                        last = pe.matmul(half_banks(t), xqT[:, k, tokens(t)], wT[:, 0, k, :], start=k == 0, stop=k == KD - 1)
                    last.then_inc(s_q, 1)

        with ExitStack() as loop:
            sl = lambda n, s, d=F32: env.sb(f"qa_{n}", s, d, loop)
            qd, kd = sl("qd", [P, 2, HG0, 4, HD0], F32R), sl("kd", [P, 2, HG0, 4, HD0], F32R)
            qT = sl("qT", [P, 2, S], F32R)
            kT = sl("kT", [P, 2, 2, S], F32R)
            vp = sl("vp", [P, 2, HG0, 32])
            prob = sl("prob", [P, 4, 2, S])
            nmax, rsum, rinv = sl("nmax", [P, 4, 2]), sl("rsum", [P, 4, 2]), sl("rinv", [P, 4, 2])
            pT = sl("pT", [P, 2, HG0, S])
            oT = sl("oT", [P, S])
            s_zero = sem("zeros_ready")
            s_dh, s_dl, s_v = sem("parts_hi_ready"), sem("parts_lo_ready"), sem("values_ready")
            s_T, s_Ta, s_Tv = sem("qk_T_in_psum"), sem("q_and_low_keys_copied"), sem("high_keys_copied")
            s_s, s_max, s_exp, s_inv = (sem(n) for n in ("scores_in_psum", "max_ready", "exp_ready", "row_inverse_ready"))
            s_pT, s_pTa, s_pTv = sem("pT_in_psum"), sem("pT_copied_by_scalar"), sem("pT_copied_by_vector")
            s_o, s_oc, s_oT, s_done = sem("oT_in_psum"), sem("oT_copied"), sem("o_in_psum"), sem("o_ready")
            block = loop.enter_context(nc.Block())
            twice = lambda v: v.rearrange("p (h d) -> p h d", h=HG0).unsqueeze(2).broadcast_to([P, HG0, 2, HD0])

            def q_cols(n, t):
                return q_grp[:].rearrange("p g t d -> p (g t d)")[:, bass.ds(n * (2 * GW) + t * GW, GW)]

            def kv_cols(n, a, t):
                return kv_grp[:].rearrange("p g a t d -> p (g a t d)")[:, bass.ds(n * (4 * GW) + (2 * a + t) * GW, GW)]

            def pT_view(u):
                return pT[:, :, 2 * (u // 2):2 * (u // 2) + 2, (u % 2) * P:(u % 2 + 1) * P]

            def pT_bank(u):
                return bank[4 + u][:].rearrange("p (k j n) -> p k j n", k=2, j=2)

            @block.gpsimd
            def _(pool):
                def parts(n):
                    wait_from_one(pool, s_T, 2 * n)
                    for t in range(2):
                        pool.tensor_copy(qd[:, t, :, 0:2, :], twice(q_cols(n, t))).then_inc(s_dh, 1)
                        pool.tensor_copy(kd[:, t, :, 0::2, :], twice(kv_cols(n, 0, t))).then_inc(s_dh, 1)

                def values(n):
                    wait_from_one(pool, s_o, 2 * n)
                    for t in range(2):
                        pool.tensor_copy(vp[:, t, :, 0:HD0], kv_cols(n, 1, t).rearrange("p (h d) -> p h d", h=HG0)
                                         ).then_inc(s_v, 1)

                pool.memset(vp[:], 0.0).then_inc(s_zero, 1)
                pool.memset(kT[:].bitcast(F32), 0.0).then_inc(s_zero, 1)
                pool.wait_ge(s_zero, 2)
                parts(0)
                values(0)
                parts(1)
                with pool.Fori(0, GROUPS - 1) as i:
                    parts(i + 2)
                    values(i + 1)

            @block.scalar
            def _(act):
                def turned(n):
                    act.wait_ge(s_T, 2 * n + 1)
                    act.activation(kT[0:64, :, 0, :], bank[0][0:64, :].rearrange("p (a n) -> p a n", a=2),
                                   ACT.Copy).then_inc(s_Ta, 1)
                    act.wait_ge(s_T, 2 * n + 2)
                    act.activation(qT[:].rearrange("p a n -> p (a n)"), bank[1][:], ACT.Copy,
                                   scale=1.0 / math.sqrt(HD0)).then_inc(s_Ta, 1)

                def exps(n):
                    for u in range(4):
                        act.wait_ge(s_max, 4 * n + u + 1)
                        for j in range(2):
                            act.activation(prob[:, u, j, :], bank[4 + u][:, j * S:(j + 1) * S], ACT.Exp,
                                           bias=nmax[:, u, j:j + 1], accum_out=rsum[:, u, j:j + 1]).then_inc(s_exp, 1)

                def probs_turned(n):
                    for u in (0, 2):
                        act.wait_ge(s_pT, 4 * n + u + 1)
                        act.activation(pT_view(u), pT_bank(u), ACT.Copy).then_inc(s_pTa, 1)

                def group(n):
                    exps(n)
                    turned(n + 1)
                    probs_turned(n)

                act.wait_ge(s_zero, 2)
                turned(0)
                group(0)
                with act.Fori(0, GROUPS - 1) as i:
                    group(i + 1)

            @block.vector
            def _(dve):
                def parts(n):
                    for t in range(2):
                        dve.wait_ge(s_dh, 4 * n + 2 * t + 2)
                        dve.tensor_tensor(qd[:, t, :, 2:4, :], twice(q_cols(n, t)), qd[:, t, :, 0:2, :].bitcast(F32),
                                          ALU.subtract).then_inc(s_dl, 1)
                        dve.tensor_tensor(kd[:, t, :, 1::2, :], twice(kv_cols(n, 0, t)),
                                          kd[:, t, :, 0::2, :].bitcast(F32), ALU.subtract).then_inc(s_dl, 1)

                def turned(n):
                    dve.wait_ge(s_T, 2 * n + 1)
                    dve.tensor_copy(kT[64:P, :, 1, :], bank[0][64:P, :].rearrange("p (a n) -> p a n", a=2)).then_inc(s_Tv, 1)

                def maxima(n):
                    for u in range(4):
                        dve.wait_ge(s_s, 4 * n + u + 1)
                        dve.tensor_reduce(nmax[:, u, :], bank[4 + u][:].rearrange("p (j n) -> p j n", j=2), AX_X,
                                          ALU.max, negate=True).then_inc(s_max, 1)

                def outputs(n):
                    for h in range(HG0):
                        if h % 2 == 0:
                            dve.wait_ge(s_o, 2 * n + h // 2 + 1)
                        r = slice(32 * h, 32 * h + 32)
                        dve.tensor_copy(oT[r, :], bank[2 + h // 2][r, (h % 2) * S:(h % 2 + 1) * S]).then_inc(s_oc, 1)

                def probs_turned(n):
                    for u in (1, 3):
                        dve.wait_ge(s_pT, 4 * n + u + 1)
                        dve.tensor_copy(pT_view(u), pT_bank(u)).then_inc(s_pTv, 1)

                def inverse(n):
                    dve.wait_ge(s_exp, 8 * n + 8)
                    dve.wait_ge(s_done, 2 * n + 1)
                    dve.reciprocal(rinv[:], rsum[:]).then_inc(s_inv, 1)

                def store(g):
                    dve.wait_ge(s_oT, g.n + 1)
                    dve.wait_ge(s_inv, g.n + 1)
                    for t in range(2):
                        o4 = bank[2][:, t * P:(t + 1) * P].rearrange("p (a j d) -> p a j d", a=2, j=2)
                        inv = rinv[:, t::2, :].unsqueeze(3).broadcast_to([P, 2, 2, HD0])
                        out = o_tok[:].rearrange("p t d -> p (t d)")[:, bass.ds(g.outer * (2 * D) + g.inner * GW + t * D, GW)]
                        dve.tensor_tensor(out.rearrange("p (a j d) -> p a j d", a=2, j=2), o4[:, :, :, 0:HD0], inv,
                                          ALU.mult).then_inc(s_done, 1)

                def begin(first):
                    parts(0)
                    turned(0)
                    maxima(0)
                    parts(1)
                    turned(1)
                    probs_turned(0)
                    inverse(0)

                def step(cur, nxt, edge):
                    maxima(nxt.n)
                    parts(nxt.n + 1)
                    outputs(cur.n)
                    turned(nxt.n + 1)
                    probs_turned(nxt.n)
                    store(cur)
                    inverse(nxt.n)

                def finish(last):
                    outputs(last.n)
                    store(last)

                dve.memset(nmax[:, 0, :], 0.0).then_inc(s_done, 1)
                dve.wait_ge(s_done, 1)
                dve.wait_ge(s_zero, 2)
                pipelined(dve, B, NG0, begin, step, finish)
                dve.wait_ge(s_done, 2 * B * NG0 + 1)

            @block.tensor
            def _(pe):
                def turn(n):
                    for to, src in ((0, kd), (1, qd)):
                        pe.wait_ge(s_dl, 4 * n + 4)
                        for p in range(2):
                            for t in range(2):
                                last = pe.transpose(bank[to][:, p * S + t * P:p * S + (t + 1) * P],
                                                    src[:, t, 2 * p:2 * p + 2, :, :].rearrange("p h a d -> p (h a d)").bitcast(F32),
                                                    env.ident[:])
                        last.then_inc(s_T, 1)

                def scores(g):
                    pe.wait_ge(s_Ta, 2 * g.n + 2)
                    pe.wait_ge(s_Tv, g.n + 1)
                    for u in range(4):
                        p, t = u // 2, u % 2
                        wait_from_one(pe, s_pTa if u % 2 == 0 else s_pTv,
                                      2 * g.n + u // 2 - 1 if not isinstance(g.n, int) or g.n else 0)
                        pe.matmul(bank[4 + u][:], qT[:, p, tokens(t)], kT[:, p].rearrange("p j n -> p (j n)"),
                                  start=True, stop=False, skip_group_check=True)
                        for part in (mask_hi, mask_lo):
                            row = part[:].rearrange("p t n -> p (t n)")[:, bass.ds(g.outer * (2 * S) + t * S, S)]
                            last = pe.matmul(bank[4 + u][:].rearrange("p (j n) -> p j n", j=2), ident_r[:],
                                             row.unsqueeze(1).broadcast_to([P, 2, S]), start=False,
                                             stop=part is mask_lo, skip_group_check=True)
                        last.then_inc(s_s, 1)

                def turn_probs(n):
                    for u in range(4):
                        pe.wait_ge(s_exp, 8 * n + 2 * u + 2)
                        for k in range(2):
                            for j in range(2):
                                last = pe.transpose(pT_bank(u)[:, k, j, :], prob[:, u, j, k * P:(k + 1) * P], env.ident[:])
                        last.then_inc(s_pT, 1)

                def attend(n):
                    pe.wait_ge(s_v, 2 * n + 2)
                    pe.wait_ge(s_done, 2 * n + 1)
                    for p in range(2):
                        pe.wait_ge(s_pTa, 2 * n + p + 1)
                        pe.wait_ge(s_pTv, 2 * n + p + 1)
                        for k in range(2):
                            last = pe.matmul(bank[2 + p][:], vp[:, k].rearrange("p h d -> p (h d)"),
                                             pT[:, k, 2 * p:2 * p + 2, :].rearrange("p h n -> p (h n)"),
                                             start=k == 0, stop=k == 1)
                        last.then_inc(s_o, 1)

                def turn_back(n):
                    pe.wait_ge(s_oc, 4 * n + 4)
                    for t in range(2):
                        last = pe.transpose(bank[2][:, t * P:(t + 1) * P], oT[:, tokens(t)], env.ident[:])
                    last.then_inc(s_oT, 1)

                def begin(first):
                    turn(0)
                    scores(first)
                    turn(1)
                    turn_probs(0)

                def step(cur, nxt, edge):
                    scores(nxt)
                    attend(cur.n)
                    turn(nxt.n + 1)
                    turn_probs(nxt.n)
                    turn_back(cur.n)

                def finish(last):
                    attend(last.n)
                    turn_back(last.n)

                pipelined(pe, B, NG0, begin, step, finish)

        with ExitStack() as fin:
            oquant = Quant(env, "qa_oq", fin, NT)
            oqT = env.sb("qa_oqT", [P, KD, TOK], BF16, fin)
            y = env.sb("qa_y", [P, NT, D], F32, fin)
            s_oTp, s_oT2, s_y, s_ys, s_add = (sem(n) for n in (
                "oqT_in_psum", "oqT_ready", "y_in_psum", "y_scaled", "residual_step"))
            block = fin.enter_context(nc.Block())

            @block.scalar
            def _(act):
                for n in range(2):
                    act.wait_ge(s_oTp, n + 1)
                    act.activation(oqT[:, :, n * 512:(n + 1) * 512],
                                   bank[n][:].bitcast(BF16).rearrange("p (k q) -> p k q", k=KD), ACT.Copy).then_inc(s_oT2, 1)

            @block.gpsimd
            def _(pool):
                pool.tensor_tensor(x[:], x[:], bias_rows[:, 3, :].unsqueeze(1).broadcast_to([P, NT, D]),
                                   ALU.add).then_inc(s_add, 1)

            @block.vector
            def _(dve):
                oquant.run(dve, o_tok[:])
                for t in range(NT):
                    dve.wait_ge(s_y, t // 2 * 2 + 2)
                    dve.scalar_tensor_tensor(y[:, t, :], half_banks(t), oquant.scale[:, t:t + 1], w_rows[:, 1, :],
                                             ALU.mult, ALU.mult).then_inc(s_ys, 1)
                dve.wait_ge(s_ys, NT)
                dve.wait_ge(s_add, 1)
                dve.tensor_tensor(x[:], x[:], y[:], ALU.add).then_inc(s_add, 1)
                dve.wait_ge(s_add, 2)

            @block.tensor
            def _(pe):
                pe.wait_ge(oquant.ready, 1)
                turn_rows(pe, oquant, s_oTp)
                for t in range(NT):
                    pe.wait_ge(s_oT2, t // 4 + 1)
                    for k in range(KD):
                        last = pe.matmul(half_banks(t), oqT[:, k, tokens(t)], wT[:, 1, k, :], start=k == 0, stop=k == KD - 1)
                    last.then_inc(s_y, 1)


GOLDEN_CENTER = 1.0 / math.e
GOLDEN_LOWER = 0.5 - math.log(4.0 / 3.0)
GOLDEN_UPPER = 0.5


I = 128
CH = 512
NC = TOK // CH
RW = 33


def experts(env, tag, layer):
    nc, dram, x = env.nc, env.dram, env.x
    E = 8 if layer == 0 else 32
    UNITS = 16 if layer == 0 else 33
    LOOPS = 7 if layer == 0 else 15
    weights = dram[f"{tag}_weights"]
    WCOLS = 2 * KD * I + D

    with ExitStack() as mem:
        sb = lambda n, s, d=F32: env.sb(f"{tag}_{n}", s, d, mem)
        sem = lambda n: env.sem(f"{tag}_{n}")
        rms_w = sb("rms_w", [P, D]) if layer else None
        norm = Norm(env, tag, mem, rms_w)
        h_hi, h_lo = sb("h_hi", [P, KD, TOK], F32R), sb("h_lo", [P, KD, TOK], F32R)
        wr = sb("wr", [P, KD, P])
        wr_hi, wr_lo = sb("wr_hi", [P, KD, P], F32R), sb("wr_lo", [P, KD, P], F32R)
        rt_bias = sb("rt_bias", [P, 32])
        logitT = sb("logitT", [32, TOK])
        sel = sb("sel", [3 * RW, RW * P], BF16)
        score = sb("score", [P, NT, 32])
        wfull = sb("wfull", [P, NT, RW])
        wpart = sb("wpart", [P, NT, 3, RW], BF16)
        wrest = sb("wrest", [P, NT, RW])
        wT = sb("wT", [3 * RW, TOK], BF16)
        stage = [sb(f"stage{j}", [P, WCOLS]) for j in range(2)]
        w_hi = [sb(f"w_hi{j}", [P, WCOLS], F32R) for j in range(2)]
        w_lo = [sb(f"w_lo{j}", [P, WCOLS], F32R) for j in range(2)]
        sg = sb("silu_gate", [P, CH])
        gu = sb("gate_up", [P, CH])
        act_f = sb("act_f", [P, CH])
        act_hi = [sb(f"act_hi{c}", [P, CH], F32R) for c in range(NC)]
        act_lo = [sb(f"act_lo{c}", [P, CH], F32R) for c in range(NC)]
        zero = sb("zero", [P, CH], BF16)
        total, no_expert = sb("total", [P, NT]), sb("no_expert", [P, NT])
        if layer == 0:
            dist, zone, rank = (sb(n, [P, NT, E]) for n in ("dist", "zone", "rank"))
            in_zone_w, fallback = sb("in_zone_w", [P, NT, E]), sb("fallback", [P, NT, E])
            pairs, before = sb("pairs", [P, NT, E, E]), sb("before", [P, E, E])
        else:
            best = sb("best", [P, NT, 8])

        s_const, s_wr, s_stage = sem("const_loaded"), sem("wr_split"), [sem(f"stage_loaded{j}") for j in range(2)]
        s_lg, s_lgc, s_lgt = sem("logitsT_in_psum"), sem("logitsT_copied"), sem("logits_in_psum")
        s_sc, s_step, s_z = sem("scores_ready"), sem("route_step"), sem("logits_scaled")
        s_dist, s_ex = sem("distance_ready"), sem("route_exps_ready")
        s_wpart, s_wTp, s_wT = sem("w_parts_ready"), sem("wT_in_psum"), sem("wT_ready")
        s_hi, s_lo = sem("unit_hi_ready"), sem("unit_lo_ready")
        s_gate, s_up, s_wb = sem("gate_in_psum"), sem("up_in_psum"), sem("w_rows_in_psum")
        s_sg, s_gu, s_act = sem("silu_ready"), sem("gate_up_ready"), sem("act_ready")
        s_ahi, s_alo = sem("act_hi_ready"), sem("act_lo_ready")
        s_down, s_zero, s_zd = sem("down_done"), sem("zero_ready"), sem("y_zeroed")
        s_add, s_twice = sem("residual_added"), sem("input_added_again")

        Y = env.bank[0:4]
        GATE, UP, WB, X7 = env.bank[4:8]
        gate_w = lambda w, k: w[:, k * I:(k + 1) * I]
        up_w = lambda w, k: w[:, (KD + k) * I:(KD + k + 1) * I]
        down_w = lambda w: w[:, 2 * KD * I:]
        block = mem.enter_context(nc.Block())

        @block.sync
        def _(sp):
            sp.dma_start(wr[:], dram[f"{tag}_wr"]).then_inc(s_const, 16)
            sp.dma_start(rt_bias[:], dram[f"{tag}_route"]).then_inc(s_const, 16)
            if layer:
                sp.dma_start(rms_w[:], dram["ln2_rows"]).then_inc(s_const, 16)
            else:
                sp.dma_start(before[:], dram["before"]).then_inc(s_const, 16)
            sp.dma_start(sel[:], dram["sel"]).then_inc(s_const, 16)
            for j in range(2):
                sp.dma_start(stage[j][:], weights[j]).then_inc(s_stage[j], 16)

            def load(u, j, it):
                sp.wait_ge(s_hi, 2 * it + j + 1)
                sp.wait_ge(s_lo, 2 * it + j + 1)
                sp.dma_start(stage[j][:], weights[u]).then_inc(s_stage[j], 16)

            with sp.Fori(0, (UNITS - 2) // 2) as it:
                for j in range(2):
                    load(2 * it + 2 + j, j, it)
            if UNITS % 2:
                load(UNITS - 1, 0, (UNITS - 3) // 2)

        n_const = 64

        @block.gpsimd
        def _(pool):
            if layer:
                pool.wait_ge(s_const, n_const)
            norm.gpsimd_rstd(pool)
            pool.wait_ge(s_wr, 1)
            pool.tensor_tensor(wr_lo[:], wr[:], wr_hi[:].bitcast(F32), ALU.subtract).then_inc(s_wr, 1)

            def lo_half(u, j, it):
                pool.wait_ge(s_hi, u + 1)
                if it is not None:
                    pool.wait_ge(s_down, 4 * it + 2 * j + 2)
                pool.tensor_tensor(w_lo[j][:], stage[j][:], w_hi[j][:].bitcast(F32),
                                   ALU.subtract).then_inc(s_lo, 1)

            for j in range(2):
                lo_half(j, j, None)
            with pool.Fori(0, (UNITS - 2) // 2) as it:
                for j in range(2):
                    lo_half(2 * it + 2 + j, j, it)
            if UNITS % 2:
                lo_half(UNITS - 1, 0, (UNITS - 3) // 2)

        @block.scalar
        def _(act):
            if layer:
                norm.scalar_stats(act)
            act.wait_ge(s_const, n_const)
            act.activation(wr_hi[:], wr[:], ACT.Copy).then_inc(s_wr, 1)

            def hi_half(u, j, it, n):
                act.wait_ge(s_stage[j], 16 * n)
                if it is not None:
                    act.wait_ge(s_down, 4 * it + 2 * j + 2)
                act.activation(w_hi[j][:], stage[j][:], ACT.Copy).then_inc(s_hi, 1)

            for j in range(2):
                hi_half(j, j, None, 1)
            norm.scalar_hi(act, [GATE, UP], h_hi)
            for c in range(NC):
                act.wait_ge(s_lg, c + 1)
                act.activation(logitT[:, c * CH:(c + 1) * CH], [WB, X7][c][0:32, :], ACT.Copy).then_inc(s_lgc, 1)
            if layer == 0:
                act.wait_ge(s_z, 1)
                act.activation(score[:, :, 0:E], score[:, :, 0:E], ACT.Sigmoid).then_inc(s_sc, 1)
                act.wait_ge(s_dist, 1)
                act.activation(in_zone_w[:], dist[:], ACT.Exp, scale=-1.0 / 0.1).then_inc(s_ex, 1)
                act.activation(fallback[:], dist[:], ACT.Exp, scale=-1.0 / 0.3).then_inc(s_ex, 1)
            else:
                act.wait_ge(s_lgt, 1)
                act.activation(score[:], env.bank[4][:, 0:NT * 32].rearrange("p (t e) -> p t e", e=32),
                               ACT.Sigmoid).then_inc(s_sc, 1)

            def unit(n):
                n, c = n
                act.wait_ge(s_gate, n + 1)
                wait_from_one(act, s_gu, n)
                act.activation(sg[:], GATE[:], ACT.Silu).then_inc(s_sg, 1)
                act.wait_ge(s_act, n + 1)
                act.activation(act_hi[c][:], act_f[:], ACT.Copy).then_inc(s_ahi, 1)

            run_units(act, unit, hi_half, LOOPS, UNITS)

        @block.vector
        def _(dve):
            if layer:
                dve.wait_ge(s_const, n_const)
            norm.vector_normalise(dve)
            norm.vector_lo(dve, [GATE, UP], h_hi, h_lo)
            dve.memset(zero[:], 0.0).then_inc(s_zero, 1)
            if layer:
                dve.tensor_tensor(x[:], x[:], env.x_in[:], ALU.add).then_inc(s_twice, 1)
            taken = [0]

            def link(ins):
                taken[0] += 1
                ins.then_inc(s_step, 1)
                dve.wait_ge(s_step, taken[0])

            row = lambda v, n: v.unsqueeze(2).broadcast_to([P, NT, n])
            if layer == 0:
                inh, e8 = score[:, :, 0:E], [P, NT, E, E]
                by_j = lambda v: v.unsqueeze(2).broadcast_to(e8)
                by_e = lambda v: v.unsqueeze(3).broadcast_to(e8)
                dve.wait_ge(s_const, n_const)
                link(dve.reciprocal(total[:, 0:1], rt_bias[:, 0:1]))
                dve.wait_ge(s_lgt, 1)
                dve.tensor_scalar(inh, GATE[:, 0:NT * 32].rearrange("p (t e) -> p t e", e=32)[:, :, 0:E],
                                  total[:, 0:1], None, ALU.mult).then_inc(s_z, 1)
                dve.wait_ge(s_sc, 1)
                link(dve.tensor_scalar(dist[:], inh, GOLDEN_CENTER, None, ALU.subtract))
                link(dve.scalar_tensor_tensor(dist[:], dist[:], -1.0, dist[:], ALU.mult, ALU.max))
                dve.tensor_scalar(zone[:], inh, GOLDEN_LOWER, None, ALU.is_ge).then_inc(s_dist, 1)
                dve.wait_ge(s_dist, 1)
                link(dve.scalar_tensor_tensor(zone[:], inh, GOLDEN_UPPER, zone[:], ALU.is_le, ALU.mult))
                dve.wait_ge(s_ex, 2)
                link(dve.tensor_tensor(in_zone_w[:], in_zone_w[:], zone[:], ALU.mult))
                link(dve.tensor_reduce(total[:], in_zone_w[:], AX_X, ALU.add))
                link(dve.tensor_scalar(no_expert[:], total[:], 1e-8, None, ALU.is_lt))
                link(dve.tensor_tensor(pairs[:], by_j(fallback[:]), by_e(fallback[:]), ALU.is_gt))
                link(dve.tensor_reduce(rank[:], pairs[:], AX_X, ALU.add))
                link(dve.tensor_tensor(pairs[:], by_j(fallback[:]), by_e(fallback[:]), ALU.is_equal))
                link(dve.tensor_tensor(pairs[:], pairs[:], before[:].unsqueeze(1).broadcast_to(e8), ALU.mult))
                link(dve.tensor_reduce(dist[:], pairs[:], AX_X, ALU.add))
                link(dve.tensor_tensor(rank[:], rank[:], dist[:], ALU.add))
                link(dve.scalar_tensor_tensor(fallback[:], rank[:], 1.5, fallback[:], ALU.is_lt, ALU.mult))
                link(dve.tensor_reduce(total[:], fallback[:], AX_X, ALU.add))
                link(dve.tensor_scalar(total[:], total[:], 1e-8, None, ALU.max))
                link(dve.reciprocal(total[:], total[:]))
                link(dve.tensor_tensor(total[:], total[:], no_expert[:], ALU.mult))
                link(dve.tensor_tensor(fallback[:], fallback[:], row(total[:], E), ALU.mult))
                link(dve.tensor_scalar(no_expert[:], no_expert[:], -1.0, 1.0, ALU.mult, ALU.add))
                link(dve.tensor_tensor(in_zone_w[:], in_zone_w[:], row(no_expert[:], E), ALU.mult))
                link(dve.tensor_tensor(in_zone_w[:], in_zone_w[:], fallback[:], ALU.add))
                link(dve.tensor_reduce(total[:], in_zone_w[:], AX_X, ALU.add))
                link(dve.tensor_scalar(total[:], total[:], 1e-8, None, ALU.max))
                link(dve.reciprocal(total[:], total[:]))
                link(dve.memset(wfull[:], 0.0))
                link(dve.tensor_tensor(wfull[:, :, 0:E], in_zone_w[:], row(total[:], E), ALU.mult))
            else:
                dve.wait_ge(s_sc, 1)
                link(dve.tensor_tensor(wrest[:, :, 0:E], score[:], rt_bias[:].unsqueeze(1).broadcast_to([P, NT, E]),
                                       ALU.add))
                for t in range(NT):
                    dve.max(best[:, t, :], wrest[:, t, 0:E]).then_inc(s_z, 1)
                dve.wait_ge(s_z, NT)
                for t in range(NT):
                    last = dve.match_replace(wfull[:, t, 0:E], best[:, t, :], wrest[:, t, 0:E], NEG)
                    last.then_inc(s_dist, 1)
                dve.wait_ge(s_dist, NT)
                link(dve.tensor_tensor(wrest[:, :, 0:E], wrest[:, :, 0:E], wfull[:, :, 0:E], ALU.not_equal))
                link(dve.tensor_tensor(score[:], score[:], wrest[:, :, 0:E], ALU.mult))
                link(dve.tensor_reduce(total[:], score[:], AX_X, ALU.add))
                link(dve.reciprocal(total[:], total[:]))
                link(dve.tensor_tensor(wfull[:, :, 0:E], score[:], row(total[:], E), ALU.mult))
                link(dve.memset(wfull[:, :, E:E + 1], 1.0))
            steps = [0]

            def step(ins):
                steps[0] += 1
                ins.then_inc(s_wpart, 1)
                dve.wait_ge(s_wpart, steps[0])

            step(dve.tensor_copy(wpart[:, :, 0, :], wfull[:]))
            step(dve.tensor_tensor(wrest[:], wfull[:], wpart[:, :, 0, :], ALU.subtract))
            step(dve.tensor_copy(wpart[:, :, 1, :], wrest[:]))
            step(dve.tensor_tensor(wfull[:], wrest[:], wpart[:, :, 1, :], ALU.subtract))
            step(dve.tensor_copy(wpart[:, :, 2, :], wfull[:]))
            for h in range(2):
                dve.wait_ge(s_wTp, h + 1)
                dve.tensor_copy(wT[:, h * CH:(h + 1) * CH],
                                [WB, X7][h][:].bitcast(BF16)[0:3 * RW, 0:CH]).then_inc(s_wT, 1)

            def unit(n):
                n, c = n
                dve.wait_ge(s_up, n + 1)
                dve.wait_ge(s_sg, n + 1)
                dve.tensor_tensor(gu[:], UP[:], sg[:], ALU.mult).then_inc(s_gu, 1)
                dve.wait_ge(s_wb, n + 1)
                dve.wait_ge(s_gu, n + 1)
                dve.tensor_tensor(act_f[:], WB[:], gu[:], ALU.mult).then_inc(s_act, 1)
                dve.wait_ge(s_ahi, n + 1)
                dve.tensor_tensor(act_lo[c][:], act_f[:], act_hi[c][:].bitcast(F32),
                                  ALU.subtract).then_inc(s_alo, 1)

            run_units(dve, unit, None, LOOPS, UNITS)
            if layer:
                dve.wait_ge(s_twice, 1)
            dve.wait_ge(s_down, NC * UNITS)
            for g in range(NT // 2):
                dve.tensor_tensor(x[:, 2 * g:2 * g + 2, :], Y[g][:].rearrange("p (t d) -> p t d", t=2),
                                  x[:, 2 * g:2 * g + 2, :], ALU.add).then_inc(s_add, 1)
            dve.wait_ge(s_add, NT // 2)

        @block.tensor
        def _(pe):
            norm.tensor_transpose(pe, [GATE, UP])
            pe.wait_ge(s_wr, 2)
            for c in range(NC):
                pe.wait_ge(norm.s_lo, 2 * c + 2)
                cols = slice(c * CH, (c + 1) * CH)
                for k in range(KD):
                    last = split3(pe, [WB, X7][c][:], (wr_hi[:, k, :], wr_lo[:, k, :]),
                                  (h_hi[:, k, cols], h_lo[:, k, cols]), k == 0, k == KD - 1)
                last.then_inc(s_lg, 1)
            pe.wait_ge(s_lgc, 2)
            pe.wait_ge(norm.s_lo, B)
            for t in range(NT):
                last = pe.transpose(GATE[:, t * 32:(t + 1) * 32], logitT[:, tokens(t)], env.ident[0:32, 0:32])
            last.then_inc(s_lgt, 1)
            pe.wait_ge(s_zero, 1)
            for g in range(NT // 2):
                last = pe.matmul(Y[g][:], zero[:, 0:P], zero[:], start=True, stop=True)
            last.then_inc(s_zd, 1)
            pe.wait_ge(s_wpart, 5)
            pe.wait_ge(s_lgc, 2)
            for h in range(2):
                for q in range(4):
                    t = 4 * h + q
                    last = pe.transpose([WB, X7][h][:].bitcast(BF16)[0:3 * RW, q * P:(q + 1) * P],
                                        wpart[:, t, :, :].rearrange("p a e -> p (a e)"), env.ident_bf[:])
                last.then_inc(s_wTp, 1)
            pe.wait_ge(s_wT, 2)
            pe.wait_ge(s_sc, 1)

            def up_part(u, c, j, n, e):
                cols = slice(c * CH, (c + 1) * CH)
                h = [(h_hi[:, k, cols], h_lo[:, k, cols]) for k in range(KD)]
                if c == 0:
                    pe.wait_ge(s_lo, u + 1)
                wait_from_one(pe, s_sg, n)
                for k in range(KD):
                    last = split3(pe, GATE[:], (gate_w(w_hi[j], k), gate_w(w_lo[j], k)), h[k], k == 0, k == KD - 1)
                last.then_inc(s_gate, 1)
                wait_from_one(pe, s_gu, n)
                for k in range(KD):
                    last = split3(pe, UP[:], (up_w(w_hi[j], k), up_w(w_lo[j], k)), h[k], k == 0, k == KD - 1)
                last.then_inc(s_up, 1)
                wait_from_one(pe, s_act, n)
                pe.matmul(WB[:], sel[:, bass.ds(e * P, P)], wT[:, cols], start=True, stop=True).then_inc(s_wb, 1)

            def down_part(c, j, n):
                pe.wait_ge(s_alo, n + 1)
                for q in range(CH // P):
                    t = c * (CH // P) + q
                    last = split3(pe, Y[t // 2][:, (t % 2) * D:(t % 2 + 1) * D],
                                  (act_hi[c][:, tokens(q)], act_lo[c][:, tokens(q)]),
                                  (down_w(w_hi[j]), down_w(w_lo[j])), False, False)
                last.then_inc(s_down, 1)

            of = (lambda it, j: it) if layer == 0 else (lambda it, j: 2 * it + j)
            up_part(0, 0, 0, 0, 0)
            with pe.Fori(0, LOOPS) as it:
                for j in range(2):
                    u = 2 * it + j
                    up_part(u, 1, j, 2 * u + 1, of(it, j))
                    down_part(0, j, 2 * u)
                    nxt = (of(it, 1) if j == 0 else of(it + 1, 0))
                    up_part(u + 1, 0, 1 - j, 2 * u + 2, nxt)
                    down_part(1, j, 2 * u + 1)
            for u in range(2 * LOOPS, UNITS):
                j = u % 2
                e = u // 2 if layer == 0 else u
                up_part(u, 1, j, 2 * u + 1, e)
                down_part(0, j, 2 * u)
                if u + 1 < UNITS:
                    up_part(u + 1, 0, 1 - j, 2 * u + 2, (u + 1) // 2 if layer == 0 else u + 1)
                down_part(1, j, 2 * u + 1)


def run_units(eng, unit, refill, loops, units):
    unit((0, 0))
    with eng.Fori(0, loops) as it:
        for j in range(2):
            n = 2 * (2 * it + j)
            unit((n + 1, 1))
            unit((n + 2, 0))
            if refill is not None:
                refill(2 * it + 2 + j, j, it, it + 2)
    for u in range(2 * loops, units):
        unit((2 * u + 1, 1))
        if u + 1 < units:
            unit((2 * u + 2, 0))
        if refill is not None and u + 2 < units:
            refill(u + 2, u % 2, u // 2, u // 2 + 2)
H1, HD1, RD = 16, 128, 64
QC, KVC = 96, 64
LOOKBACK = 8
HG = 4
NG = H1 // HG
FW = KVC + RD


def latent_attention(env):
    nc, dram, x = env.nc, env.dram, env.x
    with ExitStack() as mem:
        sb = lambda n, s, d=F32: env.sb(f"la_{n}", s, d, mem)
        sem = lambda n: env.sem(f"la_{n}")
        bank = env.bank
        keys = sb("keys", [P, NT, FW])
        kT_hi, kT_lo = sb("kT_hi", [P, TOK], F32R), sb("kT_lo", [P, TOK], F32R)
        vals = sb("vals", [P, NT, 2, KVC], F32R)
        qcT_hi, qcT_lo = sb("qcT_hi", [QC, TOK], F32R), sb("qcT_lo", [QC, TOK], F32R)
        wa_hi, wa_lo = sb("wa_hi", [QC, H1, FW], F32R), sb("wa_lo", [QC, H1, FW], F32R)
        c_hi, c_lo = sb("c_hi", [P, H1, D], F32R), sb("c_lo", [P, H1, D], F32R)
        bias = sb("bias", [P, NT, S], BF16)
        key_cos, key_sin = sb("key_cos", [P, 2, RD]), sb("key_sin", [P, 2, RD])
        s_in = sem("inputs_loaded")
        s_wdq, s_kvT, s_kvTc, s_key, s_keyc = (sem(n) for n in (
            "w_dq_split", "kv_cT_in_psum", "kv_cT_copied", "keys_in_psum", "keys_copied"))
        s_turn, s_kTp, s_kTh, s_kTl = (sem(n) for n in ("keys_turned", "kT_in_psum", "kT_hi_ready", "kT_lo_ready"))
        s_val, s_qcp, s_qch, s_qcl = (sem(n) for n in ("vals_ready", "q_cT_in_psum", "q_cT_hi_ready", "q_cT_lo_ready"))
        s_wap, s_wah, s_wal, s_qrh, s_qrl = (sem(n) for n in (
            "a_in_psum", "a_hi_ready", "a_lo_ready", "qr_hi_ready", "qr_lo_ready"))
        s_cp, s_ch, s_cl = sem("c_in_psum"), sem("c_hi_ready"), sem("c_lo_ready")
        s_bias = sem("bias_step")
        s_qslot, s_vslot = sem("batch_queries_ready"), sem("batch_values_ready")
        s_q, s_qc, s_rot, s_roped = sem("q_in_psum"), sem("q_copied"), sem("q_rotated"), sem("q_roped")
        s_qT, s_qTh, s_qTl = sem("qT_in_psum"), sem("qT_hi_ready"), sem("qT_lo_ready")
        s_s, s_max, s_exp, s_inv, s_prob = (sem(n) for n in (
            "scores_in_psum", "max_ready", "exp_ready", "row_inverse_ready", "prob_ready"))
        s_pT, s_pTh, s_pTl = sem("pT_in_psum"), sem("pT_hi_ready"), sem("pT_lo_ready")
        s_o, s_oh, s_ol = sem("oT_in_psum"), sem("oT_hi_ready"), sem("oT_lo_ready")
        s_y, s_add = sem("y_in_psum"), sem("residual_added")
        half = RD // 2
        SCALE = 1.0 / math.sqrt(HD1 + RD)
        with ExitStack() as prep:
            sb = lambda n, s, d=F32: env.sb(f"la_{n}", s, d, prep)
            norm = Norm(env, "la", prep)
            ctxT = sb("ctxT", [P, KD, TOK])
            w_kvc, w_dq = sb("w_kvc", [P, KD, KVC]), sb("w_dq", [P, KD, P])
            w_dq_hi, w_dq_lo = sb("w_dq_hi", [P, KD, P], F32R), sb("w_dq_lo", [P, KD, P], F32R)
            uqT, ukT = sb("uqT", [P, H1, QC]), sb("ukT", [P, H1, KVC])
            uvT2, wo = sb("uvT2", [P, H1, 2 * KVC]), sb("wo", [P, H1, D])
            qr = sb("qr", [QC, H1, RD])
            key_w = sb("key_w", [KVC, FW])
            kvcT = sb("kvcT", [KVC, TOK])
            turn_a, turn_b = sb("turn_a", [P, NT, RD]), sb("turn_b", [P, NT, RD])
            h_hi, h_lo = sb("h_hi", [P, KD, TOK], F32R), sb("h_lo", [P, KD, TOK], F32R)
            seg_i, seg, seg_low = sb("seg_i", [P, NT], I32), sb("seg", [P, NT]), sb("seg_low", [P, NT])
            key_id = sb("key_id", [P, S])
            not_after, good = sb("not_after", [P, NT, S], BF16), sb("good", [P, NT, S], BF16)
            credit = sb("credit", [P, 1])
            loads = [(ctxT, "ctxT"), (w_kvc, "w_kvc"), (w_dq, "w_dq"), (uqT, "uqT"), (ukT, "ukT"), (uvT2, "uvT2"),
                     (wo, "la_wo"), (qr, "qr"), (key_w, "key_w"), (key_cos, "la_cos"), (key_sin, "la_sin"),
                     (seg_i, "seg"), (key_id, "key_id")]
            n_in = 16 * len(loads)
            kvT_bank = [bank[2], bank[3]]
            block = prep.enter_context(nc.Block())

            @block.sync
            def _(sp):
                for dst, name in loads:
                    sp.dma_start(dst[:], dram[name]).then_inc(s_in, 16)

            @block.gpsimd
            def _(pool):
                norm.gpsimd_rstd(pool)
                pool.wait_ge(s_wdq, 1)
                pool.tensor_tensor(w_dq_lo[:], w_dq[:], w_dq_hi[:].bitcast(F32), ALU.subtract).then_inc(s_wdq, 1)
                pool.wait_ge(s_turn, 2)
                pool.tensor_tensor(keys[:, :, KVC:], turn_a[:], turn_b[:], ALU.add).then_inc(s_turn, 1)

                pool.wait_ge(s_qcl, 2)
                pool.wait_ge(s_val, 2)

            @block.scalar
            def _(act):
                act.wait_ge(s_in, n_in)
                act.activation(w_dq_hi[:], w_dq[:], ACT.Copy).then_inc(s_wdq, 1)
                act.activation(wa_hi[:, :, KVC:], qr[:], ACT.Copy, scale=SCALE).then_inc(s_qrh, 1)
                for c in range(2):
                    act.wait_ge(s_kvT, c + 1)
                    act.activation(kvcT[:, c * 512:(c + 1) * 512], kvT_bank[c][0:KVC, :], ACT.Copy).then_inc(s_kvTc, 1)
                for n in range(2):
                    act.wait_ge(s_key, n + 1)
                    act.activation(keys[:, 4 * n:4 * n + 4, :], bank[4 + n][:].rearrange("p (t f) -> p t f", t=4),
                                   ACT.Copy).then_inc(s_keyc, 1)
                act.wait_ge(s_keyc, 2)
                act.activation(vals[:, :, 0, :], keys[:, :, 0:KVC], ACT.Copy).then_inc(s_val, 1)
                for n in range(4):
                    act.wait_ge(s_wap, n + 1)
                    act.activation(wa_hi[:, 4 * n:4 * n + 4, 0:KVC],
                                   bank[6 + n % 2][0:QC, 0:4 * KVC].rearrange("p (h c) -> p h c", h=4),
                                   ACT.Copy, scale=SCALE).then_inc(s_wah, 1)
                for n in range(8):
                    act.wait_ge(s_cp, n + 1)
                    act.activation(c_hi[:, 2 * n:2 * n + 2, :], bank[6 + n % 2][:].rearrange("p (h d) -> p h d", h=2),
                                   ACT.Copy).then_inc(s_ch, 1)
                norm.scalar_hi(act, bank[0:2], h_hi)
                for n in range(2):
                    act.wait_ge(s_kTp, n + 1)
                    act.activation(kT_hi[:, n * 512:(n + 1) * 512], bank[4 + n][:], ACT.Copy).then_inc(s_kTh, 1)
                for c in range(2):
                    act.wait_ge(s_qcp, c + 1)
                    act.activation(qcT_hi[:, c * 512:(c + 1) * 512], bank[2 + c][0:QC, :], ACT.Copy).then_inc(s_qch, 1)

            @block.vector
            def _(dve):
                norm.vector_normalise(dve)
                dve.wait_ge(s_in, n_in)
                steps = [0]

                def link(ins):
                    steps[0] += 1
                    ins.then_inc(s_bias, 1)
                    dve.wait_ge(s_bias, steps[0])

                link(dve.tensor_copy(seg[:], seg_i[:]))
                link(dve.tensor_scalar(seg_low[:], seg[:], float(-LOOKBACK), None, ALU.add))
                for t in range(NT):
                    last = dve.tensor_scalar(not_after[:, t, :], key_id[:], seg[:, t:t + 1], None, ALU.is_le)
                    last.then_inc(s_bias, 1)
                dve.wait_ge(s_bias, 2 + NT)
                for t in range(NT):
                    dve.scalar_tensor_tensor(good[:, t, :], key_id[:], seg_low[:, t:t + 1], not_after[:, t, :],
                                             ALU.is_ge, ALU.mult).then_inc(s_bias, 1)
                dve.wait_ge(s_bias, 2 + 2 * NT)
                dve.tensor_scalar(bias[:], good[:], -1.0, -NEG, ALU.add, ALU.mult).then_inc(s_bias, 1)
                dve.wait_ge(s_keyc, 2)
                k4 = keys[:].rearrange("p (b t) f -> p b t f", t=2)
                a4, b4 = turn_a[:].rearrange("p (b t) f -> p b t f", t=2), turn_b[:].rearrange("p (b t) f -> p b t f", t=2)
                for t in range(2):
                    cs = lambda v, lo, n: v[:, t, lo:lo + n].unsqueeze(1).broadcast_to([P, B, n])
                    last = dve.tensor_tensor(a4[:, :, t, :], k4[:, :, t, KVC:], cs(key_cos, 0, RD), ALU.mult)
                    dve.tensor_tensor(b4[:, :, t, 0:half], k4[:, :, t, KVC + half:], cs(key_sin, 0, half), ALU.mult)
                    last = dve.tensor_tensor(b4[:, :, t, half:], k4[:, :, t, KVC:KVC + half], cs(key_sin, half, half), ALU.mult)
                    last.then_inc(s_turn, 1)
                dve.wait_ge(s_val, 1)
                dve.tensor_tensor(vals[:, :, 1, :], keys[:, :, 0:KVC], vals[:, :, 0, :].bitcast(F32),
                                  ALU.subtract).then_inc(s_val, 1)
                dve.wait_ge(s_qrh, 1)
                dve.scalar_tensor_tensor(wa_lo[:, :, KVC:], qr[:], SCALE, wa_hi[:, :, KVC:].bitcast(F32),
                                         ALU.mult, ALU.subtract).then_inc(s_qrl, 1)
                for n in range(4):
                    dve.wait_ge(s_wah, n + 1)
                    dve.scalar_tensor_tensor(wa_lo[:, 4 * n:4 * n + 4, 0:KVC],
                                             bank[6 + n % 2][0:QC, 0:4 * KVC].rearrange("p (h c) -> p h c", h=4), SCALE,
                                             wa_hi[:, 4 * n:4 * n + 4, 0:KVC].bitcast(F32),
                                             ALU.mult, ALU.subtract).then_inc(s_wal, 1)
                for n in range(8):
                    dve.wait_ge(s_ch, n + 1)
                    dve.tensor_tensor(c_lo[:, 2 * n:2 * n + 2, :], bank[6 + n % 2][:].rearrange("p (h d) -> p h d", h=2),
                                      c_hi[:, 2 * n:2 * n + 2, :].bitcast(F32), ALU.subtract).then_inc(s_cl, 1)
                norm.vector_lo(dve, bank[0:2], h_hi, h_lo)
                for n in range(2):
                    dve.wait_ge(s_kTh, n + 1)
                    cols = slice(n * 512, (n + 1) * 512)
                    dve.tensor_tensor(kT_lo[:, cols], bank[4 + n][:], kT_hi[:, cols].bitcast(F32),
                                      ALU.subtract).then_inc(s_kTl, 1)
                for c in range(2):
                    dve.wait_ge(s_qch, c + 1)
                    cols = slice(c * 512, (c + 1) * 512)
                    dve.tensor_tensor(qcT_lo[:, cols], bank[2 + c][0:QC, :], qcT_hi[:, cols].bitcast(F32),
                                      ALU.subtract).then_inc(s_qcl, 1)

                dve.memset(credit[:], 0.0).then_inc(s_add, 1)

            @block.tensor
            def _(pe):
                pe.wait_ge(s_in, n_in)
                for c in range(2):
                    for k in range(KD):
                        last = pe.matmul(kvT_bank[c][0:KVC, :], w_kvc[:, k, :], ctxT[:, k, c * 512:(c + 1) * 512],
                                         start=k == 0, stop=k == KD - 1)
                    last.then_inc(s_kvT, 1)
                pe.wait_ge(s_kvTc, 2)
                for t in range(NT):
                    last = pe.matmul(bank[4 + t // 4][:, (t % 4) * FW:(t % 4 + 1) * FW], kvcT[:, tokens(t)], key_w[:],
                                     start=True, stop=True)
                    if t % 4 == 3:
                        last.then_inc(s_key, 1)
                for n in range(4):
                    if n >= 2:
                        pe.wait_ge(s_wal, n - 1)
                    for j in range(4):
                        h = 4 * n + j
                        last = pe.matmul(bank[6 + n % 2][0:QC, j * KVC:(j + 1) * KVC], uqT[:, h, :], ukT[:, h, :],
                                         start=True, stop=True)
                    last.then_inc(s_wap, 1)
                for n in range(8):
                    pe.wait_ge(s_wal, min(4, 3 + n))
                    if n >= 2:
                        pe.wait_ge(s_cl, n - 1)
                    for j in range(2):
                        h = 2 * n + j
                        last = pe.matmul(bank[6 + n % 2][:, j * D:(j + 1) * D], uvT2[:, h, :], wo[:, h, :],
                                         start=True, stop=True)
                    last.then_inc(s_cp, 1)
                norm.tensor_transpose(pe, bank[0:2])
                pe.wait_ge(s_turn, 3)
                for n in range(2):
                    for j in range(4):
                        last = pe.transpose(bank[4 + n][:, j * P:(j + 1) * P], keys[:, 4 * n + j, :], env.ident[:])
                    last.then_inc(s_kTp, 1)
                pe.wait_ge(s_wdq, 2)
                for c in range(2):
                    pe.wait_ge(norm.s_lo, 2 * c + 2)
                    cols = slice(c * 512, (c + 1) * 512)
                    for k in range(KD):
                        last = split3(pe, bank[2 + c][:], (w_dq_hi[:, k, :], w_dq_lo[:, k, :]),
                                      (h_hi[:, k, cols], h_lo[:, k, cols]), k == 0, k == KD - 1)
                    last.then_inc(s_qcp, 1)
                pe.wait_ge(s_cl, 8)
                pe.wait_ge(s_qrl, 1)
                pe.wait_ge(s_kTl, 2)
                pe.wait_ge(s_qcl, 2)
                pe.wait_ge(s_bias, 3 + 2 * NT)

        sb = lambda n, s, d=F32: env.sb(f"la_{n}", s, d, mem)
        qs_hi, qs_lo = sb("qs_hi", [QC, S], F32R), sb("qs_lo", [QC, S], F32R)
        vs = sb("vs", [P, 2, 2 * KVC], F32R)
        q = sb("q", [P, 2, HG, FW])
        rot_a, rot_b = sb("rot_a", [P, 2, HG, RD]), sb("rot_b", [P, 2, HG, RD])
        qT_hi, qT_lo = sb("qT_hi", [P, 2, HG, P], F32R), sb("qT_lo", [P, 2, HG, P], F32R)
        prob = sb("prob", [P, 4, 2, S])
        nmax, rsum, rinv = sb("nmax", [P, 4, 2]), sb("rsum", [P, 4, 2]), sb("rinv", [P, 4, 2])
        pT_hi, pT_lo = sb("pT_hi", [P, 2, HG, S], F32R), sb("pT_lo", [P, 2, HG, S], F32R)
        oT_hi, oT_lo = sb("oT_hi", [P, HG, S], F32R), sb("oT_lo", [P, HG, S], F32R)

        block = mem.enter_context(nc.Block())

        TURNED = (bank[3], bank[2], bank[4], bank[5])
        Y = bank[2]
        pT_bank = lambda u: TURNED[u][:].rearrange("p (k j n) -> p k j n", k=2, j=2)
        heads = lambda tile: tile[:].rearrange("p (h n) -> p h n", h=HG)
        oT_bank = lambda p: bank[6 + p][:].rearrange("p (h n) -> p h n", h=2)

        def pT_view(t, u):
            h, p = u // 2, u % 2
            return t[:, :, 2 * p:2 * p + 2, h * P:(h + 1) * P]

        @block.gpsimd
        def _(pool):
            def group(n):
                for t in range(2):
                    pool.wait_ge(s_rot, 6 * n + 3 * t + 3)
                    pool.tensor_tensor(q[:, t, :, KVC:], rot_a[:, t], rot_b[:, t], ALU.add).then_inc(s_roped, 1)
                for u in range(4):
                    pool.wait_ge(s_inv, 4 * n + u + 1)
                    pool.tensor_tensor(prob[:, u], prob[:, u], rinv[:, u, :].unsqueeze(2).broadcast_to([P, 2, S]),
                                       ALU.mult).then_inc(s_prob, 1)

            group(0)
            with pool.Fori(0, B * NG - 1) as n:
                group(n + 1)

        @block.scalar
        def _(act):
            def q_copies(n):
                for t in range(2):
                    act.wait_ge(s_q, 2 * n + t + 1)
                    act.activation(q[:, t], bank[t][:].rearrange("p (h f) -> p h f", h=HG), ACT.Copy).then_inc(s_qc, 1)

            def q_high(n):
                for t in range(2):
                    act.wait_ge(s_qT, 2 * n + t + 1)
                    act.activation(qT_hi[:, t], heads(bank[t]), ACT.Copy).then_inc(s_qTh, 1)

            def exps(n):
                for u in range(4):
                    act.wait_ge(s_max, 4 * n + u + 1)
                    for j in range(2):
                        act.activation(prob[:, u, j, :], bank[4 + u][:, j * S:(j + 1) * S], ACT.Exp,
                                       bias=nmax[:, u, j:j + 1], accum_out=rsum[:, u, j:j + 1]).then_inc(s_exp, 1)

            def pT_high(n):
                for u in range(4):
                    act.wait_ge(s_pT, 4 * n + u + 1)
                    act.activation(pT_view(pT_hi, u), pT_bank(u), ACT.Copy).then_inc(s_pTh, 1)

            def outputs_high(n):
                for p in range(2):
                    act.wait_ge(s_o, 2 * n + p + 1)
                    act.activation(oT_hi[:, 2 * p:2 * p + 2, :], oT_bank(p), ACT.Copy).then_inc(s_oh, 1)

            def begin(first):
                q_copies(0)
                q_high(0)
                exps(0)

            def step(cur, nxt, edge):
                pT_high(cur.n)
                q_copies(nxt.n)
                outputs_high(cur.n)
                q_high(nxt.n)
                exps(nxt.n)

            def finish(last):
                pT_high(last.n)
                outputs_high(last.n)

            pipelined(act, B, NG, begin, step, finish)

        @block.vector
        def _(dve):
            def query_slot(n, b):
                wait_from_one(dve, s_q, 2 * n)
                dve.tensor_copy(qs_hi[:], qcT_hi[:, bass.ts(b, S)]).then_inc(s_qslot, 1)
                dve.tensor_copy(qs_lo[:], qcT_lo[:, bass.ts(b, S)]).then_inc(s_qslot, 1)

            def value_slot(n, b):
                wait_from_one(dve, s_o, 2 * n)
                dve.tensor_copy(vs[:], vals[:, bass.ds(2 * b, 2), :, :].rearrange("p t a c -> p t (a c)")
                                ).then_inc(s_vslot, 1)

            def rotate(n):
                for t in range(2):
                    dve.wait_ge(s_qc, 2 * n + t + 1)
                    cs = lambda v, lo, w: v[:, t, lo:lo + w].unsqueeze(1).broadcast_to([P, HG, w])
                    dve.tensor_tensor(rot_a[:, t], q[:, t, :, KVC:], cs(key_cos, 0, RD), ALU.mult).then_inc(s_rot, 1)
                    dve.tensor_tensor(rot_b[:, t, :, 0:half], q[:, t, :, KVC + half:], cs(key_sin, 0, half),
                                      ALU.mult).then_inc(s_rot, 1)
                    dve.tensor_tensor(rot_b[:, t, :, half:], q[:, t, :, KVC:KVC + half], cs(key_sin, half, half),
                                      ALU.mult).then_inc(s_rot, 1)

            def q_low(n):
                for t in range(2):
                    dve.wait_ge(s_qTh, 2 * n + t + 1)
                    dve.tensor_tensor(qT_lo[:, t], heads(bank[t]), qT_hi[:, t].bitcast(F32),
                                      ALU.subtract).then_inc(s_qTl, 1)

            def maxima(n):
                def inverse(u):
                    dve.wait_ge(s_exp, 8 * n + 2 * u + 2)
                    dve.reciprocal(rinv[:, u, :], rsum[:, u, :]).then_inc(s_inv, 1)

                for u in range(4):
                    dve.wait_ge(s_s, 4 * n + u + 1)
                    dve.tensor_reduce(nmax[:, u, :], bank[4 + u][:].rearrange("p (j n) -> p j n", j=2), AX_X,
                                      ALU.max, negate=True).then_inc(s_max, 1)
                    if u >= 2:
                        inverse(u - 2)
                inverse(2)
                inverse(3)

            def pT_low(n):
                for u in range(4):
                    dve.wait_ge(s_pTh, 4 * n + u + 1)
                    dve.tensor_tensor(pT_view(pT_lo, u), pT_bank(u), pT_view(pT_hi, u).bitcast(F32),
                                      ALU.subtract).then_inc(s_pTl, 1)

            def outputs_low(n):
                for p in range(2):
                    dve.wait_ge(s_oh, 2 * n + p + 1)
                    dve.tensor_tensor(oT_lo[:, 2 * p:2 * p + 2, :], oT_bank(p), oT_hi[:, 2 * p:2 * p + 2, :].bitcast(F32),
                                      ALU.subtract).then_inc(s_ol, 1)

            def residual(n, b):
                dve.wait_ge(s_y, n + 1)
                rows2 = x[:, bass.ds(2 * b, 2), :]
                dve.tensor_tensor(rows2, Y[:].rearrange("p (t d) -> p t d", t=2), rows2, ALU.add).then_inc(s_add, 1)

            def begin(first):
                query_slot(0, 0)
                value_slot(0, 0)
                rotate(0)
                q_low(0)
                maxima(0)

            def step(cur, nxt, edge):
                if edge:
                    query_slot(nxt.n, nxt.outer)
                pT_low(cur.n)
                rotate(nxt.n)
                outputs_low(cur.n)
                if edge:
                    value_slot(nxt.n, nxt.outer)
                q_low(nxt.n)
                maxima(nxt.n)
                residual(cur.n, cur.outer)

            def finish(last):
                pT_low(last.n)
                outputs_low(last.n)
                residual(last.n, last.outer)

            pipelined(dve, B, NG, begin, step, finish)
            dve.wait_ge(s_add, B * NG + 1)

        @block.tensor
        def _(pe):
            def project(g):
                pe.wait_ge(s_qslot, 2 * g.outer + 2)
                for t in range(2):
                    last = split3(pe, bank[t][:], (qs_hi[:, tokens(t)], qs_lo[:, tokens(t)]),
                                  (wa_hi[:].rearrange("p h f -> p (h f)")[:, bass.ts(g.inner, 512)],
                                   wa_lo[:].rearrange("p h f -> p (h f)")[:, bass.ts(g.inner, 512)]), True, True)
                    last.then_inc(s_q, 1)

            def turn_q(n):
                for t in range(2):
                    pe.wait_ge(s_roped, 2 * n + t + 1)
                    for h in range(HG):
                        last = pe.transpose(bank[t][:, h * P:(h + 1) * P], q[:, t, h, :], env.ident[:])
                    last.then_inc(s_qT, 1)

            def scores(g):
                cols = bass.ts(g.outer, S)
                for u in range(4):
                    t, p = u // 2, u % 2
                    if u == 2:
                        wait_from_one(pe, s_ol, 2 * g.n)
                    pe.wait_ge(s_qTl, 2 * g.n + t + 1)
                    for j in range(2):
                        h = 2 * p + j
                        out = bank[4 + u][:, j * S:(j + 1) * S]
                        split3(pe, out, (qT_hi[:, t, h, :], qT_lo[:, t, h, :]), (kT_hi[:, cols], kT_lo[:, cols]),
                               True, False)
                        last = pe.matmul(out, env.ident_bf[:],
                                         bias[:].rearrange("p t n -> p (t n)")[:, bass.ds(g.outer * 2 * S + t * S, S)],
                                         start=False, stop=True, skip_group_check=True)
                    last.then_inc(s_s, 1)

            def turn_probs(n):
                for u in range(4):
                    pe.wait_ge(s_prob, 4 * n + u + 1)
                    if TURNED[u] is Y:
                        pe.wait_ge(s_add, n + 1)
                    for k in range(2):
                        for j in range(2):
                            last = pe.transpose(pT_bank(u)[:, k, j, :], prob[:, u, j, k * P:(k + 1) * P], env.ident[:])
                    last.then_inc(s_pT, 1)

            def attend(g):
                pe.wait_ge(s_vslot, g.outer + 1)
                for p in range(2):
                    pe.wait_ge(s_pTl, 4 * g.n + 3 + p)
                    for k in range(2):
                        for part in (pT_hi, pT_lo):
                            last = pe.matmul(bank[6 + p][:], vs[:, k, :],
                                             part[:, k, 2 * p:2 * p + 2, :].rearrange("p h n -> p (h n)"),
                                             start=k == 0 and part is pT_hi, stop=k == 1 and part is pT_lo)
                    last.then_inc(s_o, 1)

            def output(g):
                pe.wait_ge(s_ol, 2 * g.n + 2)
                for t in range(2):
                    for h in range(HG):
                        head = bass.ds(g.inner * HG * D + h * D, D)
                        last = split3(pe, Y[:, t * D:(t + 1) * D], (oT_hi[:, h, tokens(t)], oT_lo[:, h, tokens(t)]),
                                      (c_hi[:].rearrange("p h d -> p (h d)")[:, head],
                                       c_lo[:].rearrange("p h d -> p (h d)")[:, head]), h == 0, h == HG - 1)
                last.then_inc(s_y, 1)

            def begin(first):
                project(first)
                turn_q(0)
                scores(first)

            def step(cur, nxt, edge):
                turn_probs(cur.n)
                project(nxt)
                attend(cur)
                turn_q(nxt.n)
                scores(nxt)
                output(cur)

            def finish(last):
                turn_probs(last.n)
                attend(last)
                output(last)

            pipelined(pe, B, NG, begin, step, finish)
NKV, REP, HD = 4, 8, 128
QKV = (REP + 2) * HD
NR = REP + 1


TURNS = [(), (0, 1), (2, 3), (4, 5), (6,), (7,)]


def grouped_attention(env):
    nc, dram, x = env.nc, env.dram, env.x
    SCALE = 1.0 / math.sqrt(HD)
    half = HD // 2
    bank = env.bank
    with ExitStack() as mem:
        sb = lambda n, s, d=F32: env.sb(f"ga_{n}", s, d, mem)
        sem = lambda n: env.sem(f"ga_{n}")
        h_hi, h_lo = sb("h_hi", [P, KD, TOK + S], F32R), sb("h_lo", [P, KD, TOK + S], F32R)
        with ExitStack() as prep:
            rms_w = env.sb("ga_rms_w", [P, D], F32, prep)
            layer_norm = Norm(env, "ga_ln", prep, dst=x)
            norm = Norm(env, "ga", prep, rms_w)
            s_w, s_keep = sem("norm_weight_loaded"), sem("input_kept")
            s_hi_again, s_lo_again = sem("first_batch_hi_again"), sem("first_batch_lo_again")
            block = prep.enter_context(nc.Block())

            @block.sync
            def _(sp):
                sp.dma_start(rms_w[:], dram["ln1_rows"]).then_inc(s_w, 16)

            @block.gpsimd
            def _(pool):
                pool.tensor_copy(env.x_in[:], x[:]).then_inc(s_keep, 1)
                layer_norm.gpsimd_rstd(pool)
                norm.gpsimd_rstd(pool)

            @block.scalar
            def _(act):
                act.wait_ge(layer_norm.s_xn, NT)
                norm.scalar_stats(act)
                norm.scalar_hi(act, bank[0:2], h_hi)
                act.wait_ge(norm.s_hi, 1)
                act.activation(h_hi[:, :, TOK:], h_hi[:, :, 0:S].bitcast(F32), ACT.Copy).then_inc(s_hi_again, 1)
                act.wait_ge(s_hi_again, 1)

            @block.vector
            def _(dve):
                layer_norm.vector_normalise(dve, s_keep)
                dve.wait_ge(s_w, 16)
                norm.vector_normalise(dve)
                norm.vector_lo(dve, bank[0:2], h_hi, h_lo)
                dve.wait_ge(norm.s_lo, B)
                dve.tensor_copy(h_lo[:, :, TOK:], h_lo[:, :, 0:S]).then_inc(s_lo_again, 1)
                dve.wait_ge(s_lo_again, 1)

            @block.tensor
            def _(pe):
                norm.tensor_transpose(pe, bank[0:2])

        cos, sin = sb("cos", [P, 2, HD]), sb("sin", [P, 2, HD])
        causal = sb("causal", [P, P], BF16)
        stage_w, stage_wo = sb("stage_w", [P, KD, QKV]), sb("stage_wo", [P, REP, D])
        w_hi, w_lo = sb("w_hi", [P, KD, QKV], F32R), sb("w_lo", [P, KD, QKV], F32R)
        wo_hi, wo_lo = sb("wo_hi", [P, REP, D], F32R), sb("wo_lo", [P, REP, D], F32R)
        hs_hi, hs_lo = sb("hs_hi", [P, KD, S], F32R), sb("hs_lo", [P, KD, S], F32R)
        qkv = sb("qkv", [P, 2, QKV])
        val = sb("val", [P, 2, HD])
        rot = sb("rot", [P, NR, HD])
        roped = sb("roped", [P, 2, NR, HD])
        T_hi, T_lo = sb("T_hi", [P, NR, S], F32R), sb("T_lo", [P, NR, S], F32R)
        prob = sb("prob", [P, REP, P + S])
        nmax, rsum, rinv = sb("nmax", [P, REP, 2]), sb("rsum", [P, REP, 2]), sb("rinv", [P, REP, 2])
        pT = sb("pT", [P, REP, S + P])
        oT_hi, oT_lo = sb("oT_hi", [P, REP, S], F32R), sb("oT_lo", [P, REP, S], F32R)

        s_const, s_stage, s_stwo = sem("constants_loaded"), sem("w_loaded"), sem("wo_loaded")
        s_whi, s_wlo = sem("w_hi_ready"), sem("w_lo_ready")
        s_wohi, s_wolo = sem("wo_hi_ready"), sem("wo_lo_ready")
        s_hs = sem("batch_slot_ready")
        s_q, s_qc, s_rot, s_rope = sem("qkv_in_psum"), sem("qkv_copied"), sem("qkv_rotated"), sem("qkv_roped")
        s_val, s_prot = sem("values_ready"), sem("qkv_upper_rotated")
        s_T, s_Th, s_Tl = sem("T_in_psum"), sem("T_hi_ready"), sem("T_lo_ready")
        s_s, s_max, s_exp, s_inv, s_prob = (sem(n) for n in (
            "scores_in_psum", "max_ready", "exp_ready", "row_inverse_ready", "prob_ready"))
        s_pT, s_pTc = sem("pT_in_psum"), sem("pT_copied")
        s_o, s_oh, s_ol = sem("oT_in_psum"), sem("oT_hi_ready"), sem("oT_lo_ready")
        s_y, s_add = sem("y_in_psum"), sem("residual_added")
        CHUNKS = [(1024, 256), (0, 512), (512, 512)]
        NCH = len(CHUNKS)
        TILE_COLS = ((0, slice(0, P)), (1, slice(P, P + S)))
        Y = bank[7]
        block = mem.enter_context(nc.Block())

        @block.sync
        def _(sp):
            for dst, name in ((cos, "ga_cos"), (sin, "ga_sin"), (causal, "causal")):
                sp.dma_start(dst[:], dram[name]).then_inc(s_const, 16)
            sp.dma_start(stage_w[:], dram["ga_w"][0]).then_inc(s_stage, 16)
            sp.dma_start(stage_wo[:], dram["ga_wo"][0]).then_inc(s_stwo, 16)
            with sp.Fori(0, NKV - 1) as g:
                sp.wait_ge(s_whi, NCH * g + NCH)
                sp.wait_ge(s_wlo, NCH * g + NCH)
                sp.dma_start(stage_w[:], dram["ga_w"][g + 1]).then_inc(s_stage, 16)
                sp.wait_ge(s_wohi, g + 1)
                sp.wait_ge(s_wolo, g + 1)
                sp.dma_start(stage_wo[:], dram["ga_wo"][g + 1]).then_inc(s_stwo, 16)

        @block.gpsimd
        def _(pool):
            def wo_low(g):
                pool.wait_ge(s_wohi, g + 1)
                pool.tensor_tensor(wo_lo[:], stage_wo[:], wo_hi[:].bitcast(F32), ALU.subtract).then_inc(s_wolo, 1)

            def normalise(n):
                for h in range(REP):
                    pool.wait_ge(s_inv, REP * n + h + 1)
                    for t, cols in TILE_COLS:
                        pool.tensor_tensor(prob[:, h, cols], prob[:, h, cols],
                                           rinv[:, h, t:t + 1].broadcast_to([P, cols.stop - cols.start]),
                                           ALU.mult).then_inc(s_prob, 1)

            def rotate(n):
                for t in range(2):
                    pool.wait_ge(s_qc, 2 * NCH * n + NCH * t + NCH)
                    if t or not isinstance(n, int):
                        pool.wait_ge(s_rope, 2 * n + t)
                    pool.tensor_tensor(rot[:, :, half:], qkv[:, t, 0:NR * HD].rearrange("p (h f) -> p h f", h=NR)[:, :, 0:half],
                                       sin[:, t, half:].unsqueeze(1).broadcast_to([P, NR, half]),
                                       ALU.mult).then_inc(s_prot, 1)

            def step(cur, nxt, edge):
                rotate(nxt.n)
                normalise(nxt.n)
                if edge:
                    wo_low(nxt.outer)

            pool.wait_ge(s_const, 48)
            rotate(0)
            wo_low(0)
            normalise(0)
            pipelined(pool, NKV, B, lambda first: None, step, lambda last: None)

        @block.scalar
        def _(act):
            def w_high(g):
                act.wait_ge(s_stage, 16 * g + 16)
                wait_from_one(act, s_q, 2 * NCH * B * g)
                for lo, w in CHUNKS:
                    act.activation(w_hi[:, :, lo:lo + w], stage_w[:, :, lo:lo + w], ACT.Copy).then_inc(s_whi, 1)

            def wo_high(g):
                act.wait_ge(s_stwo, 16 * g + 16)
                wait_from_one(act, s_y, B * g)
                act.activation(wo_hi[:], stage_wo[:], ACT.Copy).then_inc(s_wohi, 1)

            def project(n, m):
                t, (lo, w) = m // NCH, CHUNKS[m % NCH]
                act.wait_ge(s_q, 2 * NCH * n + m + 1)
                if m == 0:
                    wait_from_one(act, s_val, n)
                act.activation(qkv[:, t, lo:lo + w], bank[m % 2][:, 0:w], ACT.Copy).then_inc(s_qc, 1)

            def pT_copy(n, h):
                act.wait_ge(s_pT, REP * n + h + 1)
                act.activation(pT[:, h, :], bank[2 + h % 2][:, 0:S + P], ACT.Copy).then_inc(s_pTc, 1)

            def outputs(n):
                for p in range(4):
                    act.wait_ge(s_o, 4 * n + p + 1)
                    act.activation(oT_hi[:, 2 * p:2 * p + 2, :], bank[p][:].rearrange("p (h n) -> p h n", h=2),
                                   ACT.Copy).then_inc(s_oh, 1)

            def turned(n):
                act.wait_ge(s_T, 5 * n + 1)
                act.activation(T_hi[:, REP, :], bank[0][:, 0:S], ACT.Copy).then_inc(s_Th, 1)
                for i in range(4):
                    act.wait_ge(s_T, 5 * n + i + 2)
                    act.activation(T_hi[:, 2 * i:2 * i + 2, :], bank[1 - i % 2][:].rearrange("p (h n) -> p h n", h=2),
                                   ACT.Copy, scale=SCALE).then_inc(s_Th, 1)

            def exps(n):
                for h in range(REP):
                    act.wait_ge(s_max, 2 * (REP * n + h) + 2)
                    for t, cols in TILE_COLS:
                        act.activation(prob[:, h, cols], bank[4 + h % 4][:, t * S:t * S + (t + 1) * P], ACT.Exp,
                                       bias=nmax[:, h, t:t + 1], accum_out=rsum[:, h, t:t + 1]).then_inc(s_exp, 1)

            def begin(first):
                w_high(0)
                for m in range(2 * NCH):
                    project(0, m)
                wo_high(0)
                turned(0)
                exps(0)

            def step(cur, nxt, edge):
                if edge:
                    w_high(nxt.outer)
                for m in range(2 * NCH):
                    project(nxt.n, m)
                    for h in TURNS[m]:
                        pT_copy(cur.n, h)
                outputs(cur.n)
                turned(nxt.n)
                exps(nxt.n)
                if edge:
                    wo_high(nxt.outer)

            def finish(last):
                for h in range(REP):
                    pT_copy(last.n, h)
                outputs(last.n)

            pipelined(act, NKV, B, begin, step, finish)

        @block.vector
        def _(dve):
            def w_low(g):
                for n, (lo, w) in enumerate(CHUNKS):
                    dve.wait_ge(s_whi, NCH * g + n + 1)
                    dve.tensor_tensor(w_lo[:, :, lo:lo + w], stage_w[:, :, lo:lo + w], w_hi[:, :, lo:lo + w].bitcast(F32),
                                      ALU.subtract).then_inc(s_wlo, 1)

            def batch_slot(n, b):
                wait_from_one(dve, s_q, 2 * NCH * n)
                dve.tensor_copy(hs_hi[:], h_hi[:, :, bass.ds(b * S, S)]).then_inc(s_hs, 1)
                dve.tensor_copy(hs_lo[:], h_lo[:, :, bass.ds(b * S, S)]).then_inc(s_hs, 1)

            def rope(n):
                for t in range(2):
                    dve.wait_ge(s_qc, 2 * NCH * n + NCH * t + NCH)
                    q3 = qkv[:, t, 0:NR * HD].rearrange("p (h f) -> p h f", h=NR)
                    cs = lambda v, lo, w: v[:, t, lo:lo + w].unsqueeze(1).broadcast_to([P, NR, w])
                    dve.tensor_tensor(roped[:, t], q3, cs(cos, 0, HD), ALU.mult).then_inc(s_rot, 1)
                    wait_from_one(dve, s_rope, 2 * n + t)
                    dve.tensor_tensor(rot[:, :, 0:half], q3[:, :, half:], cs(sin, 0, half), ALU.mult).then_inc(s_rot, 1)
                    dve.wait_ge(s_rot, 4 * n + 2 * t + 2)
                    dve.wait_ge(s_prot, 2 * n + t + 1)
                    dve.tensor_tensor(roped[:, t], roped[:, t], rot[:], ALU.add).then_inc(s_rope, 1)

            def outputs_low(n):
                for p in range(4):
                    dve.wait_ge(s_oh, 4 * n + p + 1)
                    dve.tensor_tensor(oT_lo[:, 2 * p:2 * p + 2, :], bank[p][:].rearrange("p (h n) -> p h n", h=2),
                                      oT_hi[:, 2 * p:2 * p + 2, :].bitcast(F32), ALU.subtract).then_inc(s_ol, 1)

            def turned_low(n):
                dve.wait_ge(s_Th, 5 * n + 1)
                dve.tensor_tensor(T_lo[:, REP, :], bank[0][:, 0:S], T_hi[:, REP, :].bitcast(F32),
                                  ALU.subtract).then_inc(s_Tl, 1)
                for i in range(4):
                    dve.wait_ge(s_Th, 5 * n + i + 2)
                    dve.scalar_tensor_tensor(T_lo[:, 2 * i:2 * i + 2, :],
                                             bank[1 - i % 2][:].rearrange("p (h n) -> p h n", h=2), SCALE,
                                             T_hi[:, 2 * i:2 * i + 2, :].bitcast(F32),
                                             ALU.mult, ALU.subtract).then_inc(s_Tl, 1)

            def maxima(n):
                def inverse(h):
                    dve.wait_ge(s_exp, 2 * (REP * n + h) + 2)
                    dve.reciprocal(rinv[:, h, :], rsum[:, h, :]).then_inc(s_inv, 1)

                for h in range(REP):
                    dve.wait_ge(s_s, REP * n + h + 1)
                    for t in range(2):
                        dve.tensor_reduce(nmax[:, h, t:t + 1], bank[4 + h % 4][:, t * S:t * S + (t + 1) * P], AX_X,
                                          ALU.max, negate=True).then_inc(s_max, 1)
                    if h >= 2:
                        inverse(h - 2)
                inverse(REP - 2)
                inverse(REP - 1)

            def keep_values(n):
                wait_from_one(dve, s_o, 4 * n)
                dve.tensor_copy(val[:], qkv[:, :, NR * HD:]).then_inc(s_val, 1)

            def residual(n, b):
                dve.wait_ge(s_y, n + 1)
                rows2 = x[:, bass.ds(2 * b, 2), :]
                dve.tensor_tensor(rows2, Y[:].rearrange("p (t d) -> p t d", t=2), rows2, ALU.add).then_inc(s_add, 1)

            def begin(first):
                dve.wait_ge(s_const, 48)
                batch_slot(0, 0)
                w_low(0)
                rope(0)
                keep_values(0)
                batch_slot(1, 1)
                turned_low(0)
                maxima(0)

            def step(cur, nxt, edge):
                if edge:
                    w_low(nxt.outer)
                rope(nxt.n)
                outputs_low(cur.n)
                keep_values(nxt.n)
                turned_low(nxt.n)
                batch_slot(nxt.n + 1, nxt.inner + 1)
                residual(cur.n, cur.inner)
                maxima(nxt.n)

            def finish(last):
                outputs_low(last.n)
                residual(last.n, last.inner)

            pipelined(dve, NKV, B, begin, step, finish)
            dve.wait_ge(s_add, B * NKV)

        @block.tensor
        def _(pe):
            def project(nxt, m):
                n = nxt.n
                t, (lo, w) = m // NCH, CHUNKS[m % NCH]
                if m == 0:
                    pe.wait_ge(s_hs, 2 * n + 2)
                if m < NCH:
                    pe.wait_ge(s_wlo, NCH * nxt.outer + m + 1)
                if m >= 2:
                    pe.wait_ge(s_qc, 2 * NCH * n + m - 1)
                for k in range(KD):
                    last = split3(pe, bank[m % 2][:, 0:w], (hs_hi[:, k, tokens(t)], hs_lo[:, k, tokens(t)]),
                                  (w_hi[:, k, lo:lo + w], w_lo[:, k, lo:lo + w]), k == 0, k == KD - 1)
                last.then_inc(s_q, 1)

            def turn_probs(n, h):
                pe.wait_ge(s_prob, 2 * (REP * n + h) + 2)
                if h >= 2:
                    pe.wait_ge(s_pTc, REP * n + h - 1)
                for to, src in ((0, 0), (P, P), (S, S)):
                    last = pe.transpose(bank[2 + h % 2][:, to:to + P], prob[:, h, src:src + P], env.ident[:])
                last.then_inc(s_pT, 1)

            def attend(n):
                pe.wait_ge(s_val, n + 1)
                for p in range(4):
                    pe.wait_ge(s_pTc, REP * n + (2, 4, 7, 8)[p])
                    o3 = bank[p][:].rearrange("p (h n) -> p h n", h=2)
                    pe.matmul(bank[p][:], val[:, 0, :], pT[:, 2 * p:2 * p + 2, 0:S],
                              start=True, stop=False, skip_group_check=True)
                    pe.matmul(o3[:, :, P:], val[:, 1, :], pT[:, 2 * p:2 * p + 2, S:],
                              start=False, stop=True, skip_group_check=True).then_inc(s_o, 1)

            def turn_key(n):
                for t in range(2):
                    pe.wait_ge(s_rope, 2 * n + t + 1)
                    last = pe.transpose(bank[0][:, t * P:(t + 1) * P], roped[:, t, REP, :], env.ident[:])
                last.then_inc(s_T, 1)

            def turn_heads(n, i):
                if i >= 1:
                    pe.wait_ge(s_Tl, 5 * n + i)
                for j in range(2):
                    for t in range(2):
                        last = pe.transpose(bank[1 - i % 2][:, j * S + t * P:j * S + (t + 1) * P],
                                            roped[:, t, 2 * i + j, :], env.ident[:])
                last.then_inc(s_T, 1)

            def output(n, i):
                pe.wait_ge(s_ol, 4 * n + i + 1)
                for h in (2 * i, 2 * i + 1):
                    for t in range(2):
                        last = split3(pe, Y[:, t * D:(t + 1) * D], (oT_hi[:, h, tokens(t)], oT_lo[:, h, tokens(t)]),
                                      (wo_hi[:, h, :], wo_lo[:, h, :]), h == 0 and t == 0, h == REP - 1)
                if i == 3:
                    last.then_inc(s_y, 1)

            def scores(n):
                for h in range(REP):
                    if h == 3:
                        wait_from_one(pe, s_add, n)
                    if h >= 4:
                        pe.wait_ge(s_exp, 2 * (REP * n + h - 4) + 2)
                    pe.wait_ge(s_Tl, 5 * n + 2 + h // 2)
                    for t in range(2):
                        out = bank[4 + h % 4][:, t * S:(t + 1) * S]
                        split3(pe, out, (T_hi[:, h, tokens(t)], T_lo[:, h, tokens(t)]),
                               (T_hi[:, REP, :], T_lo[:, REP, :]), True, False)
                        last = pe.matmul(out[:, t * P:(t + 1) * P], env.ident_bf[:], causal[:], start=False, stop=True,
                                         skip_group_check=True)
                    last.then_inc(s_s, 1)

            def begin(first):
                pe.wait_ge(s_const, 48)
                for m in range(2 * NCH):
                    project(first, m)
                pe.wait_ge(s_qc, 2 * NCH)
                turn_key(0)
                for i in range(4):
                    turn_heads(0, i)
                scores(0)

            def step(cur, nxt, edge):
                for m in range(2 * NCH):
                    project(nxt, m)
                    for h in TURNS[m]:
                        turn_probs(cur.n, h)
                pe.wait_ge(s_qc, 2 * NCH * nxt.n + 2 * NCH)
                attend(cur.n)
                pe.wait_ge(s_ol, 4 * cur.n + 2)
                turn_key(nxt.n)
                pe.wait_ge(s_wolo, cur.outer + 1)
                for i in range(4):
                    turn_heads(nxt.n, i)
                    output(cur.n, i)
                scores(nxt.n)

            def finish(last):
                for h in range(REP):
                    turn_probs(last.n, h)
                attend(last.n)
                pe.wait_ge(s_wolo, NKV)
                for i in range(4):
                    output(last.n, i)

            pipelined(pe, NKV, B, begin, step, finish)


def program(nc, dram, out, stages=("A", "B", "C", "D", "E")):
    with ExitStack() as ctx:
        env = Env(nc, ctx, dram)
        env.x = env.sb("x", [P, NT, D])
        env.x_in = env.sb("x_in", [P, NT, D])
        env.ident, env.ident_bf = env.sb("ident", [P, P]), env.sb("ident_bf", [P, P], BF16)
        env.minus_half = env.sb("minus_half", [P, NT])
        env.bank = [ctx.enter_context(nc.psum_tensor(f"bank{i}", [P, 512], F32)) for i in range(8)]
        s_in, s_out, s_half = env.sem("inputs_loaded"), env.sem("out_stored"), env.sem("minus_half_ready")
        with nc.Block() as block:
            @block.sync
            def _(sp):
                sp.dma_start(env.x[:], dram["x"]).then_inc(s_in, 16)
                sp.dma_start(env.ident[:], dram["ident"]).then_inc(s_in, 16)
                sp.dma_start(env.ident_bf[:], dram["ident_bf"]).then_inc(s_in, 16)
                sp.wait_ge(s_in, 48)

            @block.gpsimd
            def _(pool):
                pool.memset(env.minus_half[:], -0.5).then_inc(s_half, 1)
                pool.wait_ge(s_half, 1)
        if "A" in stages:
            env.stage(lambda: quantised_attention(env))
        if "B" in stages:
            env.stage(lambda: experts(env, "f0", 0))
        if "C" in stages:
            env.stage(lambda: latent_attention(env))
        if "D" in stages:
            env.stage(lambda: grouped_attention(env))
        if "E" in stages:
            env.stage(lambda: experts(env, "f1", 1))
        with nc.Block() as block:
            @block.sync
            def _(sp):
                sp.dma_start(out, env.x[:]).then_inc(s_out, 16)
                sp.wait_ge(s_out, 16)


def rows(v, n=128):
    import numpy as np
    return np.broadcast_to(v, (n,) + v.shape)


def layout(i):
    import numpy as np
    bf = mybir.dt.np(BF16)
    c = lambda a: np.ascontiguousarray(a)
    tok = lambda a: c(a.reshape(NT, P, -1).transpose(1, 0, 2))
    kmaj = lambda w: w.reshape(KD, P, -1).transpose(1, 0, 2)
    d = {}
    d["x"] = tok(i["x"])
    d["ident"] = np.eye(P, dtype=np.float32)
    d["ident_bf"] = np.eye(P).astype(bf)

    def unit_weights(g, u, w):
        return np.concatenate([kmaj(g).reshape(P, -1), kmaj(u).reshape(P, -1), w], axis=1)

    g, u, w = i["L0_ffn_Wg"], i["L0_ffn_Wu"], i["L0_ffn_Wd"]
    d["f0_weights"] = c(np.stack([unit_weights(g[e][:, f], u[e][:, f], w[e][f]) for e in range(8)
                                  for f in (slice(0, 128), slice(128, 256))]))
    g, u, w = i["L1_ffn_Wg"], i["L1_ffn_Wu"], i["L1_ffn_Wd"]
    d["f1_weights"] = c(np.stack([unit_weights(g[e], u[e], w[e]) for e in range(32)]
                                 + [unit_weights(i["L1_ffn_Wsg"], i["L1_ffn_Wsu"], i["L1_ffn_Wsd"])]))
    for tag, r in (("f0", i["L0_ffn_Wr"]), ("f1", i["L1_ffn_Wr"])):
        pad = np.zeros((P, KD, P), np.float32)
        pad[:, :, :r.shape[1]] = kmaj(r)
        d[f"{tag}_wr"] = pad
    d["f0_route"] = c(np.broadcast_to(i["L0_ffn_temperature"], (P, 32)))
    d["f1_route"] = c(rows(i["L1_ffn_expert_bias"]))
    d["ln2_rows"] = c(rows(i["L1_ffn_ln2_w"]))
    d["before"] = c(rows(np.tril(np.ones((8, 8), np.float32), -1)))
    sel = np.zeros((3, RW, RW, P), np.float32)
    for e in range(RW):
        sel[:, e, e, :] = 1
    d["sel"] = sel.reshape(3 * RW, RW * P).astype(bf)

    d["wq_wo"] = c(np.concatenate([i[f"L0_xattn_w{n}"].reshape(2, P, D) for n in "qo"]).transpose(1, 0, 2))
    d["wkvT"] = c(np.concatenate([kmaj(i[f"L0_xattn_w{n}"].T) for n in "kv"], axis=2))
    d["l0_bias"] = c(rows(np.stack([i[f"L0_xattn_b{n}"] for n in "qkvo"])))
    d["mask"] = tok(i["mask_BxSxS2_ff0"])
    d["ctxT"] = c(i["ctx_2048"].reshape(TOK, KD, P).transpose(2, 1, 0))
    d["w_kvc"] = c(kmaj(i["L1_xattn_W_kvc"]))
    d["w_dq"] = np.zeros((P, KD, P), np.float32)
    d["w_dq"][:, :, :QC] = kmaj(i["L1_xattn_W_dq"])
    d["uqT"] = c(i["L1_xattn_W_uq"].reshape(QC, H1, HD1).transpose(2, 1, 0))
    d["ukT"] = c(i["L1_xattn_W_uk"].reshape(KVC, H1, HD1).transpose(2, 1, 0))
    uvT = i["L1_xattn_W_uv"].reshape(KVC, H1, HD1).transpose(2, 1, 0)
    d["uvT2"] = c(np.concatenate([uvT, uvT], axis=2))
    d["la_wo"] = c(i["L1_xattn_W_o"].reshape(H1, HD1, D).transpose(1, 0, 2))
    d["qr"] = c(i["L1_xattn_W_qr"].reshape(QC, H1, RD))
    d["key_w"] = c(np.concatenate([np.eye(KVC, dtype=np.float32), i["L1_xattn_W_kr"]], axis=1))
    d["la_cos"], d["la_sin"] = rotary(RD)
    d["seg"] = c(i["itok_BxS_0_1023"].reshape(NT, P).T)
    d["key_id"] = c(rows(np.arange(S, dtype=np.float32)))
    wq = kmaj(i["L1_ffn_Wq"]).reshape(P, KD, NKV, REP * HD)
    wk, wv = (kmaj(i[f"L1_ffn_W{n}"]).reshape(P, KD, NKV, HD) for n in "kv")
    d["ga_w"] = c(np.concatenate([wq, wk, wv], axis=3).transpose(2, 0, 1, 3))
    d["ga_wo"] = c(i["L1_ffn_Wo"].reshape(NKV, REP, HD, D).transpose(0, 2, 1, 3))
    d["ln1_rows"] = c(rows(i["L1_ffn_ln1_w"]))
    d["ga_cos"], d["ga_sin"] = rotary(HD)
    d["causal"] = np.where(np.tril(np.ones((P, P), bool)), 0.0, NEG).astype(bf)
    return d


def rotary(width):
    import numpy as np
    half = width // 2
    freq = (np.float32(1.0) / np.float32(10000.0) ** (np.arange(half, dtype=np.float32) / np.float32(half)))
    ang = (np.arange(S, dtype=np.float32)[:, None] * freq.astype(np.float32)).astype(np.float32)
    lay = lambda a, b: np.ascontiguousarray(
        np.concatenate([a, b], axis=1).astype(np.float32).reshape(S // P, P, width).transpose(1, 0, 2))
    cos, sin = np.cos(ang.astype(np.float64)), np.sin(ang.astype(np.float64))
    return lay(cos, cos), lay(-sin, sin)


def kernel(**inputs):
    import numpy as np
    import concourse.bacc as bacc
    from concourse.bass_utils import run_bass_kernel_spmd

    nc = bacc.Bacc("TRN2", target_bir_lowering=False, num_devices=1)
    arrays = {f"in_{k}": v for k, v in layout({k: np.asarray(v) for k, v in inputs.items()}).items()}
    dram = {k[3:]: nc.dram_tensor(k, v.shape, mybir.dt.from_np(v.dtype), kind="ExternalInput").ap()
            for k, v in arrays.items()}
    out = nc.dram_tensor("out", (P, NT, D), F32, kind="ExternalOutput").ap()
    program(nc, dram, out)
    r = run_bass_kernel_spmd(nc, [arrays], core_ids=[0])
    y = r.results[0]["out"]
    return np.ascontiguousarray(y.transpose(1, 0, 2)).reshape(B, S, D)
```

```python
import math
from contextlib import ExitStack

import concourse.bass as bass
from concourse import mybir

F32 = mybir.dt.float32
F32R = mybir.dt.float32r
BF16 = mybir.dt.bfloat16
I32 = mybir.dt.int32
ALU = mybir.AluOpType
ACT = mybir.ActivationFunctionType
AX_X = mybir.AxisListType.X

P = 128
B, S, D = 4, 256, 256
TOK = B * S
NT = TOK // P
KD = D // P
MAGIC = 1.5 * 2.0 ** 23
NEG = -1e30


class Env:

    def __init__(self, nc, ctx, dram):
        self.nc, self.ctx, self.dram = nc, ctx, dram
        self.stage_ctx, self.stage_sems = ctx, []

    def sb(self, name, shape, dt=F32, ctx=None):
        return (ctx or self.ctx).enter_context(self.nc.sbuf_tensor(name, shape, dt))

    def sem(self, name):
        handle = self.stage_ctx.enter_context(self.nc.semaphore(name))
        self.stage_sems.append(handle)
        return handle

    def stage(self, build):
        with ExitStack() as self.stage_ctx:
            self.stage_sems = []
            build()
            numbers = sorted(s.num for s in self.stage_sems)
            runs, first = [], numbers[0]
            for a, b in zip(numbers, numbers[1:] + [None]):
                if b != a + 1:
                    runs.append(range(first, a + 1))
                    first = b
            with self.nc.Block() as block:
                @block.sync
                def _(sp):
                    for run in runs:
                        sp.sem_clear(run)


def tokens(t):
    return slice(t * P, (t + 1) * P)


def wait_from_one(eng, sem, value):
    if not isinstance(value, int) or value > 0:
        eng.wait_ge(sem, value)


def split3(pe, out, a, b, start, stop):
    (ah, al), (bh, bl) = a, b
    pe.matmul(out, ah, bh, start=start, stop=False, skip_group_check=True)
    pe.matmul(out, ah, bl, start=False, stop=False, skip_group_check=True)
    return pe.matmul(out, al, bh, start=False, stop=stop, skip_group_check=True)


class Group:

    def __init__(self, n, outer, inner):
        self.n, self.outer, self.inner = n, outer, inner


def pipelined(eng, outer, inner, begin, step, finish):
    begin(Group(0, 0, 0))
    with eng.Fori(0, outer - 1) as o:
        with eng.Fori(0, inner - 1) as i:
            step(Group(o * inner + i, o, i), Group(o * inner + i + 1, o, i + 1), False)
        step(Group(o * inner + inner - 1, o, inner - 1), Group(o * inner + inner, o + 1, 0), True)
    last = outer - 1
    with eng.Fori(0, inner - 1) as i:
        step(Group(last * inner + i, last, i), Group(last * inner + i + 1, last, i + 1), False)
    finish(Group(outer * inner - 1, last, inner - 1))


class Norm:

    def __init__(self, env, tag, mem, rms_weight=None, dst=None):
        self.e, self.tag, self.rms = env, tag, rms_weight
        sb = lambda n, s, d=F32: env.sb(f"{tag}_{n}", s, d, mem)
        self.stats = sb("bn_stats", [P, NT, 6])
        self.moments = sb("moments", [P, NT, 2])
        self.square = sb("square", [P, D]) if rms_weight is not None else None
        self.var_eps = sb("var_eps", [P, NT])
        self.rstd = sb("rstd", [P, NT])
        self.xn = sb("xn", [P, NT, D]) if dst is None else dst
        s = lambda n: env.sem(f"{tag}_{n}")
        self.s_stats, self.s_moments, self.s_var = s("stats_done"), s("moments_done"), s("var_done")
        self.s_rstd, self.s_xn = s("rstd_done"), s("xn_ready")
        self.s_tr, self.s_hi, self.s_lo = s("xT_in_psum"), s("xT_hi_ready"), s("xT_lo_ready")

    def scalar_stats(self, act):
        for t in range(NT):
            if t:
                act.wait_ge(self.s_stats, t)
            act.activation(self.square[:], self.e.x[:, t, :], ACT.Square,
                           accum_out=self.moments[:, t, 0:1]).then_inc(self.s_stats, 1)

    def vector_normalise(self, dve, kept=None):
        x = self.e.x
        if self.rms is None:
            for t in range(NT):
                dve.bn_stats(self.stats[:, t, :], x[:, t, :]).then_inc(self.s_stats, 1)
            for t in range(NT):
                dve.wait_ge(self.s_stats, t + 1)
                dve.bn_aggr(self.moments[:, t, :], self.stats[:, t, :]).then_inc(self.s_moments, 1)
            dve.wait_ge(self.s_moments, NT)
            dve.tensor_scalar(self.var_eps[:], self.moments[:, :, 1], 1e-5, None, ALU.add).then_inc(self.s_var, 1)
        else:
            dve.wait_ge(self.s_stats, NT)
            dve.tensor_scalar(self.var_eps[:], self.moments[:, :, 0], 1.0 / D, 1e-5,
                              ALU.mult, ALU.add).then_inc(self.s_var, 1)
        dve.wait_ge(self.s_rstd, 1)
        if kept is not None:
            dve.wait_ge(kept, 1)
        for t in range(NT):
            if self.rms is None:
                dve.tensor_scalar(self.xn[:, t, :], x[:, t, :], self.moments[:, t, 0:1], self.rstd[:, t:t + 1],
                                  ALU.subtract, ALU.mult).then_inc(self.s_xn, 1)
            else:
                dve.scalar_tensor_tensor(self.xn[:, t, :], x[:, t, :], self.rstd[:, t:t + 1], self.rms[:],
                                         ALU.mult, ALU.mult).then_inc(self.s_xn, 1)

    def gpsimd_rstd(self, pool):
        pool.wait_ge(self.s_var, 1)
        pool.tensor_tensor(self.rstd[:], self.var_eps[:], self.e.minus_half[:], ALU.pow).then_inc(self.s_rstd, 1)

    def tensor_transpose(self, pe, banks):
        for b in range(B):
            pe.wait_ge(self.s_xn, 2 * b + 2)
            if b >= 2:
                pe.wait_ge(self.s_lo, b - 1)
            bank = banks[b % 2][:].rearrange("p (k t q) -> p k t q", k=KD, t=2)
            for k in range(KD):
                for t in range(2):
                    last = pe.transpose(bank[:, k, t, :], self.xn[:, 2 * b + t, k * P:(k + 1) * P], self.e.ident[:])
            last.then_inc(self.s_tr, 1)

    def scalar_hi(self, act, banks, hi):
        for b in range(B):
            act.wait_ge(self.s_tr, b + 1)
            act.activation(hi[:, :, b * S:(b + 1) * S], banks[b % 2][:].rearrange("p (k q) -> p k q", k=KD),
                           ACT.Copy).then_inc(self.s_hi, 1)

    def vector_lo(self, dve, banks, hi, lo):
        for b in range(B):
            dve.wait_ge(self.s_hi, b + 1)
            cols = slice(b * S, (b + 1) * S)
            dve.tensor_tensor(lo[:, :, cols], banks[b % 2][:].rearrange("p (k q) -> p k q", k=KD),
                              hi[:, :, cols].bitcast(F32), ALU.subtract).then_inc(self.s_lo, 1)
H0, HD0 = 16, 16
HG0 = 4
NG0 = H0 // HG0
QMAX, QEPS = 127.0, 1e-8
MASK_LOW = -1e38


class Quant:

    def __init__(self, env, tag, mem, n, parts=1):
        self.n, self.parts = n, parts
        self.scale, self.inv = env.sb(f"{tag}_scale", [P, n], F32, mem), env.sb(f"{tag}_inv", [P, n], F32, mem)
        self.work = env.sb(f"{tag}_work", [P, n, D], F32, mem)
        self.whole = env.sb(f"{tag}_whole", [P, n, D], BF16, mem)
        self.stepped, self.ready = env.sem(f"{tag}_stepped"), env.sem(f"{tag}_ready")

    def run(self, dve, rows):
        taken = 0
        for part in range(self.parts):
            m = self.n // self.parts
            t = slice(part * m, (part + 1) * m)
            scale, inv, work = self.scale[:, t], self.inv[:, t], self.work[:, t, :]
            dve.tensor_reduce(scale, rows[:, t, :], AX_X, ALU.max, apply_absolute_value=True).then_inc(self.stepped, 1)
            dve.wait_ge(self.stepped, taken + 1)
            dve.tensor_scalar(scale, scale, 1.0 / QMAX, QEPS, ALU.mult, ALU.max).then_inc(self.stepped, 1)
            dve.wait_ge(self.stepped, taken + 2)
            dve.reciprocal(inv, scale).then_inc(self.stepped, 1)
            dve.wait_ge(self.stepped, taken + 3)
            for i in range(t.start, t.stop):
                dve.tensor_scalar(self.work[:, i, :], rows[:, i, :], self.inv[:, i:i + 1], QMAX,
                                  ALU.mult, ALU.min).then_inc(self.stepped, 1)
            dve.wait_ge(self.stepped, taken + 3 + m)
            dve.tensor_scalar(work, work, -QMAX, MAGIC, ALU.max, ALU.add).then_inc(self.stepped, 1)
            taken += 4 + m
            dve.wait_ge(self.stepped, taken)
            dve.tensor_scalar(self.whole[:, t, :], work, MAGIC, None, ALU.subtract).then_inc(self.ready, 1)


def quantised_attention(env, latent):
    nc, dram, x = env.nc, env.dram, env.x
    bank = env.bank
    with ExitStack() as mem:
        sb = lambda n, s, d=F32: env.sb(f"qa_{n}", s, d, mem)
        sem = lambda n: env.sem(f"qa_{n}")
        GROUPS, GW = B * NG0, HG0 * HD0
        q_grp, kv_grp = sb("q_grp", [P, GROUPS + 1, 2, GW]), sb("kv_grp", [P, GROUPS + 1, 2, 2, GW])
        o_tok = sb("o_tok", [P, NT, D])
        mask_hi, mask_lo = sb("mask_hi", [P, NT, S], F32R), sb("mask_lo", [P, NT, S], F32R)
        ident_r = sb("ident_r", [P, P], F32R)
        w_rows = sb("w_rows", [P, 2, D])
        wT = sb("wT", [P, 2, KD, D], BF16)
        bias_rows = sb("bias_rows", [P, 4, D])
        s_mask = sem("mask_loaded")
        half_banks = lambda t: bank[4 + t // 2 % 4][:, (t % 2) * D:(t % 2 + 1) * D]

        def turn_rows(pe, quant, done):
            for n in range(2):
                pe.wait_ge(quant.ready, min(n + 1, quant.parts))
                v = bank[n][:].bitcast(BF16).rearrange("p (k t m) -> p k t m", k=KD, t=4)
                for k in range(KD):
                    for t in range(4):
                        last = pe.transpose(v[:, k, t, :], quant.whole[:, 4 * n + t, k * P:(k + 1) * P], env.ident_bf[:])
                last.then_inc(done, 1)

        with ExitStack() as prep:
            sp_ = lambda n, s, d=F32: env.sb(f"qa_{n}", s, d, prep)
            norm = Norm(env, "qa", prep)
            wq_wo = sp_("wq_wo", [P, 4, D])
            ctxT, wkvT = latent.ctxT, sp_("wkvT", [P, KD, 2 * D])
            c_hi, c_lo = sp_("c_hi", [P, KD, TOK], F32R), sp_("c_lo", [P, KD, TOK], F32R)
            wkv_hi, wkv_lo = sp_("wkv_hi", [P, KD, 2 * D], F32R), sp_("wkv_lo", [P, KD, 2 * D], F32R)
            mask = sp_("mask", [P, NT, S])
            ones, diag = sp_("ones", [P, P]), sp_("diag", [P, 4, P])
            xqT = sp_("xqT", [P, KD, TOK], BF16)
            wquant, xquant = Quant(env, "qa_wq", prep, 4), Quant(env, "qa_xq", prep, NT)
            q_scaled = xquant.work
            s_kvin, s_win, s_bin = sem("kv_inputs_loaded"), sem("query_weights_loaded"), sem("biases_loaded")
            s_hi, s_lo, s_ones = sem("hi_ready"), sem("lo_ready"), sem("ones_ready")
            s_clamp, s_mhi, s_mlo = sem("mask_clamped"), sem("mask_hi_ready"), sem("mask_lo_ready")
            s_end = sem("last_group_zero")
            s_diag, s_rows, s_rowc = sem("diag_ready"), sem("w_rows_in_psum"), sem("w_rows_copied")
            s_wTp, s_wT, s_xTp, s_xT = sem("wT_in_psum"), sem("wT_ready"), sem("xqT_in_psum"), sem("xqT_ready")
            s_kv, s_kvc, s_q, s_qs, s_qb = (sem(n) for n in (
                "kv_in_psum", "kv_ready", "q_in_psum", "q_scaled", "q_ready"))
            block = prep.enter_context(nc.Block())

            @block.sync
            def _(sp):
                sp.dma_start(wkvT[:], dram["wkvT"]).then_inc(s_kvin, 16)
                sp.dma_start(ctxT[:], dram["ctxT"]).then_inc(s_kvin, 16)
                sp.dma_start(wq_wo[:], dram["wq_wo"]).then_inc(s_win, 16)
                sp.dma_start(bias_rows[:], dram["l0_bias"]).then_inc(s_bin, 16)
                sp.dma_start(mask[:], dram["mask"]).then_inc(s_mask, 16)
                latent.sync_load(sp)

            @block.gpsimd
            def _(pool):
                pool.memset(ones[:], 1.0).then_inc(s_ones, 1)
                pool.memset(q_grp[:, GROUPS], 0.0).then_inc(s_end, 1)
                pool.memset(kv_grp[:, GROUPS], 0.0).then_inc(s_end, 1)
                norm.gpsimd_rstd(pool)
                pool.wait_ge(s_hi, 1)
                pool.tensor_tensor(wkv_lo[:], wkvT[:], wkv_hi[:].bitcast(F32), ALU.subtract).then_inc(s_lo, 1)
                for c in range(2):
                    cols = slice(c * 512, (c + 1) * 512)
                    pool.wait_ge(s_hi, 2 + c)
                    pool.tensor_tensor(c_lo[:, :, cols], ctxT[:, :, cols], c_hi[:, :, cols].bitcast(F32),
                                       ALU.subtract).then_inc(s_lo, 1)
                pool.wait_ge(s_mhi, 2)
                pool.tensor_tensor(mask_lo[:], mask[:], mask_hi[:].bitcast(F32), ALU.subtract).then_inc(s_mlo, 1)
                pool.wait_ge(s_bin, 16)
                for t in range(NT):
                    pool.wait_ge(s_qs, t + 1)
                    pool.tensor_tensor(q_grp[:, t // 2 * NG0:(t // 2 + 1) * NG0, t % 2, :],
                                       q_scaled[:, t, :].rearrange("p (g d) -> p g d", g=NG0),
                                       bias_rows[:, 0, :].rearrange("p (g d) -> p g d", g=NG0), ALU.add).then_inc(s_qb, 1)

            @block.scalar
            def _(act):
                act.wait_ge(s_kvin, 32)
                act.activation(wkv_hi[:], wkvT[:], ACT.Copy).then_inc(s_hi, 1)
                for c in range(2):
                    cols = slice(c * 512, (c + 1) * 512)
                    act.activation(c_hi[:, :, cols], ctxT[:, :, cols], ACT.Copy).then_inc(s_hi, 1)
                act.wait_ge(env.s_const, 32)
                act.activation(ident_r[:], env.ident[:], ACT.Copy).then_inc(s_mhi, 1)
                act.wait_ge(s_rows, 1)
                act.activation(w_rows[:].rearrange("p w d -> p (w d)"), bank[0][:], ACT.Copy).then_inc(s_rowc, 1)
                act.wait_ge(s_wTp, 1)
                act.activation(wT[:].rearrange("p w k d -> p (w k d)"), bank[1][:].bitcast(BF16),
                               ACT.Copy).then_inc(s_wT, 1)
                act.wait_ge(s_clamp, 1)
                act.activation(mask_hi[:], mask[:], ACT.Copy).then_inc(s_mhi, 1)
                for n in range(2):
                    act.wait_ge(s_xTp, n + 1)
                    act.activation(xqT[:, :, n * 512:(n + 1) * 512],
                                   bank[n][:].bitcast(BF16).rearrange("p (k q) -> p k q", k=KD), ACT.Copy).then_inc(s_xT, 1)

            @block.vector
            def _(dve):
                dve.wait_ge(env.s_x, 16)
                norm.vector_normalise(dve)
                dve.wait_ge(norm.s_xn, NT)
                xquant.run(dve, norm.xn[:])
                dve.wait_ge(s_win, 16)
                wquant.run(dve, wq_wo[:])
                dve.wait_ge(env.s_const, 32)
                for i in range(4):
                    dve.tensor_scalar(diag[:, i, :], env.ident[:], wquant.scale[:, i:i + 1], None, ALU.mult).then_inc(s_diag, 1)
                dve.wait_ge(s_bin, 16)
                dve.wait_ge(s_mask, 16)
                dve.tensor_scalar(mask[:], mask[:], MASK_LOW, None, ALU.max).then_inc(s_clamp, 1)
                for t in range(NT):
                    dve.wait_ge(s_kv, t + 1)
                    dve.tensor_tensor(kv_grp[:, t // 2 * NG0:(t // 2 + 1) * NG0, :, t % 2, :].rearrange("p g a d -> p a g d"),
                                      bank[2 + t % 4][:].rearrange("p (a g d) -> p a g d", a=2, g=NG0),
                                      bias_rows[:, 1:3, :].rearrange("p a (g d) -> p a g d", g=NG0),
                                      ALU.add).then_inc(s_kvc, 1)
                dve.wait_ge(s_rowc, 1)
                dve.wait_ge(xquant.ready, 1)
                for t in range(NT):
                    dve.wait_ge(s_q, t // 2 * 2 + 2)
                    dve.scalar_tensor_tensor(q_scaled[:, t, :], half_banks(t), xquant.scale[:, t:t + 1], w_rows[:, 0, :],
                                             ALU.mult, ALU.mult).then_inc(s_qs, 1)
                dve.wait_ge(s_qs, NT)
                dve.wait_ge(s_qb, NT)
                dve.wait_ge(s_kvc, NT)
                dve.wait_ge(s_mlo, 1)
                dve.wait_ge(s_end, 2)

            @block.tensor
            def _(pe):
                def keys_values(tiles):
                    for t in tiles:
                        pe.wait_ge(s_lo, 2 + t // 4)
                        if t >= 4:
                            pe.wait_ge(s_kvc, t - 3)
                        for k in range(KD):
                            last = split3(pe, bank[2 + t % 4][:], (c_hi[:, k, tokens(t)], c_lo[:, k, tokens(t)]),
                                          (wkv_hi[:, k, :], wkv_lo[:, k, :]), k == 0, k == KD - 1)
                        last.then_inc(s_kv, 1)

                keys_values(range(0, 4))
                pe.wait_ge(s_ones, 1)
                pe.wait_ge(s_diag, 4)
                pe.matmul(bank[0][:], ones[:], diag[:].rearrange("p i m -> p (i m)"), start=True, stop=True).then_inc(s_rows, 1)
                pe.wait_ge(wquant.ready, 1)
                pe.wait_ge(env.s_const, 32)
                wb = bank[1][:].bitcast(BF16).rearrange("p (w k o m) -> p w k o m", w=2, k=KD, o=2)
                for w in range(2):
                    for k in range(KD):
                        for o in range(2):
                            last = pe.transpose(wb[:, w, k, o, :], wquant.whole[:, 2 * w + o, k * P:(k + 1) * P],
                                                env.ident_bf[:])
                last.then_inc(s_wTp, 1)
                keys_values(range(4, NT))
                pe.wait_ge(s_rowc, 1)
                pe.wait_ge(s_wT, 1)
                turn_rows(pe, xquant, s_xTp)
                pe.wait_ge(s_kvc, NT)
                for t in range(NT):
                    pe.wait_ge(s_xT, t // 4 + 1)
                    for k in range(KD):
                        last = pe.matmul(half_banks(t), xqT[:, k, tokens(t)], wT[:, 0, k, :], start=k == 0, stop=k == KD - 1)
                    last.then_inc(s_q, 1)

        with ExitStack() as loop:
            sl = lambda n, s, d=F32: env.sb(f"qa_{n}", s, d, loop)
            qd, kd = sl("qd", [P, 2, HG0, 4, HD0], F32R), sl("kd", [P, 2, HG0, 4, HD0], F32R)
            qT = sl("qT", [P, 2, S], F32R)
            kT = sl("kT", [P, 2, 2, S], F32R)
            vp = sl("vp", [P, 2, HG0, 32])
            prob = sl("prob", [P, 4, 2, S])
            nmax, rsum, rinv = sl("nmax", [P, 4, 2]), sl("rsum", [P, 4, 2]), sl("rinv", [P, 4, 2])
            pT = sl("pT", [P, 2, HG0, S])
            oT = sl("oT", [P, S])
            s_zero = sem("zeros_ready")
            s_dh, s_dl, s_v = sem("parts_hi_ready"), sem("parts_lo_ready"), sem("values_ready")
            s_T, s_Ta, s_Tv = sem("qk_T_in_psum"), sem("q_and_low_keys_copied"), sem("high_keys_copied")
            s_s, s_max, s_exp, s_inv = (sem(n) for n in ("scores_in_psum", "max_ready", "exp_ready", "row_inverse_ready"))
            s_pT, s_pTa, s_pTv = sem("pT_in_psum"), sem("pT_copied_by_scalar"), sem("pT_copied_by_vector")
            s_o, s_oc, s_oT, s_done = sem("oT_in_psum"), sem("oT_copied"), sem("o_in_psum"), sem("o_ready")
            block = loop.enter_context(nc.Block())
            twice = lambda v: v.rearrange("p (h d) -> p h d", h=HG0).unsqueeze(2).broadcast_to([P, HG0, 2, HD0])

            def q_cols(n, t):
                return q_grp[:].rearrange("p g t d -> p (g t d)")[:, bass.ds(n * (2 * GW) + t * GW, GW)]

            def kv_cols(n, a, t):
                return kv_grp[:].rearrange("p g a t d -> p (g a t d)")[:, bass.ds(n * (4 * GW) + (2 * a + t) * GW, GW)]

            def pT_view(u):
                return pT[:, :, 2 * (u // 2):2 * (u // 2) + 2, (u % 2) * P:(u % 2 + 1) * P]

            def pT_bank(u):
                return bank[4 + u][:].rearrange("p (k j n) -> p k j n", k=2, j=2)

            @block.gpsimd
            def _(pool):
                def parts(n):
                    wait_from_one(pool, s_T, 2 * n)
                    for t in range(2):
                        pool.tensor_copy(qd[:, t, :, 0:2, :], twice(q_cols(n, t))).then_inc(s_dh, 1)
                        pool.tensor_copy(kd[:, t, :, 0::2, :], twice(kv_cols(n, 0, t))).then_inc(s_dh, 1)

                def values(n):
                    wait_from_one(pool, s_o, 2 * n)
                    for t in range(2):
                        pool.tensor_copy(vp[:, t, :, 0:HD0], kv_cols(n, 1, t).rearrange("p (h d) -> p h d", h=HG0)
                                         ).then_inc(s_v, 1)

                pool.memset(vp[:], 0.0).then_inc(s_zero, 1)
                pool.memset(kT[:].bitcast(F32), 0.0).then_inc(s_zero, 1)
                pool.wait_ge(s_zero, 2)
                parts(0)
                values(0)
                parts(1)
                with pool.Fori(0, GROUPS - 1) as i:
                    parts(i + 2)
                    values(i + 1)

            @block.scalar
            def _(act):
                def turned(n):
                    act.wait_ge(s_T, 2 * n + 1)
                    act.activation(kT[0:64, :, 0, :], bank[0][0:64, :].rearrange("p (a n) -> p a n", a=2),
                                   ACT.Copy).then_inc(s_Ta, 1)
                    act.wait_ge(s_T, 2 * n + 2)
                    act.activation(qT[:].rearrange("p a n -> p (a n)"), bank[1][:], ACT.Copy,
                                   scale=1.0 / math.sqrt(HD0)).then_inc(s_Ta, 1)

                def exps(n):
                    for u in range(4):
                        act.wait_ge(s_max, 4 * n + u + 1)
                        for j in range(2):
                            act.activation(prob[:, u, j, :], bank[4 + u][:, j * S:(j + 1) * S], ACT.Exp,
                                           bias=nmax[:, u, j:j + 1], accum_out=rsum[:, u, j:j + 1]).then_inc(s_exp, 1)

                def probs_turned(n):
                    for u in (0, 2):
                        act.wait_ge(s_pT, 4 * n + u + 1)
                        act.activation(pT_view(u), pT_bank(u), ACT.Copy).then_inc(s_pTa, 1)

                def group(n):
                    exps(n)
                    turned(n + 1)
                    probs_turned(n)

                act.wait_ge(s_zero, 2)
                turned(0)
                group(0)
                with act.Fori(0, GROUPS - 1) as i:
                    group(i + 1)

            @block.vector
            def _(dve):
                def parts(n):
                    for t in range(2):
                        dve.wait_ge(s_dh, 4 * n + 2 * t + 2)
                        dve.tensor_tensor(qd[:, t, :, 2:4, :], twice(q_cols(n, t)), qd[:, t, :, 0:2, :].bitcast(F32),
                                          ALU.subtract).then_inc(s_dl, 1)
                        dve.tensor_tensor(kd[:, t, :, 1::2, :], twice(kv_cols(n, 0, t)),
                                          kd[:, t, :, 0::2, :].bitcast(F32), ALU.subtract).then_inc(s_dl, 1)

                def turned(n):
                    dve.wait_ge(s_T, 2 * n + 1)
                    dve.tensor_copy(kT[64:P, :, 1, :], bank[0][64:P, :].rearrange("p (a n) -> p a n", a=2)).then_inc(s_Tv, 1)

                def maxima(n):
                    for u in range(4):
                        dve.wait_ge(s_s, 4 * n + u + 1)
                        dve.tensor_reduce(nmax[:, u, :], bank[4 + u][:].rearrange("p (j n) -> p j n", j=2), AX_X,
                                          ALU.max, negate=True).then_inc(s_max, 1)

                def outputs(n):
                    for h in range(HG0):
                        if h % 2 == 0:
                            dve.wait_ge(s_o, 2 * n + h // 2 + 1)
                        r = slice(32 * h, 32 * h + 32)
                        dve.tensor_copy(oT[r, :], bank[2 + h // 2][r, (h % 2) * S:(h % 2 + 1) * S]).then_inc(s_oc, 1)

                def probs_turned(n):
                    for u in (1, 3):
                        dve.wait_ge(s_pT, 4 * n + u + 1)
                        dve.tensor_copy(pT_view(u), pT_bank(u)).then_inc(s_pTv, 1)

                def inverse(n):
                    dve.wait_ge(s_exp, 8 * n + 8)
                    dve.wait_ge(s_done, 2 * n + 1)
                    dve.reciprocal(rinv[:], rsum[:]).then_inc(s_inv, 1)

                def store(g):
                    dve.wait_ge(s_oT, g.n + 1)
                    dve.wait_ge(s_inv, g.n + 1)
                    for t in range(2):
                        o4 = bank[2][:, t * P:(t + 1) * P].rearrange("p (a j d) -> p a j d", a=2, j=2)
                        inv = rinv[:, t::2, :].unsqueeze(3).broadcast_to([P, 2, 2, HD0])
                        out = o_tok[:].rearrange("p t d -> p (t d)")[:, bass.ds(g.outer * (2 * D) + g.inner * GW + t * D, GW)]
                        dve.tensor_tensor(out.rearrange("p (a j d) -> p a j d", a=2, j=2), o4[:, :, :, 0:HD0], inv,
                                          ALU.mult).then_inc(s_done, 1)

                def begin(first):
                    parts(0)
                    turned(0)
                    maxima(0)
                    parts(1)
                    turned(1)
                    probs_turned(0)
                    inverse(0)

                def step(cur, nxt, edge):
                    maxima(nxt.n)
                    parts(nxt.n + 1)
                    outputs(cur.n)
                    turned(nxt.n + 1)
                    probs_turned(nxt.n)
                    store(cur)
                    inverse(nxt.n)

                def finish(last):
                    outputs(last.n)
                    store(last)

                dve.memset(nmax[:, 0, :], 0.0).then_inc(s_done, 1)
                dve.wait_ge(s_done, 1)
                dve.wait_ge(s_zero, 2)
                pipelined(dve, B, NG0, begin, step, finish)
                dve.wait_ge(s_done, 2 * B * NG0 + 1)

            @block.tensor
            def _(pe):
                def turn(n):
                    for to, src in ((0, kd), (1, qd)):
                        pe.wait_ge(s_dl, 4 * n + 4)
                        for p in range(2):
                            for t in range(2):
                                last = pe.transpose(bank[to][:, p * S + t * P:p * S + (t + 1) * P],
                                                    src[:, t, 2 * p:2 * p + 2, :, :].rearrange("p h a d -> p (h a d)").bitcast(F32),
                                                    env.ident[:])
                        last.then_inc(s_T, 1)

                def scores(g):
                    pe.wait_ge(s_Ta, 2 * g.n + 2)
                    pe.wait_ge(s_Tv, g.n + 1)
                    for u in range(4):
                        p, t = u // 2, u % 2
                        wait_from_one(pe, s_pTa if u % 2 == 0 else s_pTv,
                                      2 * g.n + u // 2 - 1 if not isinstance(g.n, int) or g.n else 0)
                        pe.matmul(bank[4 + u][:], qT[:, p, tokens(t)], kT[:, p].rearrange("p j n -> p (j n)"),
                                  start=True, stop=False, skip_group_check=True)
                        for part in (mask_hi, mask_lo):
                            row = part[:].rearrange("p t n -> p (t n)")[:, bass.ds(g.outer * (2 * S) + t * S, S)]
                            last = pe.matmul(bank[4 + u][:].rearrange("p (j n) -> p j n", j=2), ident_r[:],
                                             row.unsqueeze(1).broadcast_to([P, 2, S]), start=False,
                                             stop=part is mask_lo, skip_group_check=True)
                        last.then_inc(s_s, 1)

                def turn_probs(n):
                    for u in range(4):
                        pe.wait_ge(s_exp, 8 * n + 2 * u + 2)
                        for k in range(2):
                            for j in range(2):
                                last = pe.transpose(pT_bank(u)[:, k, j, :], prob[:, u, j, k * P:(k + 1) * P], env.ident[:])
                        last.then_inc(s_pT, 1)

                def attend(n):
                    pe.wait_ge(s_v, 2 * n + 2)
                    pe.wait_ge(s_done, 2 * n + 1)
                    for p in range(2):
                        pe.wait_ge(s_pTa, 2 * n + p + 1)
                        pe.wait_ge(s_pTv, 2 * n + p + 1)
                        for k in range(2):
                            last = pe.matmul(bank[2 + p][:], vp[:, k].rearrange("p h d -> p (h d)"),
                                             pT[:, k, 2 * p:2 * p + 2, :].rearrange("p h n -> p (h n)"),
                                             start=k == 0, stop=k == 1)
                        last.then_inc(s_o, 1)

                def turn_back(n):
                    pe.wait_ge(s_oc, 4 * n + 4)
                    for t in range(2):
                        last = pe.transpose(bank[2][:, t * P:(t + 1) * P], oT[:, tokens(t)], env.ident[:])
                    last.then_inc(s_oT, 1)

                def begin(first):
                    turn(0)
                    scores(first)
                    turn(1)
                    turn_probs(0)

                def step(cur, nxt, edge):
                    scores(nxt)
                    attend(cur.n)
                    turn(nxt.n + 1)
                    turn_probs(nxt.n)
                    turn_back(cur.n)

                def finish(last):
                    attend(last.n)
                    turn_back(last.n)

                pipelined(pe, B, NG0, begin, step, finish)

        with ExitStack() as fin:
            oquant = Quant(env, "qa_oq", fin, NT, 2)
            oqT = env.sb("qa_oqT", [P, KD, TOK], BF16, fin)
            y = env.sb("qa_y", [P, NT, D], F32, fin)
            s_oTp, s_oT2, s_y, s_ys, s_add = (sem(n) for n in (
                "oqT_in_psum", "oqT_ready", "y_in_psum", "y_scaled", "residual_step"))
            block = fin.enter_context(nc.Block())

            @block.scalar
            def _(act):
                for n in range(2):
                    act.wait_ge(s_oTp, n + 1)
                    act.activation(oqT[:, :, n * 512:(n + 1) * 512],
                                   bank[n][:].bitcast(BF16).rearrange("p (k q) -> p k q", k=KD), ACT.Copy).then_inc(s_oT2, 1)

            @block.gpsimd
            def _(pool):
                pool.tensor_tensor(x[:], x[:], bias_rows[:, 3, :].unsqueeze(1).broadcast_to([P, NT, D]),
                                   ALU.add).then_inc(s_add, 1)
                pool.wait_ge(s_add, 1)
                for t in range(NT):
                    pool.wait_ge(s_ys, t + 1)
                    pool.tensor_tensor(x[:, t, :], x[:, t, :], y[:, t, :], ALU.add).then_inc(s_add, 1)
                pool.wait_ge(s_add, 1 + NT)

            @block.vector
            def _(dve):
                oquant.run(dve, o_tok[:])
                for t in range(NT):
                    dve.wait_ge(s_y, t // 2 * 2 + 2)
                    dve.scalar_tensor_tensor(y[:, t, :], half_banks(t), oquant.scale[:, t:t + 1], w_rows[:, 1, :],
                                             ALU.mult, ALU.mult).then_inc(s_ys, 1)

            @block.tensor
            def _(pe):
                turn_rows(pe, oquant, s_oTp)
                for t in range(NT):
                    pe.wait_ge(s_oT2, t // 4 + 1)
                    for k in range(KD):
                        last = pe.matmul(half_banks(t), oqT[:, k, tokens(t)], wT[:, 1, k, :], start=k == 0, stop=k == KD - 1)
                    last.then_inc(s_y, 1)


H1, HD1, RD = 16, 128, 64
QC, KVC = 96, 64
LOOKBACK = 8
FW = KVC + RD
LA_SCALE = 1.0 / math.sqrt(HD1 + RD)


class LatentSetup:

    def __init__(self, env, mem):
        self.e = env
        sb = lambda n, s, d=F32: env.sb(f"la_{n}", s, d, mem)
        sem = lambda n: env.sem(f"la_{n}")
        self.ctxT = sb("ctxT", [P, KD, TOK])
        self.w_kvc, self.w_dq = sb("w_kvc", [P, KD, KVC]), sb("w_dq", [P, KD, P])
        self.uqT, self.ukT = sb("uqT", [P, H1, QC]), sb("ukT", [P, H1, KVC])
        self.uvT2, self.wo = sb("uvT2", [P, H1, 2 * KVC]), sb("wo", [P, H1, D])
        self.qr = sb("qr", [QC, H1, RD])
        self.key_w = sb("key_w", [KVC, FW])
        self.key_cos, self.key_sin = sb("key_cos", [P, 2, RD]), sb("key_sin", [P, 2, RD])
        self.seg_i, self.key_id = sb("seg_i", [P, NT], I32), sb("key_id", [P, S])
        self.s_seg, self.s_in = sem("seg_loaded"), sem("inputs_loaded")
        self.seg_loads = [(self.seg_i, "seg"), (self.key_id, "key_id")]
        self.loads = [(self.w_kvc, "w_kvc"), (self.key_w, "key_w"), (self.key_cos, "la_cos"), (self.key_sin, "la_sin"),
                      (self.qr, "qr"), (self.w_dq, "w_dq"), (self.uqT, "uqT"), (self.ukT, "ukT"), (self.uvT2, "uvT2"),
                      (self.wo, "la_wo")]
        self.n_in = 16 * len(self.loads)

    def sync_load(self, sp):
        for dst, name in self.seg_loads:
            sp.dma_start(dst[:], self.e.dram[name]).then_inc(self.s_seg, 16)
        for dst, name in self.loads:
            sp.dma_start(dst[:], self.e.dram[name]).then_inc(self.s_in, 16)

    def keep(self, mem):
        env = self.e
        sb = lambda n, s, d=F32: env.sb(f"la_{n}", s, d, mem)
        self.keys = sb("keys", [P, NT, FW])
        self.bias = sb("bias", [P, NT, S], BF16)
        self.vals = sb("vals", [P, NT, 2, KVC], F32R)
        self.wa_hi, self.wa_lo = sb("wa_hi", [QC, H1, FW], F32R), sb("wa_lo", [QC, H1, FW], F32R)
        self.c_hi, self.c_lo = sb("c_hi", [P, H1, D], F32R), sb("c_lo", [P, H1, D], F32R)

    def begin(self, mem):
        env = self.e
        sb = lambda n, s, d=F32: env.sb(f"la_{n}", s, d, mem)
        sem = lambda n: env.sem(f"la_{n}")
        self.kvcT = sb("kvcT", [KVC, TOK])
        self.turn_a, self.turn_b = sb("turn_a", [P, NT, RD]), sb("turn_b", [P, NT, RD])
        self.seg, self.seg_low = sb("seg", [P, NT]), sb("seg_low", [P, NT])
        self.s_bias = sem("bias_step")
        self.exact = [sb(f"exact{i}", [P, 512]) for i in range(2)]
        self.s_kvT, self.s_kvTc, self.s_key, self.s_keyc = (sem(n) for n in (
            "kv_cT_in_psum", "kv_cT_copied", "keys_in_psum", "keys_copied"))
        self.s_turn, self.s_vhi, self.s_vlo = sem("keys_turned"), sem("vals_hi_ready"), sem("vals_lo_ready")
        self.s_qrs, self.s_qrh, self.s_qrl = sem("qr_scaled"), sem("qr_hi_ready"), sem("qr_lo_ready")
        self.s_p, self.s_pe, self.s_ph, self.s_pl = (sem(n) for n in (
            "product_in_psum", "product_copied", "product_hi_ready", "product_lo_ready"))

    PRODUCTS = 12

    def bank(self, n):
        return self.e.bank[n % 4]

    def product(self, n):
        if n < 4:
            heads = slice(4 * n, 4 * n + 4)
            view = lambda v: v[0:QC, 0:4 * KVC].rearrange("p (h c) -> p h c", h=4)
            return view(self.bank(n)[:]), view(self.exact[n % 2][:]), self.wa_hi[:, heads, 0:KVC], \
                self.wa_lo[:, heads, 0:KVC], LA_SCALE
        heads = slice(2 * n - 8, 2 * n - 6)
        view = lambda v: v.rearrange("p (h d) -> p h d", h=2)
        return view(self.bank(n)[:]), view(self.exact[n % 2][:]), self.c_hi[:, heads, :], self.c_lo[:, heads, :], 1.0

    def tensor_latent(self, pe):
        pe.wait_ge(self.s_in, self.n_in)
        for c in range(2):
            for k in range(KD):
                last = pe.matmul(self.bank(c)[0:KVC, :], self.w_kvc[:, k, :], self.ctxT[:, k, c * 512:(c + 1) * 512],
                                 start=k == 0, stop=k == KD - 1)
            last.then_inc(self.s_kvT, 1)

    def tensor_keys(self, pe):
        pe.wait_ge(self.s_kvTc, 2)
        for t in range(NT):
            last = pe.matmul(self.bank(2 + t // 4)[:, (t % 4) * FW:(t % 4 + 1) * FW], self.kvcT[:, tokens(t)], self.key_w[:],
                             start=True, stop=True)
            if t % 4 == 3:
                last.then_inc(self.s_key, 1)

    def tensor_products(self, pe):
        for n in range(self.PRODUCTS):
            if n == 2:
                pe.wait_ge(self.s_keyc, 2)
            if n >= 4:
                pe.wait_ge(self.s_ph, n - 3)
            if n < 4:
                for j in range(4):
                    h = 4 * n + j
                    last = pe.matmul(self.bank(n)[0:QC, j * KVC:(j + 1) * KVC], self.uqT[:, h, :], self.ukT[:, h, :],
                                     start=True, stop=True)
            else:
                for j in range(2):
                    h = 2 * n - 8 + j
                    last = pe.matmul(self.bank(n)[:, j * D:(j + 1) * D], self.uvT2[:, h, :], self.wo[:, h, :],
                                     start=True, stop=True)
            last.then_inc(self.s_p, 1)
        pe.wait_ge(self.s_ph, self.PRODUCTS)

    def scalar_weights(self, act):
        act.wait_ge(self.s_in, self.n_in)
        act.activation(self.qr[:], self.qr[:], ACT.Copy, scale=LA_SCALE).then_inc(self.s_qrs, 1)
        act.wait_ge(self.s_qrs, 1)
        act.activation(self.wa_hi[:, :, KVC:], self.qr[:], ACT.Copy).then_inc(self.s_qrh, 1)

    def scalar_latent(self, act):
        for c in range(2):
            act.wait_ge(self.s_kvT, c + 1)
            act.activation(self.kvcT[:, c * 512:(c + 1) * 512], self.bank(c)[0:KVC, :], ACT.Copy).then_inc(self.s_kvTc, 1)

    def scalar_keys(self, act):
        for n in range(2):
            act.wait_ge(self.s_key, n + 1)
            act.activation(self.keys[:, 4 * n:4 * n + 4, :], self.bank(2 + n)[:].rearrange("p (t f) -> p t f", t=4),
                           ACT.Copy).then_inc(self.s_keyc, 1)
        act.wait_ge(self.s_keyc, 2)
        act.activation(self.vals[:, :, 0, :], self.keys[:, :, 0:KVC], ACT.Copy).then_inc(self.s_vhi, 1)

    def scalar_products(self, act):
        for n in range(self.PRODUCTS):
            src, exact, hi, _, scale = self.product(n)
            act.wait_ge(self.s_p, n + 1)
            if n >= 2:
                act.wait_ge(self.s_pl, n - 1)
            act.activation(exact, src, ACT.Copy, scale=scale).then_inc(self.s_pe, 1)
            act.activation(hi, src, ACT.Copy, scale=scale).then_inc(self.s_ph, 1)

    def vector_bias(self, dve):
        s = self.s_bias
        dve.wait_ge(self.s_seg, 32)
        dve.tensor_copy(self.seg[:], self.seg_i[:]).then_inc(s, 1)
        dve.wait_ge(s, 1)
        dve.tensor_scalar(self.seg_low[:], self.seg[:], float(-LOOKBACK), None, ALU.add).then_inc(s, 1)
        for t in range(NT):
            dve.tensor_scalar(self.bias[:, t, :], self.key_id[:], self.seg[:, t:t + 1], None, ALU.is_le).then_inc(s, 1)
        dve.wait_ge(s, 2 + NT)
        for t in range(NT):
            dve.scalar_tensor_tensor(self.bias[:, t, :], self.key_id[:], self.seg_low[:, t:t + 1],
                                     self.bias[:, t, :], ALU.is_ge, ALU.mult).then_inc(s, 1)
        dve.wait_ge(s, 2 + 2 * NT)
        dve.tensor_scalar(self.bias[:], self.bias[:], -1.0, -NEG, ALU.add, ALU.mult).then_inc(s, 1)
        dve.wait_ge(s, 3 + 2 * NT)

    def gpsimd_keys(self, pool):
        half = RD // 2
        pool.wait_ge(self.s_qrh, 1)
        pool.tensor_tensor(self.wa_lo[:, :, KVC:], self.qr[:], self.wa_hi[:, :, KVC:].bitcast(F32),
                           ALU.subtract).then_inc(self.s_qrl, 1)
        pool.wait_ge(self.s_keyc, 2)
        by_batch = lambda v: v[:].rearrange("p (b t) f -> p b t f", t=2)
        k4, a4, b4 = by_batch(self.keys), by_batch(self.turn_a), by_batch(self.turn_b)
        for t in range(2):
            cs = lambda v, lo, n: v[:, t, lo:lo + n].unsqueeze(1).broadcast_to([P, B, n])
            pool.tensor_tensor(a4[:, :, t, :], k4[:, :, t, KVC:], cs(self.key_cos, 0, RD), ALU.mult).then_inc(self.s_turn, 1)
            pool.tensor_tensor(b4[:, :, t, 0:half], k4[:, :, t, KVC + half:], cs(self.key_sin, 0, half),
                               ALU.mult).then_inc(self.s_turn, 1)
            pool.tensor_tensor(b4[:, :, t, half:], k4[:, :, t, KVC:KVC + half], cs(self.key_sin, half, half),
                               ALU.mult).then_inc(self.s_turn, 1)
        pool.wait_ge(self.s_vhi, 1)
        pool.tensor_tensor(self.vals[:, :, 1, :], self.keys[:, :, 0:KVC], self.vals[:, :, 0, :].bitcast(F32),
                           ALU.subtract).then_inc(self.s_vlo, 1)
        pool.wait_ge(self.s_turn, 6)
        pool.tensor_tensor(self.keys[:, :, KVC:], self.turn_a[:], self.turn_b[:], ALU.add).then_inc(self.s_turn, 1)
        pool.wait_ge(self.s_turn, 7)
        pool.wait_ge(self.s_vlo, 1)

    def gpsimd_products(self, pool):
        for n in range(self.PRODUCTS):
            _, exact, hi, lo, _ = self.product(n)
            pool.wait_ge(self.s_pe, n + 1)
            pool.wait_ge(self.s_ph, n + 1)
            pool.tensor_tensor(lo, exact, hi.bitcast(F32), ALU.subtract).then_inc(self.s_pl, 1)
        pool.wait_ge(self.s_pl, self.PRODUCTS)
        pool.wait_ge(self.s_qrl, 1)
GOLDEN_CENTER = 1.0 / math.e
GOLDEN_LOWER = 0.5 - math.log(4.0 / 3.0)
GOLDEN_UPPER = 0.5


I = 128
CH = 512
NC = TOK // CH
RW = 33


def experts(env, tag, layer, latent=None):
    nc, dram, x = env.nc, env.dram, env.x
    E = 8 if layer == 0 else 32
    UNITS = 16 if layer == 0 else 33
    LOOPS = 7 if layer == 0 else 15
    weights = dram[f"{tag}_weights"]
    WCOLS = 2 * KD * I + D

    with ExitStack() as mem:
        sb = lambda n, s, d=F32: env.sb(f"{tag}_{n}", s, d, mem)
        sem = lambda n: env.sem(f"{tag}_{n}")
        rms_w = sb("rms_w", [P, D]) if layer else None
        norm = Norm(env, tag, mem, rms_w)
        h_hi, h_lo = sb("h_hi", [P, KD, TOK], F32R), sb("h_lo", [P, KD, TOK], F32R)
        wr = sb("wr", [P, KD, P])
        wr_hi, wr_lo = sb("wr_hi", [P, KD, P], F32R), sb("wr_lo", [P, KD, P], F32R)
        rt_bias = sb("rt_bias", [P, 32])
        logitT = sb("logitT", [32, TOK])
        NS = 8 if layer == 0 else RW
        sel = sb("sel", [3 * RW, NS * P], BF16)
        score = sb("score", [P, NT, 32])
        wfull = sb("wfull", [P, NT, RW])
        wpart = sb("wpart", [P, NT, 3, RW], BF16)
        wrest = sb("wrest", [P, NT, RW])
        wT = sb("wT", [3 * RW, TOK], BF16)
        stage = [sb(f"stage{j}", [P, WCOLS]) for j in range(2)]
        w_hi = [sb(f"w_hi{j}", [P, WCOLS], F32R) for j in range(2)]
        w_lo = [sb(f"w_lo{j}", [P, WCOLS], F32R) for j in range(2)]
        sg = sb("silu_gate", [P, CH])
        gu = sb("gate_up", [P, CH])
        act_f = sb("act_f", [P, CH])
        act_hi = [sb(f"act_hi{c}", [P, CH], F32R) for c in range(NC)]
        act_lo = [sb(f"act_lo{c}", [P, CH], F32R) for c in range(NC)]
        zero = sb("zero", [P, CH], BF16)
        total, no_expert = sb("total", [P, NT]), sb("no_expert", [P, NT])
        if layer == 0:
            dist, zone, rank = (sb(n, [P, NT, E]) for n in ("dist", "zone", "rank"))
            in_zone_w, fallback = sb("in_zone_w", [P, NT, E]), sb("fallback", [P, NT, E])
            pairs, before = sb("pairs", [P, NT, E, E]), sb("before", [P, E, E])
        else:
            best = sb("best", [P, NT, 8])

        s_const, s_wr, s_stage = sem("const_loaded"), sem("wr_split"), [sem(f"stage_loaded{j}") for j in range(2)]
        s_lg, s_lgc, s_lgt = sem("logitsT_in_psum"), sem("logitsT_copied"), sem("logits_in_psum")
        s_sc, s_step, s_z = sem("scores_ready"), sem("route_step"), sem("logits_scaled")
        s_dist, s_ex = sem("distance_ready"), sem("route_exps_ready")
        s_wpart, s_wTp, s_wT = sem("w_parts_ready"), sem("wT_in_psum"), sem("wT_ready")
        s_hi, s_lo = sem("unit_hi_ready"), sem("unit_lo_ready")
        s_gate, s_up, s_wb = sem("gate_in_psum"), sem("up_in_psum"), sem("w_rows_in_psum")
        s_sg, s_gu, s_act = sem("silu_ready"), sem("gate_up_ready"), sem("act_ready")
        s_ahi, s_alo = sem("act_hi_ready"), sem("act_lo_ready")
        s_down, s_zero, s_zd = sem("down_done"), sem("zero_ready"), sem("y_zeroed")
        s_add, s_twice = sem("residual_added"), sem("input_added_again")

        Y = env.bank[0:4]
        GATE, UP, WB, X7 = env.bank[4:8]
        gate_w = lambda w, k: w[:, k * I:(k + 1) * I]
        up_w = lambda w, k: w[:, (KD + k) * I:(KD + k + 1) * I]
        down_w = lambda w: w[:, 2 * KD * I:]
        if latent is not None:
            latent.begin(mem)
        block = mem.enter_context(nc.Block())

        @block.sync
        def _(sp):
            sp.dma_start(wr[:], dram[f"{tag}_wr"]).then_inc(s_const, 16)
            sp.dma_start(rt_bias[:], dram[f"{tag}_route"]).then_inc(s_const, 16)
            if layer:
                sp.dma_start(rms_w[:], dram["ln2_rows"]).then_inc(s_const, 16)
            else:
                sp.dma_start(before[:], dram["before"]).then_inc(s_const, 16)
            sp.dma_start(sel[:], dram["sel"][:, 0:NS * P]).then_inc(s_const, 16)
            for j in range(2):
                sp.dma_start(stage[j][:], weights[j]).then_inc(s_stage[j], 16)

            def load(u, j, it):
                sp.wait_ge(s_hi, 2 * it + j + 1)
                sp.wait_ge(s_lo, 2 * it + j + 1)
                sp.dma_start(stage[j][:], weights[u]).then_inc(s_stage[j], 16)

            with sp.Fori(0, (UNITS - 2) // 2) as it:
                for j in range(2):
                    load(2 * it + 2 + j, j, it)
            if UNITS % 2:
                load(UNITS - 1, 0, (UNITS - 3) // 2)

        n_const = 64

        @block.gpsimd
        def _(pool):
            if layer:
                pool.wait_ge(s_const, n_const)
            norm.gpsimd_rstd(pool)
            pool.wait_ge(s_wr, 1)
            pool.tensor_tensor(wr_lo[:], wr[:], wr_hi[:].bitcast(F32), ALU.subtract).then_inc(s_wr, 1)

            def lo_half(u, j, it):
                pool.wait_ge(s_hi, u + 1)
                if it is not None:
                    pool.wait_ge(s_down, 4 * it + 2 * j + 2)
                pool.tensor_tensor(w_lo[j][:], stage[j][:], w_hi[j][:].bitcast(F32),
                                   ALU.subtract).then_inc(s_lo, 1)

            for j in range(2):
                lo_half(j, j, None)
            if latent is not None:
                latent.gpsimd_keys(pool)
                latent.gpsimd_products(pool)
            with pool.Fori(0, (UNITS - 2) // 2) as it:
                for j in range(2):
                    lo_half(2 * it + 2 + j, j, it)
            if UNITS % 2:
                lo_half(UNITS - 1, 0, (UNITS - 3) // 2)

        @block.scalar
        def _(act):
            if layer:
                norm.scalar_stats(act)
            act.wait_ge(s_const, n_const)
            act.activation(wr_hi[:], wr[:], ACT.Copy).then_inc(s_wr, 1)

            def hi_half(u, j, it, n):
                act.wait_ge(s_stage[j], 16 * n)
                if it is not None:
                    act.wait_ge(s_down, 4 * it + 2 * j + 2)
                act.activation(w_hi[j][:], stage[j][:], ACT.Copy).then_inc(s_hi, 1)

            if latent is not None:
                latent.scalar_weights(act)
                latent.scalar_latent(act)
            for j in range(2):
                hi_half(j, j, None, 1)
            norm.scalar_hi(act, [GATE, UP], h_hi)
            if latent is not None:
                latent.scalar_keys(act)
            for c in range(NC):
                act.wait_ge(s_lg, c + 1)
                act.activation(logitT[:, c * CH:(c + 1) * CH], [WB, X7][c][0:32, :], ACT.Copy).then_inc(s_lgc, 1)
            if layer == 0:
                act.wait_ge(s_z, 1)
                act.activation(score[:, :, 0:E], score[:, :, 0:E], ACT.Sigmoid).then_inc(s_sc, 1)
                act.wait_ge(s_dist, 1)
                act.activation(in_zone_w[:], dist[:], ACT.Exp, scale=-1.0 / 0.1).then_inc(s_ex, 1)
                act.activation(fallback[:], dist[:], ACT.Exp, scale=-1.0 / 0.3).then_inc(s_ex, 1)
                latent.scalar_products(act)
            else:
                act.wait_ge(s_lgt, 1)
                act.activation(score[:], env.bank[4][:, 0:NT * 32].rearrange("p (t e) -> p t e", e=32),
                               ACT.Sigmoid).then_inc(s_sc, 1)

            def unit(n):
                n, c = n
                act.wait_ge(s_gate, n + 1)
                wait_from_one(act, s_gu, n)
                act.activation(sg[:], GATE[:], ACT.Silu).then_inc(s_sg, 1)
                act.wait_ge(s_act, n + 1)
                act.activation(act_hi[c][:], act_f[:], ACT.Copy).then_inc(s_ahi, 1)

            run_units(act, unit, hi_half, LOOPS, UNITS)

        @block.vector
        def _(dve):
            if layer:
                dve.wait_ge(s_const, n_const)
            norm.vector_normalise(dve)
            norm.vector_lo(dve, [GATE, UP], h_hi, h_lo)
            dve.memset(zero[:], 0.0).then_inc(s_zero, 1)
            if layer:
                dve.tensor_tensor(x[:], x[:], env.x_in[:], ALU.add).then_inc(s_twice, 1)
            taken = [0]

            def link(ins):
                taken[0] += 1
                ins.then_inc(s_step, 1)
                dve.wait_ge(s_step, taken[0])

            row = lambda v, n: v.unsqueeze(2).broadcast_to([P, NT, n])
            if layer == 0:
                inh, e8 = score[:, :, 0:E], [P, NT, E, E]
                by_j = lambda v: v.unsqueeze(2).broadcast_to(e8)
                by_e = lambda v: v.unsqueeze(3).broadcast_to(e8)
                dve.wait_ge(s_const, n_const)
                link(dve.reciprocal(total[:, 0:1], rt_bias[:, 0:1]))
                dve.wait_ge(s_lgt, 1)
                dve.tensor_scalar(inh, GATE[:, 0:NT * 32].rearrange("p (t e) -> p t e", e=32)[:, :, 0:E],
                                  total[:, 0:1], None, ALU.mult).then_inc(s_z, 1)
                dve.wait_ge(s_sc, 1)
                link(dve.tensor_scalar(dist[:], inh, GOLDEN_CENTER, None, ALU.subtract))
                link(dve.scalar_tensor_tensor(dist[:], dist[:], -1.0, dist[:], ALU.mult, ALU.max))
                dve.tensor_scalar(zone[:], inh, GOLDEN_LOWER, None, ALU.is_ge).then_inc(s_dist, 1)
                dve.wait_ge(s_dist, 1)
                link(dve.scalar_tensor_tensor(zone[:], inh, GOLDEN_UPPER, zone[:], ALU.is_le, ALU.mult))
                dve.wait_ge(s_ex, 2)
                link(dve.tensor_tensor(in_zone_w[:], in_zone_w[:], zone[:], ALU.mult))
                link(dve.tensor_reduce(total[:], in_zone_w[:], AX_X, ALU.add))
                link(dve.tensor_scalar(no_expert[:], total[:], 1e-8, None, ALU.is_lt))
                link(dve.tensor_tensor(pairs[:], by_j(fallback[:]), by_e(fallback[:]), ALU.is_gt))
                link(dve.tensor_reduce(rank[:], pairs[:], AX_X, ALU.add))
                link(dve.tensor_tensor(pairs[:], by_j(fallback[:]), by_e(fallback[:]), ALU.is_equal))
                link(dve.tensor_tensor(pairs[:], pairs[:], before[:].unsqueeze(1).broadcast_to(e8), ALU.mult))
                link(dve.tensor_reduce(dist[:], pairs[:], AX_X, ALU.add))
                link(dve.tensor_tensor(rank[:], rank[:], dist[:], ALU.add))
                link(dve.scalar_tensor_tensor(fallback[:], rank[:], 1.5, fallback[:], ALU.is_lt, ALU.mult))
                link(dve.tensor_reduce(total[:], fallback[:], AX_X, ALU.add))
                link(dve.tensor_scalar(total[:], total[:], 1e-8, None, ALU.max))
                link(dve.reciprocal(total[:], total[:]))
                link(dve.tensor_tensor(total[:], total[:], no_expert[:], ALU.mult))
                link(dve.tensor_tensor(fallback[:], fallback[:], row(total[:], E), ALU.mult))
                link(dve.tensor_scalar(no_expert[:], no_expert[:], -1.0, 1.0, ALU.mult, ALU.add))
                link(dve.tensor_tensor(in_zone_w[:], in_zone_w[:], row(no_expert[:], E), ALU.mult))
                link(dve.tensor_tensor(in_zone_w[:], in_zone_w[:], fallback[:], ALU.add))
                link(dve.tensor_reduce(total[:], in_zone_w[:], AX_X, ALU.add))
                link(dve.tensor_scalar(total[:], total[:], 1e-8, None, ALU.max))
                link(dve.reciprocal(total[:], total[:]))
                link(dve.memset(wfull[:], 0.0))
                link(dve.tensor_tensor(wfull[:, :, 0:E], in_zone_w[:], row(total[:], E), ALU.mult))
            else:
                dve.wait_ge(s_sc, 1)
                link(dve.tensor_tensor(wrest[:, :, 0:E], score[:], rt_bias[:].unsqueeze(1).broadcast_to([P, NT, E]),
                                       ALU.add))
                for t in range(NT):
                    dve.max(best[:, t, :], wrest[:, t, 0:E]).then_inc(s_z, 1)
                dve.wait_ge(s_z, NT)
                for t in range(NT):
                    last = dve.match_replace(wfull[:, t, 0:E], best[:, t, :], wrest[:, t, 0:E], NEG)
                    last.then_inc(s_dist, 1)
                dve.wait_ge(s_dist, NT)
                link(dve.tensor_tensor(wrest[:, :, 0:E], wrest[:, :, 0:E], wfull[:, :, 0:E], ALU.not_equal))
                link(dve.tensor_tensor(score[:], score[:], wrest[:, :, 0:E], ALU.mult))
                link(dve.tensor_reduce(total[:], score[:], AX_X, ALU.add))
                link(dve.reciprocal(total[:], total[:]))
                link(dve.tensor_tensor(wfull[:, :, 0:E], score[:], row(total[:], E), ALU.mult))
                link(dve.memset(wfull[:, :, E:E + 1], 1.0))
            steps = [0]

            def step(ins):
                steps[0] += 1
                ins.then_inc(s_wpart, 1)
                dve.wait_ge(s_wpart, steps[0])

            step(dve.tensor_copy(wpart[:, :, 0, :], wfull[:]))
            step(dve.tensor_tensor(wrest[:], wfull[:], wpart[:, :, 0, :], ALU.subtract))
            step(dve.tensor_copy(wpart[:, :, 1, :], wrest[:]))
            step(dve.tensor_tensor(wfull[:], wrest[:], wpart[:, :, 1, :], ALU.subtract))
            step(dve.tensor_copy(wpart[:, :, 2, :], wfull[:]))
            for h in range(2):
                dve.wait_ge(s_wTp, h + 1)
                dve.tensor_copy(wT[:, h * CH:(h + 1) * CH],
                                [WB, X7][h][:].bitcast(BF16)[0:3 * RW, 0:CH]).then_inc(s_wT, 1)
            if latent is not None:
                latent.vector_bias(dve)

            def unit(n):
                n, c = n
                dve.wait_ge(s_up, n + 1)
                dve.wait_ge(s_sg, n + 1)
                dve.tensor_tensor(gu[:], UP[:], sg[:], ALU.mult).then_inc(s_gu, 1)
                dve.wait_ge(s_wb, n + 1)
                dve.wait_ge(s_gu, n + 1)
                dve.tensor_tensor(act_f[:], WB[:], gu[:], ALU.mult).then_inc(s_act, 1)
                dve.wait_ge(s_ahi, n + 1)
                dve.tensor_tensor(act_lo[c][:], act_f[:], act_hi[c][:].bitcast(F32),
                                  ALU.subtract).then_inc(s_alo, 1)

            run_units(dve, unit, None, LOOPS, UNITS)
            if layer:
                dve.wait_ge(s_twice, 1)
            dve.wait_ge(s_down, NC * UNITS)
            for g in range(NT // 2):
                dve.tensor_tensor(x[:, 2 * g:2 * g + 2, :], Y[g][:].rearrange("p (t d) -> p t d", t=2),
                                  x[:, 2 * g:2 * g + 2, :], ALU.add).then_inc(s_add, 1)
            dve.wait_ge(s_add, NT // 2)

        @block.tensor
        def _(pe):
            if latent is not None:
                latent.tensor_latent(pe)
            norm.tensor_transpose(pe, [GATE, UP])
            if latent is not None:
                latent.tensor_keys(pe)
            pe.wait_ge(s_wr, 2)
            for c in range(NC):
                pe.wait_ge(norm.s_lo, 2 * c + 2)
                cols = slice(c * CH, (c + 1) * CH)
                for k in range(KD):
                    last = split3(pe, [WB, X7][c][:], (wr_hi[:, k, :], wr_lo[:, k, :]),
                                  (h_hi[:, k, cols], h_lo[:, k, cols]), k == 0, k == KD - 1)
                last.then_inc(s_lg, 1)
            pe.wait_ge(s_lgc, 2)
            pe.wait_ge(norm.s_lo, B)
            for t in range(NT):
                last = pe.transpose(GATE[:, t * 32:(t + 1) * 32], logitT[:, tokens(t)], env.ident[0:32, 0:32])
            last.then_inc(s_lgt, 1)
            if latent is not None:
                latent.tensor_products(pe)
            pe.wait_ge(s_zero, 1)
            for g in range(NT // 2):
                last = pe.matmul(Y[g][:], zero[:, 0:P], zero[:], start=True, stop=True)
            last.then_inc(s_zd, 1)
            pe.wait_ge(s_wpart, 5)
            pe.wait_ge(s_lgc, 2)
            for h in range(2):
                for q in range(4):
                    t = 4 * h + q
                    last = pe.transpose([WB, X7][h][:].bitcast(BF16)[0:3 * RW, q * P:(q + 1) * P],
                                        wpart[:, t, :, :].rearrange("p a e -> p (a e)"), env.ident_bf[:])
                last.then_inc(s_wTp, 1)
            pe.wait_ge(s_wT, 2)
            pe.wait_ge(s_sc, 1)

            def up_part(u, c, j, n, e):
                cols = slice(c * CH, (c + 1) * CH)
                h = [(h_hi[:, k, cols], h_lo[:, k, cols]) for k in range(KD)]
                if c == 0:
                    pe.wait_ge(s_lo, u + 1)
                wait_from_one(pe, s_sg, n)
                for k in range(KD):
                    last = split3(pe, GATE[:], (gate_w(w_hi[j], k), gate_w(w_lo[j], k)), h[k], k == 0, k == KD - 1)
                last.then_inc(s_gate, 1)
                wait_from_one(pe, s_gu, n)
                for k in range(KD):
                    last = split3(pe, UP[:], (up_w(w_hi[j], k), up_w(w_lo[j], k)), h[k], k == 0, k == KD - 1)
                last.then_inc(s_up, 1)
                wait_from_one(pe, s_act, n)
                pe.matmul(WB[:], sel[:, bass.ds(e * P, P)], wT[:, cols], start=True, stop=True).then_inc(s_wb, 1)

            def down_part(c, j, n):
                pe.wait_ge(s_alo, n + 1)
                for q in range(CH // P):
                    t = c * (CH // P) + q
                    last = split3(pe, Y[t // 2][:, (t % 2) * D:(t % 2 + 1) * D],
                                  (act_hi[c][:, tokens(q)], act_lo[c][:, tokens(q)]),
                                  (down_w(w_hi[j]), down_w(w_lo[j])), False, False)
                last.then_inc(s_down, 1)

            of = (lambda it, j: it) if layer == 0 else (lambda it, j: 2 * it + j)
            up_part(0, 0, 0, 0, 0)
            with pe.Fori(0, LOOPS) as it:
                for j in range(2):
                    u = 2 * it + j
                    up_part(u, 1, j, 2 * u + 1, of(it, j))
                    down_part(0, j, 2 * u)
                    nxt = (of(it, 1) if j == 0 else of(it + 1, 0))
                    up_part(u + 1, 0, 1 - j, 2 * u + 2, nxt)
                    down_part(1, j, 2 * u + 1)
            for u in range(2 * LOOPS, UNITS):
                j = u % 2
                e = u // 2 if layer == 0 else u
                up_part(u, 1, j, 2 * u + 1, e)
                down_part(0, j, 2 * u)
                if u + 1 < UNITS:
                    up_part(u + 1, 0, 1 - j, 2 * u + 2, (u + 1) // 2 if layer == 0 else u + 1)
                down_part(1, j, 2 * u + 1)


def run_units(eng, unit, refill, loops, units):
    unit((0, 0))
    with eng.Fori(0, loops) as it:
        for j in range(2):
            n = 2 * (2 * it + j)
            unit((n + 1, 1))
            unit((n + 2, 0))
            if refill is not None:
                refill(2 * it + 2 + j, j, it, it + 2)
    for u in range(2 * loops, units):
        unit((2 * u + 1, 1))
        if u + 1 < units:
            unit((2 * u + 2, 0))
        if refill is not None and u + 2 < units:
            refill(u + 2, u % 2, u // 2, u // 2 + 2)
HG = 4
NG = H1 // HG


def latent_attention(env, setup):
    nc, x = env.nc, env.x
    keys, vals, bias, key_cos, key_sin = setup.keys, setup.vals, setup.bias, setup.key_cos, setup.key_sin
    wa_hi, wa_lo, c_hi, c_lo, w_dq = setup.wa_hi, setup.wa_lo, setup.c_hi, setup.c_lo, setup.w_dq
    with ExitStack() as mem:
        sb = lambda n, s, d=F32: env.sb(f"la_{n}", s, d, mem)
        sem = lambda n: env.sem(f"la_{n}")
        bank = env.bank
        kT_hi, kT_lo = sb("kT_hi", [P, TOK], F32R), sb("kT_lo", [P, TOK], F32R)
        qcT_hi, qcT_lo = sb("qcT_hi", [QC, TOK], F32R), sb("qcT_lo", [QC, TOK], F32R)
        s_wdq = sem("w_dq_split")
        s_kTp, s_kTh, s_kTl = sem("kT_in_psum"), sem("kT_hi_ready"), sem("kT_lo_ready")
        s_qcp, s_qch, s_qcl = sem("q_cT_in_psum"), sem("q_cT_hi_ready"), sem("q_cT_lo_ready")
        s_qslot, s_vslot = sem("batch_queries_ready"), sem("batch_values_ready")
        s_q, s_qc, s_rot, s_roped = sem("q_in_psum"), sem("q_copied"), sem("q_rotated"), sem("q_roped")
        s_qT, s_qTh, s_qTl = sem("qT_in_psum"), sem("qT_hi_ready"), sem("qT_lo_ready")
        s_s, s_max, s_exp, s_inv, s_prob = (sem(n) for n in (
            "scores_in_psum", "max_ready", "exp_ready", "row_inverse_ready", "prob_ready"))
        s_pT, s_pTh, s_pTl = sem("pT_in_psum"), sem("pT_hi_ready"), sem("pT_lo_ready")
        s_o, s_oh, s_ol = sem("oT_in_psum"), sem("oT_hi_ready"), sem("oT_lo_ready")
        s_y, s_add = sem("y_in_psum"), sem("residual_added")
        half = RD // 2
        with ExitStack() as prep:
            sb = lambda n, s, d=F32: env.sb(f"la_{n}", s, d, prep)
            norm = Norm(env, "la", prep)
            w_dq_hi, w_dq_lo = sb("w_dq_hi", [P, KD, P], F32R), sb("w_dq_lo", [P, KD, P], F32R)
            h_hi, h_lo = sb("h_hi", [P, KD, TOK], F32R), sb("h_lo", [P, KD, TOK], F32R)
            credit = sb("credit", [P, 1])
            block = prep.enter_context(nc.Block())

            @block.gpsimd
            def _(pool):
                pool.wait_ge(s_wdq, 1)
                pool.tensor_tensor(w_dq_lo[:], w_dq[:], w_dq_hi[:].bitcast(F32), ALU.subtract).then_inc(s_wdq, 1)
                norm.gpsimd_rstd(pool)

            @block.scalar
            def _(act):
                act.activation(w_dq_hi[:], w_dq[:], ACT.Copy).then_inc(s_wdq, 1)
                for n in range(2):
                    act.wait_ge(s_kTp, n + 1)
                    act.activation(kT_hi[:, n * 512:(n + 1) * 512], bank[4 + n][:], ACT.Copy).then_inc(s_kTh, 1)
                norm.scalar_hi(act, bank[0:2], h_hi)
                for c in range(2):
                    act.wait_ge(s_qcp, c + 1)
                    act.activation(qcT_hi[:, c * 512:(c + 1) * 512], bank[2 + c][0:QC, :], ACT.Copy).then_inc(s_qch, 1)

            @block.vector
            def _(dve):
                norm.vector_normalise(dve)
                norm.vector_lo(dve, bank[0:2], h_hi, h_lo)
                for n in range(2):
                    dve.wait_ge(s_kTh, n + 1)
                    cols = slice(n * 512, (n + 1) * 512)
                    dve.tensor_tensor(kT_lo[:, cols], bank[4 + n][:], kT_hi[:, cols].bitcast(F32),
                                      ALU.subtract).then_inc(s_kTl, 1)
                for c in range(2):
                    dve.wait_ge(s_qch, c + 1)
                    cols = slice(c * 512, (c + 1) * 512)
                    dve.tensor_tensor(qcT_lo[:, cols], bank[2 + c][0:QC, :], qcT_hi[:, cols].bitcast(F32),
                                      ALU.subtract).then_inc(s_qcl, 1)
                dve.memset(credit[:], 0.0).then_inc(s_add, 1)

            @block.tensor
            def _(pe):
                for n in range(2):
                    for j in range(4):
                        last = pe.transpose(bank[4 + n][:, j * P:(j + 1) * P], keys[:, 4 * n + j, :], env.ident[:])
                    last.then_inc(s_kTp, 1)
                norm.tensor_transpose(pe, bank[0:2])
                pe.wait_ge(s_wdq, 2)
                for c in range(2):
                    pe.wait_ge(norm.s_lo, 2 * c + 2)
                    cols = slice(c * 512, (c + 1) * 512)
                    for k in range(KD):
                        last = split3(pe, bank[2 + c][:], (w_dq_hi[:, k, :], w_dq_lo[:, k, :]),
                                      (h_hi[:, k, cols], h_lo[:, k, cols]), k == 0, k == KD - 1)
                    last.then_inc(s_qcp, 1)
                pe.wait_ge(s_kTl, 2)
                pe.wait_ge(s_qcl, 2)

        sb = lambda n, s, d=F32: env.sb(f"la_{n}", s, d, mem)
        qs_hi, qs_lo = sb("qs_hi", [QC, S], F32R), sb("qs_lo", [QC, S], F32R)
        vs = sb("vs", [P, 2, 2 * KVC], F32R)
        q = sb("q", [P, 2, HG, FW])
        rot_a, rot_b = sb("rot_a", [P, 2, HG, RD]), sb("rot_b", [P, 2, HG, RD])
        qT_hi, qT_lo = sb("qT_hi", [P, 2, HG, P], F32R), sb("qT_lo", [P, 2, HG, P], F32R)
        prob = sb("prob", [P, 4, 2, S])
        nmax, rsum, rinv = sb("nmax", [P, 4, 2]), sb("rsum", [P, 4, 2]), sb("rinv", [P, 4, 2])
        pT_hi, pT_lo = sb("pT_hi", [P, 2, HG, S], F32R), sb("pT_lo", [P, 2, HG, S], F32R)
        oT_hi, oT_lo = sb("oT_hi", [P, HG, S], F32R), sb("oT_lo", [P, HG, S], F32R)

        block = mem.enter_context(nc.Block())

        TURNED = (bank[3], bank[4], bank[5], bank[2])
        Y = bank[2]
        pT_bank = lambda u: TURNED[u][:].rearrange("p (k j n) -> p k j n", k=2, j=2)
        heads = lambda tile: tile[:].rearrange("p (h n) -> p h n", h=HG)
        oT_bank = lambda p: bank[6 + p][:].rearrange("p (h n) -> p h n", h=2)

        def pT_view(t, u):
            h, p = u // 2, u % 2
            return t[:, :, 2 * p:2 * p + 2, h * P:(h + 1) * P]

        @block.gpsimd
        def _(pool):
            def group(n):
                for t in range(2):
                    pool.wait_ge(s_rot, 6 * n + 3 * t + 3)
                    pool.tensor_tensor(q[:, t, :, KVC:], rot_a[:, t], rot_b[:, t], ALU.add).then_inc(s_roped, 1)
                for u in range(4):
                    pool.wait_ge(s_inv, 4 * n + u + 1)
                    pool.tensor_tensor(prob[:, u], prob[:, u], rinv[:, u, :].unsqueeze(2).broadcast_to([P, 2, S]),
                                       ALU.mult).then_inc(s_prob, 1)

            group(0)
            with pool.Fori(0, B * NG - 1) as n:
                group(n + 1)

        @block.scalar
        def _(act):
            def q_copies(n):
                for t in range(2):
                    act.wait_ge(s_q, 2 * n + t + 1)
                    act.activation(q[:, t], bank[t][:].rearrange("p (h f) -> p h f", h=HG), ACT.Copy).then_inc(s_qc, 1)

            def q_high(n):
                for t in range(2):
                    act.wait_ge(s_qT, 2 * n + t + 1)
                    act.activation(qT_hi[:, t], heads(bank[t]), ACT.Copy).then_inc(s_qTh, 1)

            def exps(n):
                for u in range(4):
                    act.wait_ge(s_max, 4 * n + u + 1)
                    for j in range(2):
                        act.activation(prob[:, u, j, :], bank[4 + u][:, j * S:(j + 1) * S], ACT.Exp,
                                       bias=nmax[:, u, j:j + 1], accum_out=rsum[:, u, j:j + 1]).then_inc(s_exp, 1)

            def pT_high(n):
                for u in range(4):
                    act.wait_ge(s_pT, 4 * n + u + 1)
                    act.activation(pT_view(pT_hi, u), pT_bank(u), ACT.Copy).then_inc(s_pTh, 1)

            def outputs_high(n):
                for p in range(2):
                    act.wait_ge(s_o, 2 * n + p + 1)
                    act.activation(oT_hi[:, 2 * p:2 * p + 2, :], oT_bank(p), ACT.Copy).then_inc(s_oh, 1)

            def begin(first):
                q_copies(0)
                q_high(0)
                exps(0)

            def step(cur, nxt, edge):
                q_copies(nxt.n)
                pT_high(cur.n)
                q_high(nxt.n)
                outputs_high(cur.n)
                exps(nxt.n)

            def finish(last):
                pT_high(last.n)
                outputs_high(last.n)

            pipelined(act, B, NG, begin, step, finish)

        @block.vector
        def _(dve):
            def query_slot(n, b):
                wait_from_one(dve, s_q, 2 * n)
                dve.tensor_copy(qs_hi[:], qcT_hi[:, bass.ts(b, S)]).then_inc(s_qslot, 1)
                dve.tensor_copy(qs_lo[:], qcT_lo[:, bass.ts(b, S)]).then_inc(s_qslot, 1)

            def value_slot(n, b):
                wait_from_one(dve, s_o, 2 * n)
                dve.tensor_copy(vs[:], vals[:, bass.ds(2 * b, 2), :, :].rearrange("p t a c -> p t (a c)")
                                ).then_inc(s_vslot, 1)

            def rotate(n):
                for t in range(2):
                    dve.wait_ge(s_qc, 2 * n + t + 1)
                    cs = lambda v, lo, w: v[:, t, lo:lo + w].unsqueeze(1).broadcast_to([P, HG, w])
                    dve.tensor_tensor(rot_a[:, t], q[:, t, :, KVC:], cs(key_cos, 0, RD), ALU.mult).then_inc(s_rot, 1)
                    dve.tensor_tensor(rot_b[:, t, :, 0:half], q[:, t, :, KVC + half:], cs(key_sin, 0, half),
                                      ALU.mult).then_inc(s_rot, 1)
                    dve.tensor_tensor(rot_b[:, t, :, half:], q[:, t, :, KVC:KVC + half], cs(key_sin, half, half),
                                      ALU.mult).then_inc(s_rot, 1)

            def q_low(n):
                for t in range(2):
                    dve.wait_ge(s_qTh, 2 * n + t + 1)
                    dve.tensor_tensor(qT_lo[:, t], heads(bank[t]), qT_hi[:, t].bitcast(F32),
                                      ALU.subtract).then_inc(s_qTl, 1)

            def maxima(n):
                def inverse(u):
                    dve.wait_ge(s_exp, 8 * n + 2 * u + 2)
                    dve.reciprocal(rinv[:, u, :], rsum[:, u, :]).then_inc(s_inv, 1)

                for u in range(4):
                    dve.wait_ge(s_s, 4 * n + u + 1)
                    dve.tensor_reduce(nmax[:, u, :], bank[4 + u][:].rearrange("p (j n) -> p j n", j=2), AX_X,
                                      ALU.max, negate=True).then_inc(s_max, 1)
                    if u >= 2:
                        inverse(u - 2)
                inverse(2)
                inverse(3)

            def pT_low(n):
                for u in range(4):
                    dve.wait_ge(s_pTh, 4 * n + u + 1)
                    dve.tensor_tensor(pT_view(pT_lo, u), pT_bank(u), pT_view(pT_hi, u).bitcast(F32),
                                      ALU.subtract).then_inc(s_pTl, 1)

            def outputs_low(n):
                for p in range(2):
                    dve.wait_ge(s_oh, 2 * n + p + 1)
                    dve.tensor_tensor(oT_lo[:, 2 * p:2 * p + 2, :], oT_bank(p), oT_hi[:, 2 * p:2 * p + 2, :].bitcast(F32),
                                      ALU.subtract).then_inc(s_ol, 1)

            def residual(n, b):
                dve.wait_ge(s_y, n + 1)
                rows2 = x[:, bass.ds(2 * b, 2), :]
                dve.tensor_tensor(rows2, Y[:].rearrange("p (t d) -> p t d", t=2), rows2, ALU.add).then_inc(s_add, 1)

            def begin(first):
                query_slot(0, 0)
                value_slot(0, 0)
                rotate(0)
                q_low(0)
                maxima(0)

            def step(cur, nxt, edge):
                if edge:
                    query_slot(nxt.n, nxt.outer)
                rotate(nxt.n)
                pT_low(cur.n)
                q_low(nxt.n)
                outputs_low(cur.n)
                if edge:
                    value_slot(nxt.n, nxt.outer)
                maxima(nxt.n)
                residual(cur.n, cur.outer)

            def finish(last):
                pT_low(last.n)
                outputs_low(last.n)
                residual(last.n, last.outer)

            pipelined(dve, B, NG, begin, step, finish)
            dve.wait_ge(s_add, B * NG + 1)

        @block.tensor
        def _(pe):
            def project(g):
                pe.wait_ge(s_qslot, 2 * g.outer + 2)
                for t in range(2):
                    last = split3(pe, bank[t][:], (qs_hi[:, tokens(t)], qs_lo[:, tokens(t)]),
                                  (wa_hi[:].rearrange("p h f -> p (h f)")[:, bass.ts(g.inner, 512)],
                                   wa_lo[:].rearrange("p h f -> p (h f)")[:, bass.ts(g.inner, 512)]), True, True)
                    last.then_inc(s_q, 1)

            def turn_q(n):
                for t in range(2):
                    pe.wait_ge(s_roped, 2 * n + t + 1)
                    for h in range(HG):
                        last = pe.transpose(bank[t][:, h * P:(h + 1) * P], q[:, t, h, :], env.ident[:])
                    last.then_inc(s_qT, 1)

            def scores(g):
                cols = bass.ts(g.outer, S)
                for u in range(4):
                    t, p = u // 2, u % 2
                    if u == 2:
                        wait_from_one(pe, s_ol, 2 * g.n)
                    pe.wait_ge(s_qTl, 2 * g.n + t + 1)
                    for j in range(2):
                        h = 2 * p + j
                        out = bank[4 + u][:, j * S:(j + 1) * S]
                        split3(pe, out, (qT_hi[:, t, h, :], qT_lo[:, t, h, :]), (kT_hi[:, cols], kT_lo[:, cols]),
                               True, False)
                        last = pe.matmul(out, env.ident_bf[:],
                                         bias[:].rearrange("p t n -> p (t n)")[:, bass.ds(g.outer * 2 * S + t * S, S)],
                                         start=False, stop=True, skip_group_check=True)
                    last.then_inc(s_s, 1)

            def turn_probs(n):
                for u in range(4):
                    pe.wait_ge(s_prob, 4 * n + u + 1)
                    if TURNED[u] is Y:
                        pe.wait_ge(s_add, n + 1)
                    for k in range(2):
                        for j in range(2):
                            last = pe.transpose(pT_bank(u)[:, k, j, :], prob[:, u, j, k * P:(k + 1) * P], env.ident[:])
                    last.then_inc(s_pT, 1)

            def attend(g):
                pe.wait_ge(s_vslot, g.outer + 1)
                for p in range(2):
                    pe.wait_ge(s_pTl, 4 * g.n + 3 + p)
                    for k in range(2):
                        for part in (pT_hi, pT_lo):
                            last = pe.matmul(bank[6 + p][:], vs[:, k, :],
                                             part[:, k, 2 * p:2 * p + 2, :].rearrange("p h n -> p (h n)"),
                                             start=k == 0 and part is pT_hi, stop=k == 1 and part is pT_lo)
                    last.then_inc(s_o, 1)

            def output(g):
                pe.wait_ge(s_ol, 2 * g.n + 2)
                for t in range(2):
                    for h in range(HG):
                        head = bass.ds(g.inner * HG * D + h * D, D)
                        last = split3(pe, Y[:, t * D:(t + 1) * D], (oT_hi[:, h, tokens(t)], oT_lo[:, h, tokens(t)]),
                                      (c_hi[:].rearrange("p h d -> p (h d)")[:, head],
                                       c_lo[:].rearrange("p h d -> p (h d)")[:, head]), h == 0, h == HG - 1)
                last.then_inc(s_y, 1)

            def begin(first):
                project(first)
                turn_q(0)
                scores(first)

            def step(cur, nxt, edge):
                project(nxt)
                turn_probs(cur.n)
                turn_q(nxt.n)
                attend(cur)
                scores(nxt)
                output(cur)

            def finish(last):
                turn_probs(last.n)
                attend(last)
                output(last)

            pipelined(pe, B, NG, begin, step, finish)
NKV, REP, HD = 4, 8, 128
QKV = (REP + 2) * HD
NR = REP + 1


TURNS = [(), (0, 1), (2, 3), (4, 5), (6,), (7,)]


def grouped_attention(env):
    nc, dram, x = env.nc, env.dram, env.x
    SCALE = 1.0 / math.sqrt(HD)
    half = HD // 2
    bank = env.bank
    with ExitStack() as mem:
        sb = lambda n, s, d=F32: env.sb(f"ga_{n}", s, d, mem)
        sem = lambda n: env.sem(f"ga_{n}")
        h_hi, h_lo = sb("h_hi", [P, KD, TOK + S], F32R), sb("h_lo", [P, KD, TOK + S], F32R)
        cos, sin = sb("cos", [P, 2, HD]), sb("sin", [P, 2, HD])
        causal = sb("causal", [P, P], BF16)
        stage_w, stage_wo = sb("stage_w", [P, KD, QKV]), sb("stage_wo", [P, REP, D])
        w_hi, w_lo = sb("w_hi", [P, KD, QKV], F32R), sb("w_lo", [P, KD, QKV], F32R)
        wo_hi, wo_lo = sb("wo_hi", [P, REP, D], F32R), sb("wo_lo", [P, REP, D], F32R)
        s_const, s_stage, s_stwo = sem("constants_loaded"), sem("w_loaded"), sem("wo_loaded")
        s_whi, s_wlo = sem("w_hi_ready"), sem("w_lo_ready")
        CHUNKS = [(1024, 256), (0, 512), (512, 512)]
        NCH = len(CHUNKS)

        def w_high(act, g):
            act.wait_ge(s_stage, 16 * g + 16)
            for lo, w in CHUNKS:
                act.activation(w_hi[:, :, lo:lo + w], stage_w[:, :, lo:lo + w], ACT.Copy).then_inc(s_whi, 1)

        def w_low(dve, g):
            for n, (lo, w) in enumerate(CHUNKS):
                dve.wait_ge(s_whi, NCH * g + n + 1)
                dve.tensor_tensor(w_lo[:, :, lo:lo + w], stage_w[:, :, lo:lo + w], w_hi[:, :, lo:lo + w].bitcast(F32),
                                  ALU.subtract).then_inc(s_wlo, 1)

        with ExitStack() as prep:
            rms_w = env.sb("ga_rms_w", [P, D], F32, prep)
            layer_norm = Norm(env, "ga_ln", prep, dst=x)
            norm = Norm(env, "ga", prep, rms_w)
            s_w, s_keep = sem("norm_weight_loaded"), sem("input_kept")
            s_hi_again, s_lo_again = sem("first_batch_hi_again"), sem("first_batch_lo_again")
            block = prep.enter_context(nc.Block())

            @block.sync
            def _(sp):
                sp.dma_start(stage_w[:], dram["ga_w"][0]).then_inc(s_stage, 16)
                sp.dma_start(rms_w[:], dram["ln1_rows"]).then_inc(s_w, 16)
                for dst, name in ((cos, "ga_cos"), (sin, "ga_sin"), (causal, "causal")):
                    sp.dma_start(dst[:], dram[name]).then_inc(s_const, 16)
                sp.dma_start(stage_wo[:], dram["ga_wo"][0]).then_inc(s_stwo, 16)

            @block.gpsimd
            def _(pool):
                pool.tensor_copy(env.x_in[:], x[:]).then_inc(s_keep, 1)
                layer_norm.gpsimd_rstd(pool)
                norm.gpsimd_rstd(pool)

            @block.scalar
            def _(act):
                w_high(act, 0)
                act.wait_ge(layer_norm.s_xn, NT)
                norm.scalar_stats(act)
                norm.scalar_hi(act, bank[0:2], h_hi)
                act.wait_ge(norm.s_hi, 1)
                act.activation(h_hi[:, :, TOK:], h_hi[:, :, 0:S].bitcast(F32), ACT.Copy).then_inc(s_hi_again, 1)
                act.wait_ge(s_hi_again, 1)

            @block.vector
            def _(dve):
                layer_norm.vector_normalise(dve, s_keep)
                w_low(dve, 0)
                dve.wait_ge(s_w, 16)
                norm.vector_normalise(dve)
                norm.vector_lo(dve, bank[0:2], h_hi, h_lo)
                dve.wait_ge(norm.s_lo, B)
                dve.tensor_copy(h_lo[:, :, TOK:], h_lo[:, :, 0:S]).then_inc(s_lo_again, 1)
                dve.wait_ge(s_lo_again, 1)

            @block.tensor
            def _(pe):
                norm.tensor_transpose(pe, bank[0:2])

        hs_hi, hs_lo = sb("hs_hi", [P, KD, S], F32R), sb("hs_lo", [P, KD, S], F32R)
        qkv = sb("qkv", [P, 2, QKV])
        val_hi, val_lo = sb("val_hi", [P, 2, HD], F32R), sb("val_lo", [P, 2, HD], F32R)
        rot = sb("rot", [P, NR, HD])
        roped = sb("roped", [P, 2, NR, HD])
        T_hi, T_lo = sb("T_hi", [P, NR, S], F32R), sb("T_lo", [P, NR, S], F32R)
        prob = sb("prob", [P, REP, P + S])
        nmax, rsum, rinv = sb("nmax", [P, REP, 2]), sb("rsum", [P, REP, 2]), sb("rinv", [P, REP, 2])
        pT_hi, pT_lo = sb("pT_hi", [P, REP, S + P], F32R), sb("pT_lo", [P, REP, S + P], F32R)
        oT_hi, oT_lo = sb("oT_hi", [P, REP, S], F32R), sb("oT_lo", [P, REP, S], F32R)

        s_wohi, s_wolo = sem("wo_hi_ready"), sem("wo_lo_ready")
        s_hs = sem("batch_slot_ready")
        s_q, s_qc, s_rot, s_rope = sem("qkv_in_psum"), sem("qkv_copied"), sem("qkv_rotated"), sem("qkv_roped")
        s_val, s_prot = sem("values_ready"), sem("qkv_upper_rotated")
        s_T, s_Th, s_Tl = sem("T_in_psum"), sem("T_hi_ready"), sem("T_lo_ready")
        s_s, s_max, s_exp, s_inv, s_prob = (sem(n) for n in (
            "scores_in_psum", "max_ready", "exp_ready", "row_inverse_ready", "prob_ready"))
        s_pT, s_pTh, s_pTl = sem("pT_in_psum"), sem("pT_hi_ready"), sem("pT_lo_ready")
        s_o, s_oh, s_ol = sem("oT_in_psum"), sem("oT_hi_ready"), sem("oT_lo_ready")
        s_y, s_add = sem("y_in_psum"), sem("residual_added")
        TILE_COLS = ((0, slice(0, P)), (1, slice(P, P + S)))
        Y = bank[7]
        TURNED = [bank[i] for i in (2, 3, 4, 5, 6, 7, 2, 3)]
        block = mem.enter_context(nc.Block())

        @block.sync
        def _(sp):
            with sp.Fori(0, NKV - 1) as g:
                sp.wait_ge(s_whi, NCH * g + NCH)
                sp.wait_ge(s_wlo, NCH * g + NCH)
                sp.dma_start(stage_w[:], dram["ga_w"][g + 1]).then_inc(s_stage, 16)
                sp.wait_ge(s_wohi, g + 1)
                sp.wait_ge(s_wolo, g + 1)
                sp.dma_start(stage_wo[:], dram["ga_wo"][g + 1]).then_inc(s_stwo, 16)

        @block.gpsimd
        def _(pool):
            def wo_low(g):
                pool.wait_ge(s_wohi, g + 1)
                pool.tensor_tensor(wo_lo[:], stage_wo[:], wo_hi[:].bitcast(F32), ALU.subtract).then_inc(s_wolo, 1)

            def normalise(n):
                for h in range(REP):
                    pool.wait_ge(s_inv, REP * n + h + 1)
                    for t, cols in TILE_COLS:
                        pool.tensor_tensor(prob[:, h, cols], prob[:, h, cols],
                                           rinv[:, h, t:t + 1].broadcast_to([P, cols.stop - cols.start]),
                                           ALU.mult).then_inc(s_prob, 1)

            def rotate(n):
                for t in range(2):
                    pool.wait_ge(s_qc, 2 * NCH * n + NCH * t + NCH)
                    if t or not isinstance(n, int):
                        pool.wait_ge(s_rope, 2 * n + t)
                    pool.tensor_tensor(rot[:, :, half:], qkv[:, t, 0:NR * HD].rearrange("p (h f) -> p h f", h=NR)[:, :, 0:half],
                                       sin[:, t, half:].unsqueeze(1).broadcast_to([P, NR, half]),
                                       ALU.mult).then_inc(s_prot, 1)

            def step(cur, nxt, edge):
                rotate(nxt.n)
                normalise(nxt.n)
                if edge:
                    wo_low(nxt.outer)

            pool.wait_ge(s_const, 48)
            rotate(0)
            wo_low(0)
            normalise(0)
            pipelined(pool, NKV, B, lambda first: None, step, lambda last: None)

        @block.scalar
        def _(act):
            def batch_slot(n, b):
                wait_from_one(act, s_q, 2 * NCH * n)
                act.activation(hs_hi[:], h_hi[:, :, bass.ds(b * S, S)].bitcast(F32), ACT.Copy).then_inc(s_hs, 1)
                act.activation(hs_lo[:], h_lo[:, :, bass.ds(b * S, S)].bitcast(F32), ACT.Copy).then_inc(s_hs, 1)

            def wo_high(g):
                act.wait_ge(s_stwo, 16 * g + 16)
                wait_from_one(act, s_y, B * g)
                act.activation(wo_hi[:], stage_wo[:], ACT.Copy).then_inc(s_wohi, 1)

            def project(n, m):
                t, (lo, w) = m // NCH, CHUNKS[m % NCH]
                act.wait_ge(s_q, 2 * NCH * n + m + 1)
                if m == 0:
                    wait_from_one(act, s_val, 2 * n)
                act.activation(qkv[:, t, lo:lo + w], bank[m % 2][:, 0:w], ACT.Copy).then_inc(s_qc, 1)

            def pT_copy(n, h):
                act.wait_ge(s_pT, REP * n + h + 1)
                act.activation(pT_hi[:, h, :], TURNED[h][:, 0:S + P], ACT.Copy).then_inc(s_pTh, 1)

            def outputs(n):
                for p in range(4):
                    act.wait_ge(s_o, 4 * n + p + 1)
                    act.activation(oT_hi[:, 2 * p:2 * p + 2, :], bank[p][:].rearrange("p (h n) -> p h n", h=2),
                                   ACT.Copy).then_inc(s_oh, 1)

            def key_high(n):
                act.wait_ge(s_T, 5 * n + 1)
                act.activation(T_hi[:, REP, :], bank[0][:, 0:S], ACT.Copy).then_inc(s_Th, 1)

            def heads_high(n, i):
                act.wait_ge(s_T, 5 * n + i + 2)
                act.activation(T_hi[:, 2 * i:2 * i + 2, :], bank[1 - i % 2][:].rearrange("p (h n) -> p h n", h=2),
                               ACT.Copy, scale=SCALE).then_inc(s_Th, 1)

            def exps(n, heads):
                for h in heads:
                    act.wait_ge(s_max, 2 * (REP * n + h) + 2)
                    for t, cols in TILE_COLS:
                        act.activation(prob[:, h, cols], bank[4 + h % 4][:, t * S:t * S + (t + 1) * P], ACT.Exp,
                                       bias=nmax[:, h, t:t + 1], accum_out=rsum[:, h, t:t + 1]).then_inc(s_exp, 1)

            def scored(n, b):
                key_high(n)
                heads_high(n, 0)
                heads_high(n, 1)
                batch_slot(n + 1, b + 1)
                heads_high(n, 2)
                exps(n, (0, 1))
                heads_high(n, 3)
                exps(n, range(2, REP))

            def begin(first):
                batch_slot(0, 0)
                for m in range(2 * NCH):
                    project(0, m)
                wo_high(0)
                scored(0, 0)

            def step(cur, nxt, edge):
                if edge:
                    act.wait_ge(s_q, 2 * NCH * nxt.n)
                    w_high(act, nxt.outer)
                for m in range(2 * NCH):
                    project(nxt.n, m)
                    for h in TURNS[m]:
                        pT_copy(cur.n, h)
                outputs(cur.n)
                scored(nxt.n, nxt.inner)
                if edge:
                    wo_high(nxt.outer)

            def finish(last):
                for h in range(REP):
                    pT_copy(last.n, h)
                outputs(last.n)

            pipelined(act, NKV, B, begin, step, finish)

        @block.vector
        def _(dve):
            def pT_low(n, heads):
                for h in heads:
                    dve.wait_ge(s_pTh, REP * n + h + 1)
                    dve.tensor_tensor(pT_lo[:, h, :], TURNED[h][:, 0:S + P], pT_hi[:, h, :].bitcast(F32),
                                      ALU.subtract).then_inc(s_pTl, 1)

            def rope(n, tiles=(0, 1)):
                for t in tiles:
                    dve.wait_ge(s_qc, 2 * NCH * n + NCH * t + NCH)
                    q3 = qkv[:, t, 0:NR * HD].rearrange("p (h f) -> p h f", h=NR)
                    cs = lambda v, lo, w: v[:, t, lo:lo + w].unsqueeze(1).broadcast_to([P, NR, w])
                    dve.tensor_tensor(roped[:, t], q3, cs(cos, 0, HD), ALU.mult).then_inc(s_rot, 1)
                    wait_from_one(dve, s_rope, 2 * n + t)
                    dve.tensor_tensor(rot[:, :, 0:half], q3[:, :, half:], cs(sin, 0, half), ALU.mult).then_inc(s_rot, 1)
                    dve.wait_ge(s_rot, 4 * n + 2 * t + 2)
                    dve.wait_ge(s_prot, 2 * n + t + 1)
                    dve.tensor_tensor(roped[:, t], roped[:, t], rot[:], ALU.add).then_inc(s_rope, 1)

            def outputs_low(n, pairs):
                for p in pairs:
                    dve.wait_ge(s_oh, 4 * n + p + 1)
                    dve.tensor_tensor(oT_lo[:, 2 * p:2 * p + 2, :], bank[p][:].rearrange("p (h n) -> p h n", h=2),
                                      oT_hi[:, 2 * p:2 * p + 2, :].bitcast(F32), ALU.subtract).then_inc(s_ol, 1)

            def key_low(n):
                dve.wait_ge(s_Th, 5 * n + 1)
                dve.tensor_tensor(T_lo[:, REP, :], bank[0][:, 0:S], T_hi[:, REP, :].bitcast(F32),
                                  ALU.subtract).then_inc(s_Tl, 1)

            def heads_low(n, i):
                dve.wait_ge(s_Th, 5 * n + i + 2)
                dve.scalar_tensor_tensor(T_lo[:, 2 * i:2 * i + 2, :],
                                         bank[1 - i % 2][:].rearrange("p (h n) -> p h n", h=2), SCALE,
                                         T_hi[:, 2 * i:2 * i + 2, :].bitcast(F32),
                                         ALU.mult, ALU.subtract).then_inc(s_Tl, 1)

            def inverse(n, h):
                dve.wait_ge(s_exp, 2 * (REP * n + h) + 2)
                dve.reciprocal(rinv[:, h, :], rsum[:, h, :]).then_inc(s_inv, 1)

            def maxima(n, heads):
                for h in heads:
                    dve.wait_ge(s_s, REP * n + h + 1)
                    for t in range(2):
                        dve.tensor_reduce(nmax[:, h, t:t + 1], bank[4 + h % 4][:, t * S:t * S + (t + 1) * P], AX_X,
                                          ALU.max, negate=True).then_inc(s_max, 1)
                    if h >= 2:
                        inverse(n, h - 2)

            def scored(n, between):
                key_low(n)
                heads_low(n, 0)
                heads_low(n, 1)
                between()
                maxima(n, (0, 1))
                heads_low(n, 2)
                maxima(n, (2, 3))
                heads_low(n, 3)
                maxima(n, range(4, REP))
                inverse(n, REP - 2)
                inverse(n, REP - 1)

            def keep_values(n):
                wait_from_one(dve, s_o, 4 * n)
                dve.tensor_copy(val_hi[:], qkv[:, :, NR * HD:]).then_inc(s_val, 1)
                dve.wait_ge(s_val, 2 * n + 1)
                dve.tensor_tensor(val_lo[:], qkv[:, :, NR * HD:], val_hi[:].bitcast(F32), ALU.subtract).then_inc(s_val, 1)

            def residual(n, b):
                dve.wait_ge(s_y, n + 1)
                rows2 = x[:, bass.ds(2 * b, 2), :]
                dve.tensor_tensor(rows2, Y[:].rearrange("p (t d) -> p t d", t=2), rows2, ALU.add).then_inc(s_add, 1)

            def begin(first):
                dve.wait_ge(s_const, 48)
                rope(0)
                scored(0, lambda: keep_values(0))

            def step(cur, nxt, edge):
                if edge:
                    w_low(dve, nxt.outer)
                pT_low(cur.n, range(0, 4))
                rope(nxt.n, (0,))
                pT_low(cur.n, range(4, REP))
                outputs_low(cur.n, (0, 1))
                rope(nxt.n, (1,))
                outputs_low(cur.n, (2, 3))

                def between():
                    residual(cur.n, cur.inner)
                    keep_values(nxt.n)

                scored(nxt.n, between)

            def finish(last):
                pT_low(last.n, range(REP))
                outputs_low(last.n, range(4))
                residual(last.n, last.inner)

            pipelined(dve, NKV, B, begin, step, finish)
            dve.wait_ge(s_add, B * NKV)

        @block.tensor
        def _(pe):
            def project(nxt, m):
                n = nxt.n
                t, (lo, w) = m // NCH, CHUNKS[m % NCH]
                if m == 0:
                    pe.wait_ge(s_hs, 2 * n + 2)
                if m < NCH:
                    pe.wait_ge(s_wlo, NCH * nxt.outer + m + 1)
                if m >= 2:
                    pe.wait_ge(s_qc, 2 * NCH * n + m - 1)
                for k in range(KD):
                    last = split3(pe, bank[m % 2][:, 0:w], (hs_hi[:, k, tokens(t)], hs_lo[:, k, tokens(t)]),
                                  (w_hi[:, k, lo:lo + w], w_lo[:, k, lo:lo + w]), k == 0, k == KD - 1)
                last.then_inc(s_q, 1)

            def turn_probs(n, h):
                pe.wait_ge(s_prob, 2 * (REP * n + h) + 2)
                if 2 <= h < 6:
                    pe.wait_ge(s_exp, 2 * (REP * n + h + 2) + 2)
                if h >= 6:
                    pe.wait_ge(s_pTl, REP * n + h - 5)
                for to, src in ((0, 0), (P, P), (S, S)):
                    last = pe.transpose(TURNED[h][:, to:to + P], prob[:, h, src:src + P], env.ident[:])
                last.then_inc(s_pT, 1)

            def attend(n, bank_free):
                pe.wait_ge(s_val, 2 * n + 2)
                for p in range(4):
                    bank_free(p)
                    pe.wait_ge(s_pTl, REP * n + (2, 4, 7, 8)[p])
                    o3 = bank[p][:].rearrange("p (h n) -> p h n", h=2)
                    heads = slice(2 * p, 2 * p + 2)
                    split3(pe, bank[p][:], (val_hi[:, 0, :], val_lo[:, 0, :]),
                           (pT_hi[:, heads, 0:S], pT_lo[:, heads, 0:S]), True, False)
                    split3(pe, o3[:, :, P:], (val_hi[:, 1, :], val_lo[:, 1, :]),
                           (pT_hi[:, heads, S:], pT_lo[:, heads, S:]), False, True).then_inc(s_o, 1)

            def turn_key(n):
                for t in range(2):
                    pe.wait_ge(s_rope, 2 * n + t + 1)
                    last = pe.transpose(bank[0][:, t * P:(t + 1) * P], roped[:, t, REP, :], env.ident[:])
                last.then_inc(s_T, 1)

            def turn_heads(n, i):
                if i >= 1:
                    pe.wait_ge(s_Tl, 5 * n + i)
                for j in range(2):
                    for t in range(2):
                        last = pe.transpose(bank[1 - i % 2][:, j * S + t * P:j * S + (t + 1) * P],
                                            roped[:, t, 2 * i + j, :], env.ident[:])
                last.then_inc(s_T, 1)

            def output(n, i):
                pe.wait_ge(s_ol, 4 * n + i + 1)
                for h in (2 * i, 2 * i + 1):
                    for t in range(2):
                        last = split3(pe, Y[:, t * D:(t + 1) * D], (oT_hi[:, h, tokens(t)], oT_lo[:, h, tokens(t)]),
                                      (wo_hi[:, h, :], wo_lo[:, h, :]), h == 0 and t == 0, h == REP - 1)
                if i == 3:
                    last.then_inc(s_y, 1)

            def scores(n, heads):
                for h in heads:
                    if h == 3:
                        wait_from_one(pe, s_add, n)
                    if h >= 4:
                        pe.wait_ge(s_exp, 2 * (REP * n + h - 4) + 2)
                    pe.wait_ge(s_Tl, 5 * n + 2 + h // 2)
                    for t in range(2):
                        out = bank[4 + h % 4][:, t * S:(t + 1) * S]
                        split3(pe, out, (T_hi[:, h, tokens(t)], T_lo[:, h, tokens(t)]),
                               (T_hi[:, REP, :], T_lo[:, REP, :]), True, False)
                        last = pe.matmul(out[:, t * P:(t + 1) * P], env.ident_bf[:], causal[:], start=False, stop=True,
                                         skip_group_check=True)
                    last.then_inc(s_s, 1)

            def scored(n, between):
                turn_key(n)
                turn_heads(n, 0)
                between(2)
                turn_heads(n, 1)
                between(3)
                scores(n, (0, 1))
                turn_heads(n, 2)
                scores(n, (2, 3))
                turn_heads(n, 3)
                scores(n, range(4, REP))

            def begin(first):
                pe.wait_ge(s_const, 48)
                for m in range(2 * NCH):
                    project(first, m)
                pe.wait_ge(s_qc, 2 * NCH)
                scored(0, lambda i: None)

            def step(cur, nxt, edge):
                for m in range(2 * NCH):
                    project(nxt, m)
                    for h in TURNS[m]:
                        turn_probs(cur.n, h)
                attend(cur.n, lambda p: p < 2 and pe.wait_ge(s_qc, 2 * NCH * nxt.n + 2 * NCH - 1 + p))
                pe.wait_ge(s_wolo, cur.outer + 1)
                output(cur.n, 0)
                output(cur.n, 1)
                scored(nxt.n, lambda i: output(cur.n, i))

            def finish(last):
                for h in range(REP):
                    turn_probs(last.n, h)
                attend(last.n, lambda p: None)
                pe.wait_ge(s_wolo, NKV)
                for i in range(4):
                    output(last.n, i)

            pipelined(pe, NKV, B, begin, step, finish)
def program(nc, dram, out):
    with ExitStack() as ctx:
        env = Env(nc, ctx, dram)
        env.x = env.sb("x", [P, NT, D])
        env.ident, env.ident_bf = env.sb("ident", [P, P]), env.sb("ident_bf", [P, P], BF16)
        env.minus_half = env.sb("minus_half", [P, NT])
        env.bank = [ctx.enter_context(nc.psum_tensor(f"bank{i}", [P, 512], F32)) for i in range(8)]
        env.s_x, env.s_const = env.sem("x_loaded"), env.sem("identities_loaded")
        s_out, s_half = env.sem("out_stored"), env.sem("minus_half_ready")
        with nc.Block() as block:
            @block.sync
            def _(sp):
                sp.dma_start(env.x[:], dram["x"]).then_inc(env.s_x, 16)
                sp.dma_start(env.ident[:], dram["ident"]).then_inc(env.s_const, 16)
                sp.dma_start(env.ident_bf[:], dram["ident_bf"]).then_inc(env.s_const, 16)

            @block.gpsimd
            def _(pool):
                pool.memset(env.minus_half[:], -0.5).then_inc(s_half, 1)
                pool.wait_ge(s_half, 1)
        with ExitStack() as mem:
            latent = LatentSetup(env, mem)
            env.stage(lambda: quantised_attention(env, latent))
            latent.keep(mem)
            env.stage(lambda: experts(env, "f0", 0, latent))
            env.stage(lambda: latent_attention(env, latent))
        env.x_in = env.sb("x_in", [P, NT, D])
        env.stage(lambda: grouped_attention(env))
        env.stage(lambda: experts(env, "f1", 1))
        with nc.Block() as block:
            @block.sync
            def _(sp):
                sp.dma_start(out, env.x[:]).then_inc(s_out, 16)
                sp.wait_ge(s_out, 16)


def rows(v, n=128):
    import numpy as np
    return np.broadcast_to(v, (n,) + v.shape)


def layout(i):
    import numpy as np
    bf = mybir.dt.np(BF16)
    c = lambda a: np.ascontiguousarray(a)
    tok = lambda a: c(a.reshape(NT, P, -1).transpose(1, 0, 2))
    kmaj = lambda w: w.reshape(KD, P, -1).transpose(1, 0, 2)
    d = {}
    d["x"] = tok(i["x"])
    d["ident"] = np.eye(P, dtype=np.float32)
    d["ident_bf"] = np.eye(P).astype(bf)

    def unit_weights(g, u, w):
        return np.concatenate([kmaj(g).reshape(P, -1), kmaj(u).reshape(P, -1), w], axis=1)

    g, u, w = i["L0_ffn_Wg"], i["L0_ffn_Wu"], i["L0_ffn_Wd"]
    d["f0_weights"] = c(np.stack([unit_weights(g[e][:, f], u[e][:, f], w[e][f]) for e in range(8)
                                  for f in (slice(0, 128), slice(128, 256))]))
    g, u, w = i["L1_ffn_Wg"], i["L1_ffn_Wu"], i["L1_ffn_Wd"]
    d["f1_weights"] = c(np.stack([unit_weights(g[e], u[e], w[e]) for e in range(32)]
                                 + [unit_weights(i["L1_ffn_Wsg"], i["L1_ffn_Wsu"], i["L1_ffn_Wsd"])]))
    for tag, r in (("f0", i["L0_ffn_Wr"]), ("f1", i["L1_ffn_Wr"])):
        pad = np.zeros((P, KD, P), np.float32)
        pad[:, :, :r.shape[1]] = kmaj(r)
        d[f"{tag}_wr"] = pad
    d["f0_route"] = c(np.broadcast_to(i["L0_ffn_temperature"], (P, 32)))
    d["f1_route"] = c(rows(i["L1_ffn_expert_bias"]))
    d["ln2_rows"] = c(rows(i["L1_ffn_ln2_w"]))
    d["before"] = c(rows(np.tril(np.ones((8, 8), np.float32), -1)))
    sel = np.zeros((3, RW, RW, P), np.float32)
    for e in range(RW):
        sel[:, e, e, :] = 1
    d["sel"] = sel.reshape(3 * RW, RW * P).astype(bf)

    d["wq_wo"] = c(np.concatenate([i[f"L0_xattn_w{n}"].reshape(2, P, D) for n in "qo"]).transpose(1, 0, 2))
    d["wkvT"] = c(np.concatenate([kmaj(i[f"L0_xattn_w{n}"].T) for n in "kv"], axis=2))
    d["l0_bias"] = c(rows(np.stack([i[f"L0_xattn_b{n}"] for n in "qkvo"])))
    d["mask"] = tok(i["mask_BxSxS2_ff0"])
    d["ctxT"] = c(i["ctx_2048"].reshape(TOK, KD, P).transpose(2, 1, 0))
    d["w_kvc"] = c(kmaj(i["L1_xattn_W_kvc"]))
    d["w_dq"] = np.zeros((P, KD, P), np.float32)
    d["w_dq"][:, :, :QC] = kmaj(i["L1_xattn_W_dq"])
    d["uqT"] = c(i["L1_xattn_W_uq"].reshape(QC, H1, HD1).transpose(2, 1, 0))
    d["ukT"] = c(i["L1_xattn_W_uk"].reshape(KVC, H1, HD1).transpose(2, 1, 0))
    uvT = i["L1_xattn_W_uv"].reshape(KVC, H1, HD1).transpose(2, 1, 0)
    d["uvT2"] = c(np.concatenate([uvT, uvT], axis=2))
    d["la_wo"] = c(i["L1_xattn_W_o"].reshape(H1, HD1, D).transpose(1, 0, 2))
    d["qr"] = c(i["L1_xattn_W_qr"].reshape(QC, H1, RD))
    d["key_w"] = c(np.concatenate([np.eye(KVC, dtype=np.float32), i["L1_xattn_W_kr"]], axis=1))
    d["la_cos"], d["la_sin"] = rotary(RD)
    d["seg"] = c(i["itok_BxS_0_1023"].reshape(NT, P).T)
    d["key_id"] = c(rows(np.arange(S, dtype=np.float32)))
    wq = kmaj(i["L1_ffn_Wq"]).reshape(P, KD, NKV, REP * HD)
    wk, wv = (kmaj(i[f"L1_ffn_W{n}"]).reshape(P, KD, NKV, HD) for n in "kv")
    d["ga_w"] = c(np.concatenate([wq, wk, wv], axis=3).transpose(2, 0, 1, 3))
    d["ga_wo"] = c(i["L1_ffn_Wo"].reshape(NKV, REP, HD, D).transpose(0, 2, 1, 3))
    d["ln1_rows"] = c(rows(i["L1_ffn_ln1_w"]))
    d["ga_cos"], d["ga_sin"] = rotary(HD)
    d["causal"] = np.where(np.tril(np.ones((P, P), bool)), 0.0, NEG).astype(bf)
    return d


def rotary(width):
    import numpy as np
    half = width // 2
    freq = (np.float32(1.0) / np.float32(10000.0) ** (np.arange(half, dtype=np.float32) / np.float32(half)))
    ang = (np.arange(S, dtype=np.float32)[:, None] * freq.astype(np.float32)).astype(np.float32)
    lay = lambda a, b: np.ascontiguousarray(
        np.concatenate([a, b], axis=1).astype(np.float32).reshape(S // P, P, width).transpose(1, 0, 2))
    cos, sin = np.cos(ang.astype(np.float64)), np.sin(ang.astype(np.float64))
    return lay(cos, cos), lay(-sin, sin)


def kernel(**inputs):
    import numpy as np
    import concourse.bacc as bacc
    from concourse.bass_utils import run_bass_kernel_spmd

    nc = bacc.Bacc("TRN2", target_bir_lowering=False, num_devices=1)
    arrays = {f"in_{k}": v for k, v in layout({k: np.asarray(v) for k, v in inputs.items()}).items()}
    dram = {k[3:]: nc.dram_tensor(k, v.shape, mybir.dt.from_np(v.dtype), kind="ExternalInput").ap()
            for k, v in arrays.items()}
    out = nc.dram_tensor("out", (P, NT, D), F32, kind="ExternalOutput").ap()
    program(nc, dram, out)
    r = run_bass_kernel_spmd(nc, [arrays], core_ids=[0])
    y = r.results[0]["out"]
    return np.ascontiguousarray(y.transpose(1, 0, 2)).reshape(B, S, D)
```
